# Optimizing a Trainium2 kernel written in Bass

```python
import numpy as np
import jax
import jax.numpy as jnp

def _softmax(x, axis=-1):
    return jax.nn.softmax(x, axis=axis)

def _gelu(x):
    return jax.nn.gelu(x, approximate=True)

def _silu(x):
    return jax.nn.silu(x)

def _sigmoid(x):
    return jax.nn.sigmoid(x)

def _layernorm(x, axis=-1, eps=1e-05):
    m = jnp.mean(x, axis=axis, keepdims=True)
    v = jnp.var(x, axis=axis, keepdims=True)
    return (x - m) / jnp.sqrt(v + eps)

def _scatter_add(tgt, idx, src, axis=0):
    return tgt.at[idx].add(src)

def _segment_sum(src, seg, n):
    return jax.ops.segment_sum(src, seg, n)
kernel_name = 'mk_gnn_preln_d4_gnn_r32_9e9c52'

def setup_inputs(seed: int=0):
    np.random.seed(seed)
    _w = jnp.asarray

    def _rec_inputs():
        import jax
        import jax.numpy as jnp
        _gk = jax.random.key(seed)
        x = -0.0009044 + 1 * jax.random.normal(jax.random.fold_in(_gk, 1), (3125, 32), jnp.float32)
        _s = jax.random.randint(jax.random.fold_in(_gk, 2), (50000,), 0, 3125, jnp.int32)
        _d = jax.random.randint(jax.random.fold_in(_gk, 3), (50000,), 0, 3125, jnp.int32)
        _loop = jnp.arange(3125, dtype=jnp.int32)
        src = jnp.concatenate([_s, _d, _loop])
        dst = jnp.concatenate([_d, _s, _loop])
        _o = jnp.argsort(dst, stable=True)
        src = src[_o]
        dst = dst[_o]
        edge_attr_2 = jax.random.uniform(jax.random.fold_in(_gk, 11), (103125, 2), jnp.float32, 0.0, 0.999999)
        edge_attr_3 = jax.random.uniform(jax.random.fold_in(_gk, 12), (103125, 3), jnp.float32, 0.0, 0.999998)
        return (x, src, dst, edge_attr_2, edge_attr_3)
    x, src, dst, edge_attr_2, edge_attr_3 = _rec_inputs()

    def _L0_gnn_setup():
        import jax, jax.numpy as jnp
        import numpy as np
        N_NODES = 50000
        DEG = 16
        N_HEAD = 4
        F_IN = 32
        F_OUT = 32
        key = jax.random.key(seed)
        k_h, k_w, k_fw, k_fb = jax.random.split(key, 4)
        h = jax.random.normal(k_h, (N_NODES, F_IN), dtype=jnp.float32)
        src = jnp.repeat(jnp.arange(N_NODES, dtype=jnp.int64), DEG)
        offs = (jnp.arange(DEG, dtype=jnp.int64) + 1) * 97
        dst = (src.reshape(N_NODES, DEG) + offs[None, :]).reshape(-1) % N_NODES
        edge_index = jnp.stack([src, dst], axis=0)
        gain = 1.414
        bound_w = gain * np.sqrt(6.0 / (F_IN + F_OUT))
        w = jax.random.uniform(k_w, (N_HEAD, F_IN, F_OUT), jnp.float32, -bound_w, bound_w)
        bound_fc = np.sqrt(1.0 / (2 * F_OUT))
        fc_w = jax.random.uniform(k_fw, (1, 2 * F_OUT), jnp.float32, -bound_fc, bound_fc)
        fc_b = jax.random.uniform(k_fb, (1,), jnp.float32, -bound_fc, bound_fc)
        bias = jnp.zeros((F_OUT,), jnp.float32)
        return {'h': h, 'edge_index': edge_index, 'w': w, 'fc_w': fc_w, 'fc_b': fc_b, 'bias': bias}
    _L0_gnn_all = _L0_gnn_setup()
    _L0_gnn_in = {k: v for k, v in _L0_gnn_all.items() if k in ('w', 'fc_w', 'fc_b', 'bias')}
    del _L0_gnn_all

    def _L1_gnn_setup():
        import jax, jax.numpy as jnp
        import numpy as np
        N = 3125
        E = 50000
        IN_C, HID, OUT_C = (32, 64, 32)

        def _mean_aggregate(x, src, dst, num_nodes):
            summed = jax.ops.segment_sum(x[src], dst, num_segments=num_nodes)
            deg = jax.ops.segment_sum(jnp.ones((src.shape[0],), x.dtype), dst, num_segments=num_nodes)
            return summed / jnp.maximum(deg, 1.0)[:, None]

        def _sage_conv(x, src, dst, W_l, b, W_r):
            agg = _mean_aggregate(x, src, dst, x.shape[0])
            return agg @ W_l + b + x @ W_r
        key = jax.random.key(seed)
        ks = jax.random.split(key, 8)
        x = jax.random.normal(ks[0], (N, IN_C), dtype=jnp.float32)
        edge_index = jax.random.randint(ks[1], (2, E), 0, N, dtype=jnp.int64)
        s1 = 1.0 / np.sqrt(IN_C)
        s2 = 1.0 / np.sqrt(HID)
        W1_l = jax.random.uniform(ks[2], (IN_C, HID), jnp.float32, -s1, s1)
        b1 = jnp.zeros((HID,), jnp.float32)
        W1_r = jax.random.uniform(ks[3], (IN_C, HID), jnp.float32, -s1, s1)
        W2_l = jax.random.uniform(ks[4], (HID, OUT_C), jnp.float32, -s2, s2)
        b2 = jnp.zeros((OUT_C,), jnp.float32)
        W2_r = jax.random.uniform(ks[5], (HID, OUT_C), jnp.float32, -s2, s2)
        return {'x': x, 'edge_index': edge_index, 'W1_l': W1_l, 'b1': b1, 'W1_r': W1_r, 'W2_l': W2_l, 'b2': b2, 'W2_r': W2_r}
    _L1_gnn_all = _L1_gnn_setup()
    _L1_gnn_in = {k: v for k, v in _L1_gnn_all.items() if k in ('W1_l', 'b1', 'W1_r', 'W2_l', 'b2', 'W2_r')}
    del _L1_gnn_all

    def _L2_gnn_setup():
        import jax, jax.numpy as jnp
        import numpy as np
        N, E = (163842, 30720)
        CIN, COUT, DIM, K = (32, 32, 2, 3)
        EPS = 1e-15
        key = jax.random.key(seed)
        ks = jax.random.split(key, 8)
        x = jax.random.normal(ks[0], (N, CIN), dtype=jnp.float32)
        edges = jax.random.randint(ks[1], (2, E), 0, N, dtype=jnp.int64)
        edge_vectors = jax.random.uniform(ks[2], (E, DIM), dtype=jnp.float32)
        g = jax.random.normal(ks[3], (CIN, K * COUT), dtype=jnp.float32) / np.sqrt(CIN)
        mu = jax.random.normal(ks[4], (K, DIM), dtype=jnp.float32)
        sigma = jax.random.uniform(ks[5], (K, DIM), dtype=jnp.float32) + 0.5
        root = jax.random.normal(ks[6], (CIN, COUT), dtype=jnp.float32) / np.sqrt(CIN)
        bias = jnp.zeros((COUT,), dtype=jnp.float32)
        return {'x': x, 'edges': edges, 'edge_vectors': edge_vectors, 'g': g, 'mu': mu, 'sigma': sigma, 'root': root, 'bias': bias}
    _L2_gnn_all = _L2_gnn_setup()
    _L2_gnn_in = {k: v for k, v in _L2_gnn_all.items() if k in ('g', 'mu', 'sigma', 'root', 'bias')}
    del _L2_gnn_all

    def _L3_gnn_setup():
        import jax, jax.numpy as jnp
        import numpy as np
        D = 3
        KS = 5
        K = KS ** D
        S = 2 ** D
        _COMBOS = np.array([[s >> d & 1 for d in range(D)] for s in range(S)], dtype=np.int32)
        _STRIDES = np.array([KS ** (D - 1 - d) for d in range(D)], dtype=np.int32)

        def spline_basis(pseudo):
            pos = pseudo * (KS - 1)
            i0 = jnp.clip(jnp.floor(pos), 0, KS - 2).astype(jnp.int32)
            frac = pos - i0
            combos = jnp.asarray(_COMBOS)
            basis = jnp.prod(jnp.where(combos[None] == 1, frac[:, None, :], 1.0 - frac[:, None, :]), axis=-1)
            idx = jnp.sum((i0[:, None, :] + combos[None]) * jnp.asarray(_STRIDES)[None, None, :], axis=-1)
            return (basis, idx)

        def spline_conv(x, row, col, basis, idx, W, b):
            N = x.shape[0]
            Fout = W.shape[2]
            z = jnp.einsum('ni,kio->nko', x, W).reshape(N * K, Fout)
            gathered = z[col[:, None] * K + idx]
            msg = jnp.einsum('es,eso->eo', basis, gathered)
            out = jax.ops.segment_sum(msg, row, num_segments=N)
            deg = jax.ops.segment_sum(jnp.ones_like(msg[:, 0]), row, num_segments=N)
            return out / jnp.maximum(deg, 1.0)[:, None] + b
        key = jax.random.key(seed)
        ks = jax.random.split(key, 13)
        N, E, Fin, Fout = (625, 10000, 32, 32)

        def u(k, shape, size):
            bound = 1.0 / np.sqrt(size)
            return jax.random.uniform(k, shape, jnp.float32, -bound, bound)
        return dict(x=jax.random.normal(ks[0], (N, Fin), jnp.float32), edge_index=jax.random.randint(ks[1], (2, E), 0, N, dtype=jnp.int32), pseudo=jax.random.uniform(ks[2], (E, D), jnp.float32), stn1_w=u(ks[3], (K, 1, 64), 1 * S), stn1_b=u(ks[4], (64,), 1 * S), stn2_w=u(ks[5], (K, 64, 64), 64 * S), stn2_b=u(ks[6], (64,), 64 * S), stn3_w=u(ks[7], (64, 64), 64), stn3_b=u(ks[8], (64,), 64), stn4_w=u(ks[9], (64, 3), 64), stn4_b=u(ks[10], (3,), 64), conv_w=u(ks[11], (K, Fin, Fout), Fin * S), conv_b=u(ks[12], (Fout,), Fin * S))
    _L3_gnn_all = _L3_gnn_setup()
    _L3_gnn_in = {k: v for k, v in _L3_gnn_all.items() if k in ('stn1_w', 'stn1_b', 'stn2_w', 'stn2_b', 'stn3_w', 'stn3_b', 'stn4_w', 'stn4_b', 'conv_w', 'conv_b')}
    del _L3_gnn_all
    return {'x': x, 'src': src, 'dst': dst, 'edge_attr_2': edge_attr_2, 'edge_attr_3': edge_attr_3, 'L0_gnn_w': _L0_gnn_in['w'], 'L0_gnn_fc_w': _L0_gnn_in['fc_w'], 'L0_gnn_fc_b': _L0_gnn_in['fc_b'], 'L0_gnn_bias': _L0_gnn_in['bias'], 'L1_gnn_W1_l': _L1_gnn_in['W1_l'], 'L1_gnn_b1': _L1_gnn_in['b1'], 'L1_gnn_W1_r': _L1_gnn_in['W1_r'], 'L1_gnn_W2_l': _L1_gnn_in['W2_l'], 'L1_gnn_b2': _L1_gnn_in['b2'], 'L1_gnn_W2_r': _L1_gnn_in['W2_r'], 'L2_gnn_g': _L2_gnn_in['g'], 'L2_gnn_mu': _L2_gnn_in['mu'], 'L2_gnn_sigma': _L2_gnn_in['sigma'], 'L2_gnn_root': _L2_gnn_in['root'], 'L2_gnn_bias': _L2_gnn_in['bias'], 'L3_gnn_stn1_w': _L3_gnn_in['stn1_w'], 'L3_gnn_stn1_b': _L3_gnn_in['stn1_b'], 'L3_gnn_stn2_w': _L3_gnn_in['stn2_w'], 'L3_gnn_stn2_b': _L3_gnn_in['stn2_b'], 'L3_gnn_stn3_w': _L3_gnn_in['stn3_w'], 'L3_gnn_stn3_b': _L3_gnn_in['stn3_b'], 'L3_gnn_stn4_w': _L3_gnn_in['stn4_w'], 'L3_gnn_stn4_b': _L3_gnn_in['stn4_b'], 'L3_gnn_conv_w': _L3_gnn_in['conv_w'], 'L3_gnn_conv_b': _L3_gnn_in['conv_b']}

def reference(x, src, dst, edge_attr_2, edge_attr_3, L0_gnn_w, L0_gnn_fc_w, L0_gnn_fc_b, L0_gnn_bias, L1_gnn_W1_l, L1_gnn_b1, L1_gnn_W1_r, L1_gnn_W2_l, L1_gnn_b2, L1_gnn_W2_r, L2_gnn_g, L2_gnn_mu, L2_gnn_sigma, L2_gnn_root, L2_gnn_bias, L3_gnn_stn1_w, L3_gnn_stn1_b, L3_gnn_stn2_w, L3_gnn_stn2_b, L3_gnn_stn3_w, L3_gnn_stn3_b, L3_gnn_stn4_w, L3_gnn_stn4_b, L3_gnn_conv_w, L3_gnn_conv_b):
    import jax
    import jax.numpy as jnp

    def _L0_gnn_ref(h, edge_index, w, fc_w, fc_b, bias):
        import jax, jax.numpy as jnp
        import numpy as np
        N_NODES = 50000
        DEG = 16
        N_HEAD = 4
        F_IN = 32
        F_OUT = 32
        n_head, f_in, f_out = w.shape
        n = h.shape[0]
        src, dst = (edge_index[0], edge_index[1])
        hp = jnp.einsum('nf,hfo->hno', h, w)
        w_src = fc_w[0, :f_out]
        w_dst = fc_w[0, f_out:]
        a_src = jnp.einsum('hnf,f->hn', hp, w_src)
        a_dst = jnp.einsum('hnf,f->hn', hp, w_dst)
        e = a_src[:, src] + a_dst[:, dst] + fc_b[0]
        e = jax.nn.leaky_relu(e, negative_slope=0.2)
        seg_max = jax.ops.segment_max(e.T, src, num_segments=n)
        e = jnp.exp(e - seg_max.T[:, src])
        seg_sum = jax.ops.segment_sum(e.T, src, num_segments=n)
        att = e / seg_sum.T[:, src]
        msg = att[:, :, None] * hp[:, dst, :]
        agg = jax.vmap(lambda m: jax.ops.segment_sum(m, src, num_segments=n))(msg)
        out = agg.mean(axis=0) + bias
        return out

    def _L1_gnn_ref(x, edge_index, W1_l, b1, W1_r, W2_l, b2, W2_r):
        import jax, jax.numpy as jnp
        import numpy as np
        N = 3125
        E = 50000
        IN_C, HID, OUT_C = (32, 64, 32)

        def _mean_aggregate(x, src, dst, num_nodes):
            summed = jax.ops.segment_sum(x[src], dst, num_segments=num_nodes)
            deg = jax.ops.segment_sum(jnp.ones((src.shape[0],), x.dtype), dst, num_segments=num_nodes)
            return summed / jnp.maximum(deg, 1.0)[:, None]

        def _sage_conv(x, src, dst, W_l, b, W_r):
            agg = _mean_aggregate(x, src, dst, x.shape[0])
            return agg @ W_l + b + x @ W_r
        src, dst = (edge_index[0], edge_index[1])
        h = jax.nn.relu(_sage_conv(x, src, dst, W1_l, b1, W1_r))
        return _sage_conv(h, src, dst, W2_l, b2, W2_r)

    def _L2_gnn_ref(x, edges, edge_vectors, g, mu, sigma, root, bias):
        import jax, jax.numpy as jnp
        import numpy as np
        N, E = (163842, 30720)
        CIN, COUT, DIM, K = (32, 32, 2, 3)
        EPS = 1e-15
        n, cin = x.shape
        e, d = edge_vectors.shape
        k = mu.shape[0]
        cout = root.shape[1]
        src, dst = (edges[0], edges[1])
        diff = edge_vectors[:, None, :] - mu[None, :, :]
        gauss = jnp.exp(-0.5 * jnp.sum(diff * diff / (EPS + sigma[None] ** 2), axis=-1))
        xj = x[src] @ g
        msg = jnp.sum(xj.reshape(e, k, cout) * gauss[:, :, None], axis=1)
        summed = jax.ops.segment_sum(msg, dst, num_segments=n)
        count = jax.ops.segment_sum(jnp.ones((e,), x.dtype), dst, num_segments=n)
        out = summed / jnp.maximum(count, 1.0)[:, None]
        return out + x @ root + bias

    def _L3_gnn_ref(x, edge_index, pseudo, stn1_w, stn1_b, stn2_w, stn2_b, stn3_w, stn3_b, stn4_w, stn4_b, conv_w, conv_b):
        import jax, jax.numpy as jnp
        import numpy as np
        D = 3
        KS = 5
        K = KS ** D
        S = 2 ** D
        _COMBOS = np.array([[s >> d & 1 for d in range(D)] for s in range(S)], dtype=np.int32)
        _STRIDES = np.array([KS ** (D - 1 - d) for d in range(D)], dtype=np.int32)

        def spline_basis(pseudo):
            pos = pseudo * (KS - 1)
            i0 = jnp.clip(jnp.floor(pos), 0, KS - 2).astype(jnp.int32)
            frac = pos - i0
            combos = jnp.asarray(_COMBOS)
            basis = jnp.prod(jnp.where(combos[None] == 1, frac[:, None, :], 1.0 - frac[:, None, :]), axis=-1)
            idx = jnp.sum((i0[:, None, :] + combos[None]) * jnp.asarray(_STRIDES)[None, None, :], axis=-1)
            return (basis, idx)

        def spline_conv(x, row, col, basis, idx, W, b):
            N = x.shape[0]
            Fout = W.shape[2]
            z = jnp.einsum('ni,kio->nko', x, W).reshape(N * K, Fout)
            gathered = z[col[:, None] * K + idx]
            msg = jnp.einsum('es,eso->eo', basis, gathered)
            out = jax.ops.segment_sum(msg, row, num_segments=N)
            deg = jax.ops.segment_sum(jnp.ones_like(msg[:, 0]), row, num_segments=N)
            return out / jnp.maximum(deg, 1.0)[:, None] + b
        N = x.shape[0]
        row, col = (edge_index[0], edge_index[1])
        basis, idx = spline_basis(pseudo)
        h = jnp.ones((N, 1), x.dtype)
        h = jax.nn.elu(spline_conv(h, row, col, basis, idx, stn1_w, stn1_b))
        h = jax.nn.elu(spline_conv(h, row, col, basis, idx, stn2_w, stn2_b))
        h = jax.nn.elu(h @ stn3_w + stn3_b)
        t = h @ stn4_w + stn4_b
        new_pseudo = jnp.clip(pseudo + t[col] - t[row], 0.0, 1.0)
        basis2, idx2 = spline_basis(new_pseudo)
        return spline_conv(x, row, col, basis2, idx2, conv_w, conv_b)
    edge_index = jnp.stack([src, dst])
    h = jnp.maximum(_layernorm(x, axis=-1), 0.0)
    x = x + _L0_gnn_ref(h, edge_index, L0_gnn_w, L0_gnn_fc_w, L0_gnn_fc_b, L0_gnn_bias)
    h = jnp.maximum(_layernorm(x, axis=-1), 0.0)
    x = x + _L1_gnn_ref(h, edge_index, L1_gnn_W1_l, L1_gnn_b1, L1_gnn_W1_r, L1_gnn_W2_l, L1_gnn_b2, L1_gnn_W2_r)
    h = jnp.maximum(_layernorm(x, axis=-1), 0.0)
    x = x + _L2_gnn_ref(h, edge_index, edge_attr_2, L2_gnn_g, L2_gnn_mu, L2_gnn_sigma, L2_gnn_root, L2_gnn_bias)
    h = jnp.maximum(_layernorm(x, axis=-1), 0.0)
    x = x + _L3_gnn_ref(h, edge_index, edge_attr_3, L3_gnn_stn1_w, L3_gnn_stn1_b, L3_gnn_stn2_w, L3_gnn_stn2_b, L3_gnn_stn3_w, L3_gnn_stn3_b, L3_gnn_stn4_w, L3_gnn_stn4_b, L3_gnn_conv_w, L3_gnn_conv_b)
    return x

_drawn_inputs = setup_inputs


def setup_inputs(seed=0):
    import zlib

    import numpy as np

    out = dict(_drawn_inputs(seed))
    spreads = {'L0_gnn_bias': (0.0, 0.1),
     'L1_gnn_b1': (0.0, 0.1),
     'L1_gnn_b2': (0.0, 0.1),
     'L2_gnn_bias': (0.0, 0.1)}
    factors = {'edge_attr_2': 8.721,
     'edge_attr_3': 5.351,
     'L3_gnn_stn1_w': 8.0,
     'L3_gnn_stn1_b': 64.0,
     'L3_gnn_stn2_w': 8.0,
     'L3_gnn_stn2_b': 8.0,
     'L3_gnn_stn3_w': 8.0,
     'L3_gnn_stn3_b': 8.0,
     'L3_gnn_stn4_w': 8.0,
     'L3_gnn_stn4_b': 8.0,
     'L3_gnn_conv_w': 4.466,
     'L2_gnn_sigma': 3.477}
    for name, (base, spread) in spreads.items():
        noise = np.random.default_rng([zlib.crc32(name.encode()), seed]).standard_normal(out[name].shape)
        drawn = base * np.exp(spread * noise) if base else spread * noise
        out[name] = jnp.asarray(drawn.astype(out[name].dtype))
    for name, factor in factors.items():
        out[name] = (out[name] * factor).astype(out[name].dtype)
    return out
```

```python
from contextlib import ExitStack

import concourse.bass as bass
from concourse import mybir

F32 = mybir.dt.float32
I32 = mybir.dt.int32
BF16 = mybir.dt.bfloat16
ALU = mybir.AluOpType
ACT = mybir.ActivationFunctionType
AX = mybir.AxisListType

P = 128
N = 3125
E = 103125
NB = -(-N // P)
NP = NB * P
NH = NB + 1
HB = 13
STEPS = E // (HB * P) + 1
EP = STEPS * HB * P
PAD_KEY = NB * P
PAD_START = 5.0e7
BIG = 1.0e30
TB = 32
F = 32
EPS_LN = 1e-5


class Order:

    def __init__(self, name, chunk, words, pairs):
        self.name, self.chunk, self.words, self.pairs = name, chunk, words, pairs
        self.shift = chunk.bit_length() - 1
        self.per_tile = P // chunk
        self.blocks = 2 * pairs
        self.tiles = self.blocks * TB
        self.chunks = self.tiles * self.per_tile
        self.vb = TB * self.per_tile
        self.slots = self.tiles * P
        assert self.chunks >= N + E // chunk


class Shared:
    pass


class Chain:

    def __init__(self, eng, sem):
        self.eng, self.sem, self.n = eng, sem, 0

    def step(self, ins):
        ins.then_inc(self.sem, 1)
        self.n += 1
        self.eng.wait_ge(self.sem, self.n)

    def restart(self):
        self.eng.sem_clear(self.sem)
        self.n = 0


def new_sem(nc, c, name):
    handle = nc.alloc_semaphore(name)
    c.callback(nc.release_semaphore, handle)
    c.callback(nc.gpsimd.sem_clear, handle)
    return handle


def rows_sem(nc, name):
    return nc.alloc_semaphore(name)


def stage_setup(nc, g, ins):
    R, D = g.R, g.D
    with ExitStack() as c:
        sb = lambda name, shape, dt: c.enter_context(nc.sbuf_tensor(name, shape, dt))
        sem = lambda name: new_sem(nc, c, name)
        iota_i = sb("su_iota_i", [P, P], I32)
        pidx_i = sb("su_pidx_i", [P, 1], I32)
        node_i = sb("su_node_i", [P, NH], I32)
        node_f = sb("su_node_f", [P, NH], F32)
        pg_i = sb("su_pg_i", [P, 2], I32)
        pg_f = sb("su_pg_f", [P, 2], F32)
        cg_i = sb("su_cg_i", [P, P], I32)
        cg_f = sb("su_cg_f", [P, P], F32)
        fill_r = sb("su_fill_r", [P, R.tiles * R.words], I32)
        fill_d = sb("su_fill_d", [P, D.tiles * D.words], I32)
        zeros = sb("su_zeros", [P, 256], F32)
        pad_key = sb("su_pad_key", [1, EP - E], I32)
        iotas = sem("su_iotas")
        fills = sem("su_fills")
        copied = sem("su_copied")
        steps = sem("su_steps")
        with nc.Block() as block:
            @block.gpsimd
            def _(pool):
                nc.gpsimd.iota(iota_i[:], [[1, P]], base=0, channel_multiplier=0).then_inc(iotas, 1)
                nc.gpsimd.iota(pidx_i[:], [[0, 1]], base=0, channel_multiplier=1).then_inc(iotas, 1)
                nc.gpsimd.iota(node_i[:], [[P, NH]], base=0, channel_multiplier=1).then_inc(iotas, 1)
                nc.gpsimd.memset(zeros[:], 0.0).then_inc(fills, 1)
                nc.gpsimd.memset(pad_key[:], PAD_KEY).then_inc(fills, 1)

            @block.vector
            def _(dve):
                ch = Chain(dve, steps)
                for o, fill in ((R, fill_r), (D, fill_d)):
                    ch.step(nc.vector.memset(fill[:], 0))
                    nc.vector.memset(fill[:].rearrange("p (t w) -> p t w", w=o.words)[:, :, 0], N).then_inc(fills, 1)
                nc.vector.memset(g.ones[:], 1.0)
                nc.vector.memset(g.zero_bf[:], 0.0)
                dve.wait_ge(iotas, 3)
                nc.vector.tensor_copy(g.iota_row[:], iota_i[:])
                ch.step(nc.vector.tensor_copy(g.pidx[:], pidx_i[:]))
                ch.step(nc.vector.tensor_copy(node_f[:], node_i[:]))
                nc.vector.tensor_scalar(g.valid[:], node_f[:, 0:NB], float(N), None, ALU.is_lt)
                for k, o in enumerate((R, D)):
                    nc.vector.tensor_scalar(pg_i[:, k:k + 1], pidx_i[:], o.shift, None, ALU.logical_shift_right)
                ch.step(nc.vector.tensor_scalar(cg_i[:], iota_i[:], R.shift, None, ALU.logical_shift_right))
                nc.vector.tensor_copy(pg_f[:], pg_i[:])
                ch.step(nc.vector.tensor_copy(cg_f[:], cg_i[:]))
                nc.vector.tensor_scalar(g.ident[:], g.iota_row[:], g.pidx[:], None, ALU.is_equal)
                nc.vector.tensor_scalar(g.below[:], g.iota_row[:], g.pidx[:], None, ALU.is_gt)
                nc.vector.tensor_scalar(g.before[:], g.iota_row[:], g.pidx[:], None, ALU.is_lt)
                nc.vector.tensor_scalar(R.mask[:], g.iota_row[:, 0:R.per_tile], pg_f[:, 0:1], None, ALU.is_equal)
                nc.vector.tensor_scalar(D.mask[:], g.iota_row[:, 0:D.per_tile], pg_f[:, 1:2], None, ALU.is_equal)
                nc.vector.tensor_scalar(R.mask_t[:], cg_f[0:R.per_tile, :], g.pidx[0:R.per_tile, :], None, ALU.is_equal)

            @block.sync
            def _(sp):
                for name, width in (("src", 1), ("dst", 1), ("edge_attr_3", 3), ("edge_attr_2", 2)):
                    flat = ins[name] if width == 1 else ins[name].rearrange("e w -> (e w)")
                    sp.dma_start(g.pad[name][0:E * width].rearrange("(p f) -> p f", p=125),
                                 flat.rearrange("(p f) -> p f", p=125)).then_inc(copied, 16)
                sp.wait_ge(fills, 4)
                for name in ("src", "dst"):
                    sp.dma_start(g.pad[name][E:EP].rearrange("(p f) -> p f", p=1), pad_key[:]).then_inc(copied, 16)
                for name, width in (("edge_attr_3", 3), ("edge_attr_2", 2)):
                    sp.dma_start(g.pad[name][E * width:EP * width].rearrange("(p f) -> p f", p=1),
                                 zeros[0:1, 0:(EP - E) * width]).then_inc(copied, 16)
                for o, fill in ((R, fill_r), (D, fill_d)):
                    sp.dma_start(o.rec.rearrange("(p t) w -> p (t w)", p=P), fill[:]).then_inc(copied, 16)
                    sp.dma_start(o.first.rearrange("(p f) w -> p (f w)", p=P), zeros[:, 0:o.chunks // P]).then_inc(copied, 16)
                sp.wait_ge(copied, 12 * 16)


def stage_histogram(nc, g):
    keys = ("src", "dst")
    with ExitStack() as c:
        sb = lambda name, shape, dt: c.enter_context(nc.sbuf_tensor(name, shape, dt))
        sem = lambda name: new_sem(nc, c, name)
        lo_i = sb("hi_lo_i", [P, STEPS * HB], I32)
        hi_i = sb("hi_hi_i", [P, STEPS * HB], I32)
        lo1 = [sb(f"hi_lo1_{i}", [P, HB, P], BF16) for i in range(4)]
        hi1 = [sb(f"hi_hi1_{i}", [P, HB, NH], BF16) for i in range(4)]
        count = [c.enter_context(nc.psum_tensor(f"hi_count_{k}", [P, NH], F32)) for k in keys]
        loaded, steps = sem("hi_loaded"), sem("hi_steps")
        onehots, counted = sem("hi_onehots"), sem("hi_counted")
        with nc.Block() as block:
            @block.sync
            def _(sp):
                for k in keys:
                    sp.dma_start(g.key_i[k][:].rearrange("p (s j) -> p s j", j=HB),
                                 g.pad[k].rearrange("(s p j) -> p s j", p=P, j=HB)).then_inc(loaded, 16)
                for name, width in (("edge_attr_3", 3), ("edge_attr_2", 2)):
                    sp.dma_start(g.attr[name][:].rearrange("p (s j) -> p s j", j=HB * width),
                                 g.pad[name].rearrange("(s p j) -> p s j", p=P, j=HB * width)).then_inc(loaded, 16)
                sp.wait_ge(loaded, 64)

            @block.vector
            def _(dve):
                ch = Chain(dve, steps)
                dve.wait_ge(loaded, 64)
                for k in keys:
                    ch.step(nc.vector.tensor_copy(g.key_f[k][:], g.key_i[k][:]))
                    ch.step(nc.vector.tensor_scalar(lo_i[:], g.key_i[k][:], P - 1, None, ALU.bitwise_and))
                    ch.step(nc.vector.tensor_scalar(hi_i[:], g.key_i[k][:], 7, None, ALU.logical_shift_right))
                    ch.step(nc.vector.tensor_copy(g.lo[k][:], lo_i[:]))
                    ch.step(nc.vector.tensor_copy(g.hi[k][:], hi_i[:]))

                def half(step, slot, k):
                    cols = bass.ds(step * HB, HB)
                    nc.vector.tensor_tensor(lo1[slot][:], g.iota_row[:].unsqueeze(1).to_broadcast([P, HB, P]),
                                            g.lo[k][:, cols].unsqueeze(2).to_broadcast([P, HB, P]), ALU.is_equal)
                    nc.vector.tensor_tensor(hi1[slot][:], g.iota_row[:, 0:NH].unsqueeze(1).to_broadcast([P, HB, NH]),
                                            g.hi[k][:, cols].unsqueeze(2).to_broadcast([P, HB, NH]),
                                            ALU.is_equal).then_inc(onehots, 1)

                for slot in range(4):
                    half(slot // 2, slot, keys[slot % 2])
                with dve.Fori(1, STEPS // 2) as i:
                    for slot in range(4):
                        dve.wait_ge(counted, i * 4 + (slot - 3))
                        half(i * 2 + slot // 2, slot, keys[slot % 2])
                dve.wait_ge(counted, STEPS * 2 + 2)
                for k, cnt in zip(keys, count):
                    nc.vector.tensor_copy(g.degree[k][:], cnt[:])

            @block.tensor
            def _(pe):
                for cnt in count:
                    nc.tensor.matmul(cnt[:], g.zero_bf[:], g.zero_bf[:, 0:NH], start=True, stop=False)
                with pe.Fori(0, STEPS // 2) as i:
                    for slot in range(4):
                        pe.wait_ge(onehots, i * 4 + (slot + 1))
                        for j in range(HB):
                            last = nc.tensor.matmul(count[slot % 2][:], lo1[slot][:, j, :], hi1[slot][:, j, :],
                                                    start=False, stop=False)
                        last.then_inc(counted, 1)
                for cnt in count:
                    nc.tensor.matmul(cnt[:], g.zero_bf[:], g.zero_bf[:, 0:NH],
                                     start=False, stop=True).then_inc(counted, 1)


def stage_starts(nc, g):
    with ExitStack() as c:
        sb = lambda name, shape, dt: c.enter_context(nc.sbuf_tensor(name, shape, dt))
        sem = lambda name: new_sem(nc, c, name)
        tmp_i = sb("st_tmp_i", [P, NB], I32)
        need = sb("st_need", [P, NB], F32)
        total = sb("st_total", [P, NB], F32)
        upto = sb("st_upto", [P, NB], F32)
        start = sb("st_start", [P, NB], F32)
        marked = sb("st_marked", [P, NB], F32)
        mark = [sb(f"st_mark_{o.name}", [P, NB], I32) for o in g.orders]
        ps_in = c.enter_context(nc.psum_tensor("st_ps_in", [P, NB], F32))
        ps_tot = c.enter_context(nc.psum_tensor("st_ps_tot", [P, NB], F32))
        steps, needed, summed = sem("st_steps"), sem("st_needed"), sem("st_summed")
        ready, scattered = sem("st_ready"), rows_sem(nc, "st_scattered")
        with nc.Block() as block:
            @block.vector
            def _(dve):
                ch = Chain(dve, steps)
                for n, o in enumerate(g.orders):
                    deg = g.degree[o.key][:, 0:NB]
                    ch.step(nc.vector.tensor_scalar(o.inv_degree[:], deg, 1.0, None, ALU.max))
                    ch.step(nc.vector.reciprocal(o.inv_degree[:], o.inv_degree[:]))
                    ch.step(nc.vector.tensor_scalar(tmp_i[:], deg, float(o.chunk - 1), None, ALU.add))
                    ch.step(nc.vector.tensor_scalar(tmp_i[:], tmp_i[:], o.shift, None, ALU.logical_shift_right))
                    ch.step(nc.vector.tensor_copy(need[:], tmp_i[:]))
                    ch.step(nc.vector.scalar_tensor_tensor(need[:], need[:], 1.0, g.valid[:], ALU.max, ALU.mult))
                    dve.sem_inc(needed, 1)
                    dve.wait_ge(summed, n + 1)
                    ch.step(nc.vector.tensor_copy(total[:], ps_tot[:]))
                    ch.step(nc.vector.tensor_tensor_scan(upto[:], g.ones[:, 0:NB], total[:], 0.0, ALU.mult, ALU.add))
                    ch.step(nc.vector.tensor_sub(upto[:], upto[:], total[:]))
                    ch.step(nc.vector.tensor_add(start[:], ps_in[:], upto[:]))
                    nc.vector.memset(o.slot0[:, NB:NH], PAD_START)
                    ch.step(nc.vector.tensor_scalar(o.slot0[:, 0:NB], start[:], float(o.chunk), None, ALU.mult))
                    ch.step(nc.vector.tensor_add(marked[:], start[:], need[:]))
                    ch.step(nc.vector.tensor_scalar(marked[:], marked[:], -1.0, None, ALU.add))
                    ch.step(nc.vector.tensor_copy(o.last[:], marked[:]))
                    ch.step(nc.vector.tensor_scalar(marked[:], g.valid[:], -PAD_START, PAD_START, ALU.mult, ALU.add))
                    ch.step(nc.vector.tensor_add(marked[:], marked[:], start[:]))
                    nc.vector.tensor_copy(mark[n][:], marked[:]).then_inc(ready, 1)

            @block.tensor
            def _(pe):
                for n, o in enumerate(g.orders):
                    pe.wait_ge(needed, n + 1)
                    nc.tensor.matmul(ps_in[:], g.below[:], need[:], start=True, stop=True)
                    nc.tensor.matmul(ps_tot[:], g.ones[:], need[:], start=True, stop=True).then_inc(summed, 1)

            @block.gpsimd
            def _(pool):
                for n, o in enumerate(g.orders):
                    pool.wait_ge(ready, n + 1)
                    for b in range(NB):
                        pool.indirect_dma_start(
                            out=o.first[:, :], out_offset=bass.IndirectOffsetOnAxis(ap=mark[n][:, b:b + 1], axis=0),
                            in_=g.ones[:, 0:1], in_offset=None, bounds_check=o.chunks - 1,
                            oob_is_err=False).then_inc(scattered, 16)
                pool.wait_ge(scattered, 2 * NB * 16)


def stage_sort(nc, g, o):
    W = o.words
    A = W - 1
    with ExitStack() as c:
        sb = lambda name, shape, dt: c.enter_context(nc.sbuf_tensor(f"so_{o.name}_{name}", shape, dt))
        ps = lambda name, shape: c.enter_context(nc.psum_tensor(f"so_{o.name}_{name}", shape, F32))
        sem = lambda name: new_sem(nc, c, f"so_{o.name}_{name}")
        two = range(2)
        row = [sb(f"row{i}", [P, P * HB], I32) for i in two]
        row_lo = sb("row_lo", [P, P * HB], I32)
        lo_t = [sb(f"lo_t{i}", [P, P, HB], F32) for i in two]
        lo1 = [sb(f"lo1{i}", [P, HB, P], BF16) for i in two]
        hi1 = [sb(f"hi1{i}", [P, HB, NH], BF16) for i in two]
        same = sb("same", [P, HB, P], BF16)
        rank = [sb(f"rank{i}", [P, HB], F32) for i in two]
        table = [sb(f"table{i}", [P, HB + 1, NH], F32) for i in two]
        pick = sb("pick", [P, HB, NH], F32)
        slot = sb("slot", [P, HB], F32)
        slot_i = sb("slot_i", [P, HB], I32)
        part_i = sb("part_i", [P, HB], I32)
        part = sb("part", [P, HB], F32)
        place = [sb(f"place{i}", [P, HB], I32) for i in two]
        rec = [sb(f"rec{i}", [P, HB, W], I32) for i in two]
        ps_hist = [ps(f"hist{i}", [P, HB, NH]) for i in two]
        ps_look = [ps(f"look{i}", [P, HB, NH]) for i in two]
        row_in = [sem(f"row_in{i}") for i in two]
        row_used, onehots, hist, tables, looked = sem("row_used"), sem("onehots"), sem("hist"), sem("tables"), sem("looked")
        looks_read, placed, taken = sem("looks_read"), sem("placed"), sem("taken")
        scattered = [rows_sem(nc, f"so_{o.name}_scattered{i}") for i in two]
        steps = sem("steps")
        half = STEPS // 2
        with nc.Block() as block:
            @block.sync
            def _(sp):
                def load(step, b):
                    src = g.pad[o.key][bass.ds(step * (P * HB), P * HB)]
                    sp.dma_start(row[b][:], src.rearrange("(a f) -> a f", a=1).to_broadcast([P, P * HB])).then_inc(row_in[b], 16)

                for b in two:
                    load(b, b)
                with sp.Fori(1, half) as i:
                    for b in two:
                        sp.wait_ge(row_used, i * 2 + (b - 1))
                        load(i * 2 + b, b)
                sp.wait_ge(row_in[0], 16 * half)
                sp.wait_ge(row_in[1], 16 * half)

            @block.vector
            def _(dve):
                ch = Chain(dve, steps)

                def digits(step, b, turn, first):
                    cols = bass.ds(step * HB, HB)
                    dve.wait_ge(row_in[b], turn * 16 + 16)
                    nc.vector.tensor_tensor(lo1[b][:], g.iota_row[:].unsqueeze(1).to_broadcast([P, HB, P]),
                                            g.lo[o.key][:, cols].unsqueeze(2).to_broadcast([P, HB, P]), ALU.is_equal)
                    nc.vector.tensor_tensor(hi1[b][:], g.iota_row[:, 0:NH].unsqueeze(1).to_broadcast([P, HB, NH]),
                                            g.hi[o.key][:, cols].unsqueeze(2).to_broadcast([P, HB, NH]),
                                            ALU.is_equal).then_inc(onehots, 1)
                    ch.step(nc.vector.tensor_scalar(row_lo[:], row[b][:], P - 1, None, ALU.bitwise_and))
                    nc.vector.tensor_scalar(lo_t[b][:].rearrange("p e j -> p (e j)"), row_lo[:], g.pidx[:], None, ALU.is_equal)
                    keys = row[b][:].rearrange("p (e j) -> p e j", j=HB)
                    for j in range(HB):
                        last = nc.vector.scalar_tensor_tensor(same[:, j, :], keys[:, :, j], g.key_f[o.key][:, bass.ds(step * HB + j, 1)],
                                                              g.before[:], ALU.is_equal, ALU.mult, accum_out=rank[b][:, j:j + 1])
                    last.then_inc(row_used, 1)
                    dve.wait_ge(hist, step + 1)
                    if first:
                        ch.step(nc.vector.tensor_copy(table[b][:, 0, :], o.slot0[:]))
                    else:
                        ch.step(nc.vector.tensor_copy(table[b][:, 0, :], table[1 - b][:, HB, :]))
                    for j in range(HB):
                        ins = nc.vector.tensor_add(table[b][:, j + 1, :], table[b][:, j, :], ps_hist[b][:, j, :])
                        ch.step(ins)
                    dve.sem_inc(tables, 1)

                def places(step, b, turn, first):
                    cols = bass.ds(step * HB, HB)
                    dve.wait_ge(looked, step + 1)
                    nc.vector.tensor_mul(pick[:], ps_look[b][:], hi1[b][:]).then_inc(looks_read, 1)
                    dve.wait_ge(looks_read, step + 1)
                    ch.step(nc.vector.tensor_reduce(slot[:], pick[:], AX.X, ALU.add))
                    ch.step(nc.vector.tensor_add(slot[:], slot[:], rank[b][:]))
                    ch.step(nc.vector.tensor_copy(slot_i[:], slot[:]))
                    ch.step(nc.vector.tensor_scalar(part_i[:], slot_i[:], P - 1, None, ALU.bitwise_and))
                    ch.step(nc.vector.tensor_copy(part[:], part_i[:]))
                    ch.step(nc.vector.tensor_scalar(slot_i[:], slot_i[:], 7, None, ALU.logical_shift_right))
                    ch.step(nc.vector.tensor_copy(slot[:], slot_i[:]))
                    if not first:
                        dve.wait_ge(scattered[b], turn * (16 * HB))
                    nc.vector.scalar_tensor_tensor(place[b][:], part[:], float(o.tiles), slot[:], ALU.mult, ALU.add)
                    nc.vector.tensor_copy(rec[b][:, :, 0], g.key_i[o.other][:, cols])
                    nc.vector.tensor_copy(rec[b][:, :, 1:W].bitcast(F32),
                                          g.attr[o.attr][:, bass.ds(step * (HB * A), HB * A)].rearrange("p (j a) -> p j a", a=A)).then_inc(placed, 1)

                digits(0, 0, 0, True)
                digits(1, 1, 0, False)
                places(0, 0, 0, True)
                ch.restart()
                digits(2, 0, 1, False)
                places(1, 1, 0, True)
                with dve.Fori(1, half - 1) as i:
                    ch.restart()
                    digits(i * 2 + 1, 1, i, False)
                    places(i * 2, 0, i, False)
                    digits(i * 2 + 2, 0, i + 1, False)
                    places(i * 2 + 1, 1, i, False)
                ch.restart()
                digits(STEPS - 1, 1, half - 1, False)
                places(STEPS - 2, 0, half - 1, False)
                places(STEPS - 1, 1, half - 1, False)

            @block.tensor
            def _(pe):
                def histograms(step, b):
                    pe.wait_ge(onehots, step + 1)
                    for j in range(HB):
                        last = nc.tensor.matmul(ps_hist[b][:, j, :], lo1[b][:, j, :], hi1[b][:, j, :], start=True, stop=True)
                    last.then_inc(hist, 1)

                def lookups(step, b):
                    pe.wait_ge(tables, step + 1)
                    for j in range(HB):
                        last = nc.tensor.matmul(ps_look[b][:, j, :], lo_t[b][:, :, j], table[b][:, j, :], start=True, stop=True)
                    last.then_inc(looked, 1)

                histograms(0, 0)
                lookups(0, 0)
                with pe.Fori(0, half - 1) as i:
                    histograms(i * 2 + 1, 1)
                    lookups(i * 2 + 1, 1)
                    histograms(i * 2 + 2, 0)
                    lookups(i * 2 + 2, 0)
                histograms(STEPS - 1, 1)
                lookups(STEPS - 1, 1)

            @block.gpsimd
            def _(pool):
                bound = pool.to_reg(o.slots - 1)
                with pool.Fori(0, half) as i:
                    for b in two:
                        pool.wait_ge(placed, i * 2 + (b + 1))
                        pool.sem_inc(taken, 1)
                        for j in range(HB):
                            pool.indirect_dma_start(
                                out=o.rec[:, :], out_offset=bass.IndirectOffsetOnAxis(ap=place[b][:, j:j + 1], axis=0),
                                in_=rec[b][:, j, :], in_offset=None, bounds_check=bound,
                                oob_is_err=False).then_inc(scattered[b], 16)
                for b in two:
                    pool.wait_ge(scattered[b], half * 16 * HB)



def stage_chunks(nc, g):
    with ExitStack() as c:
        sb = lambda name, shape, dt=F32: c.enter_context(nc.sbuf_tensor(name, shape, dt))
        sem = lambda name: new_sem(nc, c, name)
        first = {o.name: sb(f"ck_first_{o.name}", [P, o.chunks // P]) for o in g.orders}
        keep = {o.name: sb(f"ck_keep_{o.name}", [P, o.chunks // P]) for o in g.orders}
        line = sb("ck_line", [1, g.R.chunks])
        line_one = sb("ck_line_one", [1, g.R.chunks])
        nodes = sb("ck_nodes", [1, g.R.chunks])
        nodes_i = sb("ck_nodes_i", [1, g.R.chunks], I32)
        loaded, steps, made, stored = sem("ck_loaded"), sem("ck_steps"), sem("ck_made"), sem("ck_stored")
        with nc.Block() as block:
            @block.sync
            def _(sp):
                for o in g.orders:
                    sp.dma_start(first[o.name][:], o.first.rearrange("(p f) w -> p (f w)", p=P)).then_inc(loaded, 16)
                sp.dma_start(line[:], g.R.first.rearrange("v w -> w v")).then_inc(loaded, 16)
                sp.wait_ge(made, 2)
                for o in g.orders:
                    sp.dma_start(o.keep.rearrange("(p f) -> p f", p=P), keep[o.name][:]).then_inc(stored, 16)
                sp.wait_ge(made, 3)
                sp.dma_start(g.chunk_node.rearrange("(a v) -> a v", a=1), nodes_i[:]).then_inc(stored, 16)
                sp.wait_ge(stored, 48)
                sp.dma_start(g.chunk_row[:], g.chunk_node.rearrange("(p f) -> p f", p=P)).then_inc(loaded, 16)
                sp.wait_ge(loaded, 64)

            @block.vector
            def _(dve):
                ch = Chain(dve, steps)
                ch.step(nc.vector.memset(line_one[:], 1.0))
                dve.wait_ge(loaded, 48)
                for o in g.orders:
                    nc.vector.tensor_scalar(keep[o.name][:], first[o.name][:], -1.0, 1.0, ALU.mult, ALU.add).then_inc(made, 1)
                ch.step(nc.vector.tensor_tensor_scan(nodes[:], line_one[:], line[:], -1.0, ALU.mult, ALU.add))
                nc.vector.tensor_copy(nodes_i[:], nodes[:]).then_inc(made, 1)


def stage_spread(nc, g, name, table, width, to):
    per = g.R.chunks // P
    with ExitStack() as c:
        rows = c.enter_context(nc.sbuf_tensor(f"{name}_rows", [P, per, width], F32))
        got, stored = rows_sem(nc, f"{name}_got"), new_sem(nc, c, f"{name}_stored")
        with nc.Block() as block:
            @block.gpsimd
            def _(pool):
                for j in range(per):
                    pool.indirect_dma_start(out=rows[:, j, :], out_offset=None, in_=table[:, :],
                                            in_offset=bass.IndirectOffsetOnAxis(ap=g.chunk_row[:, j:j + 1], axis=0)).then_inc(got, 16)

            @block.sync
            def _(sp):
                sp.wait_ge(got, 16 * per)
                sp.dma_start(to.rearrange("(p f) w -> p (f w)", p=P), rows[:].rearrange("p f w -> p (f w)")).then_inc(stored, 16)
                sp.wait_ge(stored, 16)


def stage_collect(nc, g, name, o, sums, width, to):
    with ExitStack() as c:
        got = rows_sem(nc, f"{name}_got")
        with nc.Block() as block:
            @block.gpsimd
            def _(pool):
                for b in range(NB):
                    pool.indirect_dma_start(out=to[:, b, :], out_offset=None, in_=sums[:, :],
                                            in_offset=bass.IndirectOffsetOnAxis(ap=o.last[:, b:b + 1], axis=0)).then_inc(got, 16)
                pool.wait_ge(got, 16 * NB)


def stage_dense(nc, g, name, src, k, weights, width, dst, weight_parts):
    G5 = 5
    with ExitStack() as c:
        sb = lambda nm, shape, dt=F32: c.enter_context(nc.sbuf_tensor(f"{name}_{nm}", shape, dt))
        sem = lambda nm: new_sem(nc, c, f"{name}_{nm}")
        rows = sb("rows", [P, G5, k])
        cols = sb("cols", [k, G5, P])
        ps_t = [c.enter_context(nc.psum_tensor(f"{name}_ps_t{i}", [k, 4, P], F32)) for i in range(2)]
        ps_o = c.enter_context(nc.psum_tensor(f"{name}_ps_o", [P, G5, width], F32))
        loaded, staged, turned, copied, done, taken, seen = (
            sem(n) for n in ("loaded", "staged", "turned", "copied", "done", "taken", "seen"))
        with nc.Block() as block:
            @block.sync
            def _(sp):
                for to, view in weight_parts:
                    sp.dma_start(to, view).then_inc(loaded, 16)
                if weight_parts:
                    sp.wait_ge(loaded, 16 * len(weight_parts))

            @block.vector
            def _(dve):
                with dve.Fori(0, NB // G5) as i:
                    nc.vector.tensor_copy(rows[:], src[:, bass.ds(i * G5, G5), 0:k]).then_inc(staged, 1)
                    dve.wait_ge(done, i + 1)
                    nc.vector.tensor_copy(dst[:, bass.ds(i * G5, G5), :], ps_o[:]).then_inc(taken, 1)
                    dve.wait_ge(taken, i + 1)

            @block.tensor
            def _(pe):
                if weight_parts:
                    pe.wait_ge(loaded, 16 * len(weight_parts))
                with pe.Fori(0, NB // G5) as i:
                    pe.wait_ge(staged, i + 1)
                    pe.sem_inc(seen, 1)
                    for j in range(G5):
                        last = nc.tensor.transpose(ps_t[j // 4][:, j % 4, :], rows[:, j, :], g.ident[:])
                    last.then_inc(turned, 1)
                    pe.wait_ge(copied, i + 1)
                    for j in range(G5):
                        last = nc.tensor.matmul(ps_o[:, j, :], cols[:, j, :], weights, start=True, stop=True)
                    last.then_inc(done, 1)

            @block.scalar
            def _(act):
                with act.Fori(0, NB // G5) as i:
                    act.wait_ge(turned, i + 1)
                    nc.scalar.copy(cols[:, 0:4, :], ps_t[0][:])
                    nc.scalar.copy(cols[:, 4:5, :], ps_t[1][:, 0:1, :]).then_inc(copied, 1)


def layernorm(ch, nc, g, t, out, act):
    b3 = lambda ap: ap.unsqueeze(2).to_broadcast([P, NB, F])
    ch.step(nc.vector.tensor_reduce(t.mean[:], g.x[:], AX.X, ALU.add))
    ch.step(nc.vector.tensor_scalar(t.mean[:], t.mean[:], 1.0 / F, None, ALU.mult))
    ch.step(nc.vector.tensor_sub(t.centred[:], g.x[:], b3(t.mean[:])))
    ch.step(nc.vector.tensor_mul(t.square[:], t.centred[:], t.centred[:]))
    ch.step(nc.vector.tensor_reduce(t.var[:], t.square[:], AX.X, ALU.add))
    ch.step(nc.vector.tensor_scalar(t.var[:], t.var[:], 1.0 / F, EPS_LN, ALU.mult, ALU.add))
    act(t.var[:], ACT.Sqrt)
    ch.step(nc.vector.reciprocal(t.var[:], t.var[:]))
    ch.step(nc.vector.tensor_mul(t.centred[:], t.centred[:], b3(t.var[:])))
    ch.step(nc.vector.tensor_scalar(t.centred[:], t.centred[:], 0.0, None, ALU.max))
    ch.step(nc.vector.tensor_mul(out, t.centred[:], b3(g.valid[:])))


class NormBuffers:
    def __init__(self, nc, c, name):
        sb = lambda nm, shape: c.enter_context(nc.sbuf_tensor(f"{name}_{nm}", shape, F32))
        self.mean, self.var = sb("mean", [P, NB]), sb("var", [P, NB])
        self.centred, self.square = sb("centred", [P, NB, F]), sb("square", [P, NB, F])


def node_rows(table):
    return table.rearrange("(b p) w -> p b w", p=P)



def stage_attention_inputs(nc, g, ins):
    with ExitStack() as c:
        sb = lambda name, shape, dt=F32: c.enter_context(nc.sbuf_tensor(name, shape, dt))
        sem = lambda name: new_sem(nc, c, name)
        w = sb("a0_w", [F, 4, F])
        fc = sb("a0_fc", [F, 2 * F])
        prod = sb("a0_prod", [F, 4, F])
        loaded, steps, zeroed = sem("a0_loaded"), sem("a0_steps"), sem("a0_zeroed")
        full = (NB - 1) * P
        with nc.Block() as block:
            @block.gpsimd
            def _(pool):
                nc.gpsimd.memset(g.x[:], 0.0).then_inc(zeroed, 1)

            @block.sync
            def _(sp):
                sp.dma_start(w[:], ins["L0_gnn_w"].rearrange("h f o -> f h o")).then_inc(loaded, 16)
                sp.dma_start(fc[:], ins["L0_gnn_fc_w"].to_broadcast([F, 2 * F])).then_inc(loaded, 16)
                sp.wait_ge(zeroed, 1)
                sp.dma_start(g.x[:, 0:NB - 1, :], ins["x"][0:full, :].rearrange("(b p) f -> p b f", p=P)).then_inc(loaded, 16)
                sp.dma_start(g.x[0:N - full, NB - 1, :], ins["x"][full:N, :]).then_inc(loaded, 16)
                sp.wait_ge(loaded, 64)

            @block.vector
            def _(dve):
                ch = Chain(dve, steps)
                dve.wait_ge(loaded, 64)
                for half in range(2):
                    ch.step(nc.vector.tensor_mul(prod[:], w[:], fc[:, half * F:(half + 1) * F].unsqueeze(1).to_broadcast([F, 4, F])))
                    ch.step(nc.vector.tensor_reduce(g.att_w[:, half * 4:half * 4 + 4], prod[:], AX.X, ALU.add))


def stage_attention_tables(nc, g, ins):
    with ExitStack() as c:
        sb = lambda name, shape, dt=F32: c.enter_context(nc.sbuf_tensor(name, shape, dt))
        sem = lambda name: new_sem(nc, c, name)
        row = sb("a1_row", [P, NB, 37])
        near = sb("a1_near", [P, NB, 4])
        off = sb("a1_off", [P, NB])
        fc_b = sb("a1_fc_b", [P, 1])
        loaded, steps, made, stored = sem("a1_loaded"), sem("a1_steps"), sem("a1_made"), sem("a1_stored")
        with nc.Block() as block:
            @block.sync
            def _(sp):
                sp.dma_start(fc_b[:], ins["L0_gnn_fc_b"].rearrange("(a b) -> a b", a=1).to_broadcast([P, 1])).then_inc(loaded, 16)
                sp.wait_ge(made, 1)
                sp.dma_start(node_rows(g.att_table), row[:]).then_inc(stored, 16)
                sp.dma_start(node_rows(g.near_table), near[:]).then_inc(stored, 16)
                sp.wait_ge(stored, 32)

            @block.vector
            def _(dve):
                ch = Chain(dve, steps)
                nc.vector.tensor_copy(row[:, :, 0:F], g.h[:])
                nc.vector.tensor_copy(row[:, :, F], g.valid[:])
                ch.step(nc.vector.tensor_scalar(off[:], g.valid[:], BIG, -BIG, ALU.mult, ALU.add))
                ch.step(nc.vector.tensor_add(row[:, :, F + 1:F + 5], g.att[:, :, 4:8], off[:].unsqueeze(2).to_broadcast([P, NB, 4])))
                dve.wait_ge(loaded, 16)
                nc.vector.tensor_scalar(near[:], g.att[:, :, 0:4], fc_b[:], None, ALU.add).then_inc(made, 1)


def stage_attention(nc, g):
    o = g.R
    C8, S = o.per_tile, o.chunk
    with ExitStack() as c:
        sb = lambda name, shape, dt=F32: c.enter_context(nc.sbuf_tensor(f"at_{name}", shape, dt))
        ps = lambda name, shape: c.enter_context(nc.psum_tensor(f"at_{name}", shape, F32))
        sem = lambda name: new_sem(nc, c, f"at_{name}")
        two = range(2)
        rec = [sb(f"rec{b}", [P, TB, o.words], I32) for b in two]
        far = [sb(f"far{b}", [P, TB, 37]) for b in two]
        near = [sb(f"near{b}", [P, C8]) for b in two]
        score = sb("score", [P, C8, S])
        leaky = sb("leaky", [P, C8, S])
        shifted = sb("shifted", [P, C8, S])
        top = [sb(f"top{b}", [P, C8]) for b in two]
        prob = sb("prob", [P, P])
        term = sb("term", [P, 4, TB])
        spread = sb("spread", [P, TB, 4, C8])
        sums = [sb(f"sums{b}", [F + 1, 4, TB, C8]) for b in two]
        ps_far, ps_prob = ps("ps_far", [P, C8, S]), ps("ps_prob", [P, 4, TB])
        ps_sum = [ps(f"ps_sum{k}", [F + 1, TB // 2, 4, C8]) for k in two]
        rec_in, near_in = [sem(f"rec_in{b}") for b in two], [sem(f"near_in{b}") for b in two]
        far_in = [rows_sem(nc, f"at_far_in{b}") for b in two]
        sums_out, top_out = [sem(f"sums_out{b}") for b in two], [sem(f"top_out{b}") for b in two]
        steps, taken, terms = sem("steps"), sem("taken"), sem("terms")
        turned, shifts, probs, turned_back, spreads, summed, copied = (
            sem(n) for n in ("turned", "shifts", "probs", "turned_back", "spreads", "summed", "copied"))
        rec_v = o.rec.rearrange("(p t) w -> p t w", p=P)
        near_v = g.near_chunk.rearrange("(t c) h -> h t c", c=C8)
        with nc.Block() as block:
            @block.sync
            def _(sp):
                def load(n, b):
                    sp.dma_start(rec[b][:], rec_v[:, bass.ds(n * TB, TB), :]).then_inc(rec_in[b], 16)
                    for h in range(4):
                        sp.dma_start(near[b][h * TB:(h + 1) * TB, :], near_v[h, bass.ds(n * TB, TB), :],
                                     allow_slow_non_contiguous=True).then_inc(near_in[b], 16)

                for b in two:
                    load(b, b)
                with sp.Fori(1, o.pairs) as i:
                    for b in two:
                        sp.wait_ge(summed, i * 2 + b)
                        load(i * 2 + b, b)

            @block.gpsimd
            def _(pool):
                with pool.Fori(0, o.pairs) as i:
                    for b in two:
                        pool.wait_ge(rec_in[b], i * 16 + 16)
                        pool.sem_inc(taken, 1)
                        for t in range(TB):
                            pool.indirect_dma_start(out=far[b][:, t, :], out_offset=None, in_=g.att_table[:, :],
                                                    in_offset=bass.IndirectOffsetOnAxis(ap=rec[b][:, t, 0:1], axis=0)).then_inc(far_in[b], 16)

            @block.tensor
            def _(pe):
                pe.sem_inc(summed, 1)
                pe.sem_inc(turned, 1)
                pe.sem_inc(turned_back, 1)
                with pe.Fori(0, o.pairs) as i:
                    for b in two:
                        n = i * 2 + b
                        pe.wait_ge(terms, n + 1)
                        pe.wait_ge(shifts, n + 1)
                        nc.tensor.transpose(ps_far[:].rearrange("p c s -> p (c s)"),
                                            term[:].rearrange("p h t -> p (h t)"), g.ident[:]).then_inc(turned, 1)
                        pe.wait_ge(probs, n + 2)
                        nc.tensor.transpose(ps_prob[:].rearrange("p h t -> p (h t)"), prob[:], g.ident[:]).then_inc(turned_back, 1)
                        pe.wait_ge(spreads, n + 1)
                        pe.wait_ge(copied, n + 1)
                        for t in range(TB):
                            last = nc.tensor.matmul(ps_sum[t // (TB // 2)][:, t % (TB // 2), :, :], far[b][:, t, 0:F + 1],
                                                    spread[:, t, :, :], start=True, stop=True)
                        last.then_inc(summed, 1)

            @block.vector
            def _(dve):
                dve.sem_inc(shifts, 1)
                ch = Chain(dve, steps)
                with dve.Fori(0, o.pairs) as i:
                    ch.restart()
                    for b in two:
                        n = i * 2 + b
                        dve.wait_ge(turned, n + 2)
                        dve.wait_ge(near_in[b], i * 64 + 64)
                        ch.step(nc.vector.tensor_add(score[:], ps_far[:], near[b][:].unsqueeze(2).to_broadcast([P, C8, S])))
                        ch.step(nc.vector.scalar_tensor_tensor(leaky[:], score[:], 0.2, score[:], ALU.mult, ALU.max))
                        dve.wait_ge(top_out[b], i * 64 + 64)
                        ch.step(nc.vector.tensor_reduce(top[b][:], leaky[:], AX.X, ALU.max))
                        dve.wait_ge(probs, n + 1)
                        nc.vector.tensor_sub(shifted[:], leaky[:], top[b][:].unsqueeze(2).to_broadcast([P, C8, S])).then_inc(shifts, 1)
                        dve.wait_ge(turned_back, n + 2)
                        dve.wait_ge(summed, n + 1)
                        nc.vector.tensor_mul(spread[:], ps_prob[:].rearrange("p h t -> p t h").unsqueeze(3).to_broadcast([P, TB, 4, C8]),
                                             o.mask[:].unsqueeze(1).unsqueeze(1).to_broadcast([P, TB, 4, C8])).then_inc(spreads, 1)

            @block.scalar
            def _(act):
                act.sem_inc(copied, 1)
                act.sem_inc(probs, 1)
                for b in two:
                    act.sem_inc(top_out[b], 64)
                for b in two:
                    act.sem_inc(sums_out[b], 16)
                with act.Fori(0, o.pairs) as i:
                    for b in two:
                        n = i * 2 + b
                        act.wait_ge(far_in[b], i * (16 * TB) + 16 * TB)
                        act.wait_ge(turned, n + 1)
                        nc.scalar.copy(term[:], far[b][:, :, F + 1:F + 5].rearrange("p t h -> p h t")).then_inc(terms, 1)
                        act.wait_ge(shifts, n + 2)
                        act.wait_ge(turned_back, n + 1)
                        nc.scalar.activation(prob[:], shifted[:].rearrange("p c s -> p (c s)"), ACT.Exp).then_inc(probs, 1)
                        for h in range(4):
                            act.dma_start(g.top[h, bass.ds(n * o.vb, o.vb)].rearrange("(t c) -> t c", c=C8),
                                          top[b][h * TB:(h + 1) * TB, :]).then_inc(top_out[b], 16)
                        act.wait_ge(summed, n + 2)
                        act.wait_ge(sums_out[b], i * 16 + 16)
                        for k in two:
                            half = slice(k * (TB // 2), (k + 1) * (TB // 2))
                            last = nc.scalar.copy(sums[b][:, :, half, :].rearrange("f h t c -> f t h c"), ps_sum[k][:])
                        last.then_inc(copied, 1)
                        act.wait_ge(copied, n + 2)
                        act.dma_start(g.att_raw[:, bass.ds(n * (4 * o.vb), 4 * o.vb)],
                                      sums[b][:].rearrange("f h t c -> f (h t c)")).then_inc(sums_out[b], 16)
                for b in two:
                    act.wait_ge(sums_out[b], 16 * o.pairs + 16)
                    act.wait_ge(top_out[b], 64 * o.pairs + 64)


def stage_attention_factors(nc, g):
    o = g.R
    V = o.chunks
    with ExitStack() as c:
        sb = lambda name, shape, dt=F32: c.enter_context(nc.sbuf_tensor(f"af_{name}", shape, dt))
        sem = lambda name: new_sem(nc, c, f"af_{name}")
        top, keep, upto = sb("top", [4, V]), sb("keep", [4, V]), sb("upto", [4, V])
        decay = sb("decay", [4, V])
        loaded, steps, differences, exps, made, stored = (sem(n) for n in ("loaded", "steps", "differences", "exps", "made", "stored"))
        with nc.Block() as block:
            @block.sync
            def _(sp):
                sp.dma_start(top[:], g.top).then_inc(loaded, 16)
                sp.dma_start(keep[:], o.keep.rearrange("(a v) -> a v", a=1).to_broadcast([4, V])).then_inc(loaded, 16)
                sp.wait_ge(exps, 1)
                sp.dma_start(g.factor, top[:]).then_inc(stored, 16)
                sp.wait_ge(made, 1)
                sp.dma_start(g.decay, decay[:]).then_inc(stored, 16)
                sp.wait_ge(stored, 32)

            @block.vector
            def _(dve):
                ch = Chain(dve, steps)
                dve.wait_ge(loaded, 32)
                ch.step(nc.vector.tensor_scalar(decay[:], keep[:], 1.0e38, -1.0e38, ALU.mult, ALU.add))
                ch.step(nc.vector.tensor_tensor_scan(upto[:], decay[:], top[:], 0.0, ALU.add, ALU.max))
                nc.vector.tensor_sub(top[:], top[:], upto[:]).then_inc(differences, 1)
                ch.step(nc.vector.memset(decay[:, 0:1], 0.0))
                ch.step(nc.vector.tensor_sub(decay[:, 1:V], upto[:, 0:V - 1], upto[:, 1:V]))
                nc.vector.tensor_scalar(decay[:], decay[:], 0.0, None, ALU.min).then_inc(differences, 1)
                dve.wait_ge(exps, 2)
                nc.vector.tensor_mul(decay[:], decay[:], keep[:]).then_inc(made, 1)

            @block.scalar
            def _(act):
                act.wait_ge(differences, 1)
                nc.scalar.activation(top[:], top[:], ACT.Exp).then_inc(exps, 1)
                act.wait_ge(differences, 2)
                nc.scalar.activation(decay[:], decay[:], ACT.Exp).then_inc(exps, 1)


def stage_attention_join(nc, g):
    o = g.R
    V, W = o.vb, 4 * (F + 1)
    parts = V // P
    with ExitStack() as c:
        sb = lambda name, shape, dt=F32: c.enter_context(nc.sbuf_tensor(f"aj_{name}", shape, dt))
        sem = lambda name: new_sem(nc, c, f"aj_{name}")
        two = range(2)
        raw = [sb(f"raw{b}", [F + 1, 4, V]) for b in two]
        factor = [sb(f"factor{b}", [F + 1, 4, V]) for b in two]
        decay = [sb(f"decay{b}", [F + 1, 4, V]) for b in two]
        run = [sb(f"run{b}", [F + 1, 4, V]) for b in two]
        rows = [sb(f"rows{b}", [P, parts, W]) for b in two]
        ps_rows = c.enter_context(nc.psum_tensor("aj_ps_rows", [P, parts, 256], F32))
        loaded, out = [sem(f"loaded{b}") for b in two], [sem(f"out{b}") for b in two]
        steps, scanned, turned, copied, seen = (sem(n) for n in ("steps", "scanned", "turned", "copied", "seen"))
        with nc.Block() as block:
            @block.sync
            def _(sp):
                def load(n, b):
                    sp.dma_start(raw[b][:].rearrange("f h v -> f (h v)"),
                                 g.att_raw[:, bass.ds(n * (4 * V), 4 * V)]).then_inc(loaded[b], 16)
                    for src, to in ((g.factor, factor), (g.decay, decay)):
                        sp.dma_start(to[b][:], src[:, bass.ds(n * V, V)].unsqueeze(0).to_broadcast([F + 1, 4, V])).then_inc(loaded[b], 16)

                for b in two:
                    load(b, b)
                with sp.Fori(1, o.pairs) as i:
                    for b in two:
                        sp.wait_ge(scanned, i * 2 + (b - 1))
                        load(i * 2 + b, b)

            @block.vector
            def _(dve):
                ch = Chain(dve, steps)
                ch.step(nc.vector.memset(run[1][:], 0.0))
                with dve.Fori(0, o.pairs) as i:
                    ch.restart()
                    for b in two:
                        n = i * 2 + b
                        dve.wait_ge(loaded[b], i * 48 + 48)
                        ch.step(nc.vector.tensor_mul(raw[b][:], raw[b][:], factor[b][:]))
                        dve.wait_ge(turned, i * 2 + 1)
                        for h in range(4):
                            ins = nc.vector.tensor_tensor_scan(run[b][:, h, :], decay[b][:, h, :], raw[b][:, h, :],
                                                               run[1 - b][:, h, V - 1:V], ALU.mult, ALU.add)
                            ch.step(ins)
                        dve.sem_inc(scanned, 1)

            @block.tensor
            def _(pe):
                pe.sem_inc(turned, 1)
                with pe.Fori(0, o.pairs) as i:
                    for b in two:
                        n = i * 2 + b
                        pe.wait_ge(scanned, n + 1)
                        pe.wait_ge(copied, n + 1)
                        pe.sem_inc(seen, 1)
                        for q in range(parts):
                            for h in range(4):
                                last = nc.tensor.transpose(ps_rows[:, q, h * (F + 1):(h + 1) * (F + 1)],
                                                           run[b][:, h, q * P:(q + 1) * P], g.ident[0:F + 1, 0:F + 1])
                        last.then_inc(turned, 1)

            @block.scalar
            def _(act):
                act.sem_inc(copied, 1)
                for b in two:
                    act.sem_inc(out[b], 16)
                with act.Fori(0, o.pairs) as i:
                    for b in two:
                        n = i * 2 + b
                        act.wait_ge(turned, n + 2)
                        act.wait_ge(out[b], i * 16 + 16)
                        nc.scalar.copy(rows[b][:], ps_rows[:, :, 0:W]).then_inc(copied, 1)
                        act.wait_ge(copied, n + 2)
                        act.dma_start(g.att_sums[bass.ds(n * V, V), :].rearrange("(q p) w -> p q w", p=P), rows[b][:]).then_inc(out[b], 16)
                for b in two:
                    act.wait_ge(out[b], 16 * o.pairs + 16)


def stage_attention_mean(nc, g, got, normed):
    with ExitStack() as c:
        weight = c.enter_context(nc.sbuf_tensor("am_weight", [P, NB, 4], F32))
        steps = new_sem(nc, c, "am_steps")
        with nc.Block() as block:
            @block.vector
            def _(dve):
                ch = Chain(dve, steps)
                v = got[:].rearrange("p b (h f) -> p b h f", f=F + 1)
                ch.step(nc.vector.tensor_scalar(weight[:], v[:, :, :, F], 1e-30, None, ALU.max))
                ch.step(nc.vector.reciprocal(weight[:], weight[:]))
                ch.step(nc.vector.tensor_mul(normed[:].rearrange("p b (h f) -> p b h f", f=F), v[:, :, :, 0:F],
                                             weight[:].unsqueeze(3).to_broadcast([P, NB, 4, F])))



def stage_aggregate(nc, g, name, table, sums, mix=None):
    o = g.D
    W = F * 3 if mix else F
    V = o.vb
    parts = V // P
    with ExitStack() as c:
        sb = lambda nm, shape, dt=F32: c.enter_context(nc.sbuf_tensor(f"{name}_{nm}", shape, dt))
        ps = lambda nm, shape: c.enter_context(nc.psum_tensor(f"{name}_{nm}", shape, F32))
        sem = lambda nm: new_sem(nc, c, f"{name}_{nm}")
        two = range(2)
        rec = [sb(f"rec{b}", [P, TB, o.words], I32) for b in two]
        keep = [sb(f"keep{b}", [W, V]) for b in two]
        got = [sb(f"got{b}", [P, TB, F]) for b in two]
        run = [sb(f"run{b}", [W, V]) for b in two]
        rows = [sb(f"rows{b}", [P, parts, W]) for b in two]
        if mix:
            mu, scale = sb("mu", [P, 3, 2]), sb("scale", [P, 3, 2])
            diff, dist, gauss = sb("diff", [P, TB, 3, 2]), sb("dist", [P, TB, 3]), sb("gauss", [P, TB, 3])
            mixed = [sb(f"mixed{b}", [P, TB, 3, F]) for b in two]
        ps_sum = [ps(f"ps_sum{b}", [W, V]) for b in two]
        ps_rows = [ps(f"ps_rows{b}", [P, parts, W]) for b in two]
        loaded, out = ([sem(f"{n}{b}") for b in two] for n in ("loaded", "out"))
        gathered = [rows_sem(nc, f"{name}_gathered{b}") for b in two]
        const, steps, taken, seen = sem("const"), sem("steps"), sem("taken"), sem("seen")
        dists, gausses, mixes, summed, scanned, turned, copied = (
            sem(n) for n in ("dists", "gausses", "mixes", "summed", "scanned", "turned", "copied"))
        rec_v = o.rec.rearrange("(p t) w -> p t w", p=P)
        keep_v = o.keep.rearrange("(a v) -> a v", a=1)
        with nc.Block() as block:
            @block.sync
            def _(sp):
                if mix:
                    for to, view in ((mu, mix[0]), (scale, mix[1])):
                        sp.dma_start(to[:].rearrange("p k d -> p (k d)"),
                                     view.rearrange("k d -> (k d)").unsqueeze(0).to_broadcast([P, 6])).then_inc(const, 16)

                def load(n, b):
                    sp.dma_start(rec[b][:], rec_v[:, bass.ds(n * TB, TB), :]).then_inc(loaded[b], 16)
                    sp.dma_start(keep[b][:], keep_v[:, bass.ds(n * V, V)].to_broadcast([W, V])).then_inc(loaded[b], 16)

                for b in two:
                    load(b, b)
                with sp.Fori(1, o.pairs) as i:
                    for b in two:
                        sp.wait_ge(scanned, i * 2 + b)
                        load(i * 2 + b, b)

            @block.gpsimd
            def _(pool):
                with pool.Fori(0, o.pairs) as i:
                    for b in two:
                        pool.wait_ge(loaded[b], i * 32 + 32)
                        pool.sem_inc(taken, 1)
                        for t in range(TB):
                            pool.indirect_dma_start(out=got[b][:, t, :], out_offset=None, in_=table[:, :],
                                                    in_offset=bass.IndirectOffsetOnAxis(ap=rec[b][:, t, 0:1], axis=0)).then_inc(gathered[b], 16)

            @block.tensor
            def _(pe):
                pe.sem_inc(turned, 1)
                with pe.Fori(0, o.pairs) as i:
                    for b in two:
                        n = i * 2 + b
                        if mix:
                            pe.wait_ge(mixes, n + 2)
                        else:
                            pe.wait_ge(gathered[b], i * (16 * TB) + 16 * TB)
                        pe.wait_ge(scanned, i * 2 + 1)
                        for t in range(TB):
                            lhs = mixed[b][:, t, :, :].rearrange("p k f -> p (k f)") if mix else got[b][:, t, :]
                            last = nc.tensor.matmul(ps_sum[b][:, t * o.per_tile:(t + 1) * o.per_tile], lhs, o.mask[:], start=True, stop=True)
                        last.then_inc(summed, 1)
                        pe.wait_ge(scanned, n + 2)
                        pe.wait_ge(copied, i * 2 + 1)
                        pe.sem_inc(seen, 1)
                        for q in range(parts):
                            last = nc.tensor.transpose(ps_rows[b][:, q, :], run[b][:, q * P:(q + 1) * P], g.ident[0:W, 0:W])
                        last.then_inc(turned, 1)

            @block.vector
            def _(dve):
                dve.sem_inc(scanned, 1)
                if mix:
                    dve.sem_inc(mixes, 1)
                ch = Chain(dve, steps)
                ch.step(nc.vector.memset(run[1][:], 0.0))
                if mix:
                    dve.wait_ge(const, 32)
                    ch.step(nc.vector.tensor_mul(scale[:], scale[:], scale[:]))
                    ch.step(nc.vector.tensor_scalar(scale[:], scale[:], 1e-15, None, ALU.add))
                    ch.step(nc.vector.reciprocal(scale[:], scale[:]))
                with dve.Fori(0, o.pairs) as i:
                    ch.restart()
                    for b in two:
                        n = i * 2 + b
                        if mix:
                            dve.wait_ge(loaded[b], i * 32 + 32)
                            attr = rec[b][:, :, 1:3].bitcast(F32)
                            b4 = [P, TB, 3, 2]
                            ch.step(nc.vector.tensor_sub(diff[:], attr.unsqueeze(2).to_broadcast(b4), mu[:].unsqueeze(1).to_broadcast(b4)))
                            ch.step(nc.vector.tensor_mul(diff[:], diff[:], diff[:]))
                            ch.step(nc.vector.tensor_mul(diff[:], diff[:], scale[:].unsqueeze(1).to_broadcast(b4)))
                            dve.wait_ge(gausses, n + 1)
                            nc.vector.tensor_reduce(dist[:], diff[:], AX.X, ALU.add).then_inc(dists, 1)
                            dve.wait_ge(gausses, n + 2)
                            dve.wait_ge(gathered[b], i * (16 * TB) + 16 * TB)
                            nc.vector.tensor_mul(mixed[b][:], got[b][:].unsqueeze(2).to_broadcast([P, TB, 3, F]),
                                                 gauss[:].unsqueeze(3).to_broadcast([P, TB, 3, F])).then_inc(mixes, 1)
                        dve.wait_ge(summed, n + 1)
                        dve.wait_ge(loaded[b], i * 32 + 32)
                        dve.wait_ge(turned, i * 2 + 1)
                        nc.vector.tensor_tensor_scan(run[b][:], keep[b][:], ps_sum[b][:], run[1 - b][:, V - 1:V],
                                                     ALU.mult, ALU.add).then_inc(scanned, 1)
                        dve.wait_ge(scanned, n + 2)

            @block.scalar
            def _(act):
                act.sem_inc(copied, 1)
                if mix:
                    act.sem_inc(gausses, 1)
                for b in two:
                    act.sem_inc(out[b], 16)
                with act.Fori(0, o.pairs) as i:
                    for b in two:
                        n = i * 2 + b
                        if mix:
                            act.wait_ge(dists, n + 1)
                            act.wait_ge(mixes, n + 1)
                            nc.scalar.activation(gauss[:], dist[:], ACT.Exp, scale=-0.5).then_inc(gausses, 1)
                        act.wait_ge(turned, n + 2)
                        act.wait_ge(out[b], i * 16 + 16)
                        nc.scalar.copy(rows[b][:], ps_rows[b][:]).then_inc(copied, 1)
                        act.wait_ge(copied, n + 2)
                        act.dma_start(sums[bass.ds(n * V, V), :].rearrange("(q p) w -> p q w", p=P), rows[b][:]).then_inc(out[b], 16)
                for b in two:
                    act.wait_ge(out[b], 16 * o.pairs + 16)



def stage_spline(nc, g, name, weights, fin, fout, sums, table=None, width=0, near=None):
    o = g.R
    C8, V, K = o.per_tile, o.vb, 125
    parts = V // P
    XT = 4 if fin > 1 else TB
    XS = TB // XT
    HT = TB // 2
    with ExitStack() as c:
        sb = lambda nm, shape, dt=F32: c.enter_context(nc.sbuf_tensor(f"{name}_{nm}", shape, dt))
        ps = lambda nm, shape: c.enter_context(nc.psum_tensor(f"{name}_{nm}", shape, F32))
        sem = lambda nm: new_sem(nc, c, f"{name}_{nm}")
        two = range(2)
        w_sb = sb("w", [K, fin, fout])
        rec = [sb(f"rec{b}", [P, TB, o.words], I32) for b in two]
        keep = [sb(f"keep{b}", [fout, V]) for b in two]
        far = [sb(f"far{b}", [P, TB, max(width, 1)]) for b in two]
        shift = [sb(f"shift{b}", [C8, TB, 3]) for b in two]
        pos = sb("pos", [P, TB, 3])
        up, down = sb("up", [P, TB * 3, 5]), sb("down", [P, TB * 3, 5])
        pair = sb("pair", [P, TB, 25])
        basis = [sb(f"basis{k}", [P, HT, K]) for k in two]
        lows, highs, floor, roof = (sb(n, [P, 5]) for n in ("lows", "highs", "floor", "roof"))
        spread = [sb(f"spread{k}", [P, XT, fin, C8]) for k in two]
        outer = sb("outer", [K, fin, V])
        run = [sb(f"run{b}", [fout, V]) for b in two]
        rows = [sb(f"rows{b}", [P, parts, fout]) for b in two]
        ps_outer = [ps(f"ps_outer{k}", [K, fin, C8]) for k in range(4)]
        ps_out = ps("ps_out", [fout, V])
        ps_rows = ps("ps_rows", [P, parts, fout])
        ps_shift = ps("ps_shift", [P, TB, 3])
        loaded, out = ([sem(f"{n}{b}") for b in two] for n in ("loaded", "out"))
        gathered = [rows_sem(nc, f"{name}_gathered{b}") for b in two]
        const, steps, taken, seen = sem("const"), sem("steps"), sem("taken"), sem("seen")
        shifts, positions, bases, spreads, products, outers, made, scanned, turned, copied = (
            sem(n) for n in ("shifts", "positions", "bases", "spreads", "products", "outers", "made", "scanned", "turned", "copied"))
        loads = 32 + (16 if near is not None else 0)
        rec_v = o.rec.rearrange("(p t) w -> p t w", p=P)
        keep_v = o.keep.rearrange("(a v) -> a v", a=1)
        with nc.Block() as block:
            @block.sync
            def _(sp):
                sp.dma_start(w_sb[:], weights).then_inc(const, 16)

                def load(n, b):
                    sp.dma_start(rec[b][:], rec_v[:, bass.ds(n * TB, TB), :]).then_inc(loaded[b], 16)
                    sp.dma_start(keep[b][:], keep_v[:, bass.ds(n * V, V)].to_broadcast([fout, V])).then_inc(loaded[b], 16)
                    if near is not None:
                        sp.dma_start(shift[b][:], near[bass.ds(n * V, V), :].rearrange("(t c) d -> c t d", c=C8)).then_inc(loaded[b], 16)

                for b in two:
                    load(b, b)
                with sp.Fori(1, o.pairs) as i:
                    for b in two:
                        sp.wait_ge(scanned, i * 2 + b)
                        load(i * 2 + b, b)

            if table is not None:
                @block.gpsimd
                def _(pool):
                    with pool.Fori(0, o.pairs) as i:
                        for b in two:
                            pool.wait_ge(loaded[b], i * loads + loads)
                            pool.sem_inc(taken, 1)
                            for t in range(TB):
                                pool.indirect_dma_start(out=far[b][:, t, :], out_offset=None, in_=table[:, :],
                                                        in_offset=bass.IndirectOffsetOnAxis(ap=rec[b][:, t, 0:1], axis=0)).then_inc(gathered[b], 16)

            @block.vector
            def _(dve):
                dve.sem_inc(scanned, 1)
                dve.sem_inc(positions, 1)
                ch = Chain(dve, steps)
                ends = 3.0e38
                for k, (lo, hi) in enumerate(((ends, 0.0), (-ends, 0.0), (0.0, 0.0), (0.0, -ends), (0.0, ends))):
                    nc.vector.memset(lows[:, k:k + 1], float(k - 1))
                    nc.vector.memset(highs[:, k:k + 1], float(k + 1))
                    nc.vector.memset(floor[:, k:k + 1], lo)
                    nc.vector.memset(roof[:, k:k + 1], hi)
                ch.step(nc.vector.memset(run[1][:], 0.0))
                b5 = [P, TB * 3, 5]
                wide = lambda ap: ap.unsqueeze(1).to_broadcast(b5)
                with dve.Fori(0, o.pairs) as i:
                    ch.restart()
                    for b in two:
                        n = i * 2 + b
                        dve.wait_ge(loaded[b], i * loads + loads)
                        pseudo = rec[b][:, :, 1:4].bitcast(F32)
                        if near is not None:
                            dve.wait_ge(shifts, n + 1)
                            dve.wait_ge(gathered[b], i * (16 * TB) + 16 * TB)
                            ch.step(nc.vector.tensor_add(pos[:], pseudo, far[b][:, :, fin:fin + 3]))
                            nc.vector.tensor_sub(pos[:], pos[:], ps_shift[:]).then_inc(positions, 1)
                            dve.wait_ge(positions, n + 2)
                            ch.step(nc.vector.tensor_scalar(pos[:], pos[:], 0.0, 1.0, ALU.max, ALU.min))
                            ch.step(nc.vector.tensor_scalar(pos[:], pos[:], 4.0, None, ALU.mult))
                        else:
                            ch.step(nc.vector.tensor_scalar(pos[:], pseudo, 4.0, None, ALU.mult))
                        x = pos[:].rearrange("p t d -> p (t d)").unsqueeze(2).to_broadcast(b5)
                        ch.step(nc.vector.tensor_sub(up[:], x, wide(lows[:])))
                        ch.step(nc.vector.tensor_tensor(up[:], up[:], wide(floor[:]), ALU.max))
                        ch.step(nc.vector.tensor_sub(down[:], wide(highs[:]), x))
                        ch.step(nc.vector.tensor_tensor(down[:], down[:], wide(roof[:]), ALU.max))
                        ch.step(nc.vector.tensor_tensor(up[:], up[:], down[:], ALU.min))
                        v = up[:].rearrange("p (t d) k -> p t d k", d=3)
                        b55 = [P, TB, 5, 5]
                        ch.step(nc.vector.tensor_mul(pair[:].rearrange("p t (a b) -> p t a b", a=5),
                                                     v[:, :, 0, :].unsqueeze(3).to_broadcast(b55), v[:, :, 1, :].unsqueeze(2).to_broadcast(b55)))
                        dve.wait_ge(products, n * TB + 1)
                        for k in two:
                            ts = slice(k * HT, (k + 1) * HT)
                            b255 = [P, HT, 25, 5]
                            nc.vector.tensor_mul(basis[k][:].rearrange("p t (a b) -> p t a b", b=5),
                                                 pair[:, ts, :].unsqueeze(3).to_broadcast(b255),
                                                 v[:, ts, 2, :].unsqueeze(2).to_broadcast(b255)).then_inc(bases, 1)
                        if fin > 1 and near is None:
                            dve.wait_ge(gathered[b], i * (16 * TB) + 16 * TB)
                        elif fin == 1:
                            ch.step(nc.vector.tensor_scalar(far[b][:, :, 0], rec[b][:, :, 0], float(N), None, ALU.is_lt))
                        for s in range(XS):
                            if s >= 2:
                                dve.wait_ge(products, n * TB + (s - 1) * XT + 1)
                            bx = [P, XT, fin, C8]
                            nc.vector.tensor_mul(spread[s % 2][:], far[b][:, s * XT:(s + 1) * XT, 0:fin].unsqueeze(3).to_broadcast(bx),
                                                 o.mask[:].unsqueeze(1).unsqueeze(1).to_broadcast(bx)).then_inc(spreads, 1)
                        dve.wait_ge(made, n + 2)
                        dve.wait_ge(turned, i * 2 + 1)
                        nc.vector.tensor_tensor_scan(run[b][:], keep[b][:], ps_out[:], run[1 - b][:, V - 1:V],
                                                     ALU.mult, ALU.add).then_inc(scanned, 1)
                        dve.wait_ge(scanned, n + 2)

            @block.tensor
            def _(pe):
                pe.sem_inc(products, 1)
                pe.sem_inc(turned, 1)
                pe.sem_inc(made, 1)
                pe.wait_ge(const, 16)
                with pe.Fori(0, o.pairs) as i:
                    for b in two:
                        n = i * 2 + b
                        if near is not None:
                            pe.wait_ge(loaded[b], i * loads + loads)
                            pe.wait_ge(positions, n + 1)
                            nc.tensor.matmul(ps_shift[:].rearrange("p t d -> p (t d)"), o.mask_t[:],
                                             shift[b][:].rearrange("c t d -> c (t d)"), start=True, stop=True).then_inc(shifts, 1)
                        for t in range(TB):
                            if t % HT == 0:
                                pe.wait_ge(bases, i * 4 + (b * 2 + t // HT + 1))
                            if t % XT == 0:
                                pe.wait_ge(spreads, i * (2 * XS) + (b * XS + t // XT + 1))
                            if t >= 4:
                                pe.wait_ge(outers, n * TB + (t - 3))
                            nc.tensor.matmul(ps_outer[t % 4][:].rearrange("k f c -> k (f c)"), basis[t // HT][:, t % HT, :],
                                             spread[(t // XT) % 2][:, t % XT, :, :].rearrange("p f c -> p (f c)"),
                                             start=True, stop=True).then_inc(products, 1)
                        pe.wait_ge(outers, n * TB + TB)
                        pe.wait_ge(scanned, n + 1)
                        for f in range(fin):
                            last = nc.tensor.matmul(ps_out[:], w_sb[:, f, :], outer[:, f, :], start=(f == 0), stop=(f == fin - 1))
                        last.then_inc(made, 1)
                        pe.wait_ge(scanned, n + 2)
                        pe.wait_ge(copied, n + 1)
                        pe.sem_inc(seen, 1)
                        for q in range(parts):
                            last = nc.tensor.transpose(ps_rows[:, q, :], run[b][:, q * P:(q + 1) * P], g.ident[0:fout, 0:fout])
                        last.then_inc(turned, 1)

            @block.scalar
            def _(act):
                act.sem_inc(copied, 1)
                for b in two:
                    act.sem_inc(out[b], 16)
                with act.Fori(0, o.pairs) as i:
                    for b in two:
                        n = i * 2 + b
                        act.wait_ge(made, n + 1)
                        for t in range(TB):
                            act.wait_ge(products, n * TB + (t + 2))
                            nc.scalar.copy(outer[:, :, t * C8:(t + 1) * C8], ps_outer[t % 4][:]).then_inc(outers, 1)
                        act.wait_ge(turned, n + 2)
                        act.wait_ge(out[b], i * 16 + 16)
                        nc.scalar.copy(rows[b][:], ps_rows[:]).then_inc(copied, 1)
                        act.wait_ge(copied, n + 2)
                        act.dma_start(sums[bass.ds(n * V, V), :].rearrange("(q p) w -> p q w", p=P), rows[b][:]).then_inc(out[b], 16)
                for b in two:
                    act.wait_ge(out[b], 16 * o.pairs + 16)



def stage_nodes(nc, g, name, biases, work, stores=()):
    with ExitStack() as c:
        sb = lambda nm, shape: c.enter_context(nc.sbuf_tensor(f"{name}_{nm}", shape, F32))
        sem = lambda nm: new_sem(nc, c, f"{name}_{nm}")
        rows = [sb(f"bias{k}", [P, view.shape[0]]) for k, view in enumerate(biases)]
        t = NormBuffers(nc, c, name)
        loaded, steps, finished, stored, act_in, act_out = (
            sem(n) for n in ("loaded", "steps", "finished", "stored", "act_in", "act_out"))
        calls = []

        with nc.Block() as block:
            @block.sync
            def _(sp):
                for to, view in zip(rows, biases):
                    sp.dma_start(to[:], view.unsqueeze(0).to_broadcast([P, view.shape[0]])).then_inc(loaded, 16)
                sp.wait_ge(finished, 1)
                for table, tile in stores:
                    sp.dma_start(table, tile).then_inc(stored, 16)
                if stores:
                    sp.wait_ge(stored, 16 * len(stores))

            @block.vector
            def _(dve):
                ch = Chain(dve, steps)
                if biases:
                    dve.wait_ge(loaded, 16 * len(biases))

                def act_in_place(ap, func):
                    calls.append((ap, func))
                    dve.sem_inc(act_in, 1)
                    dve.wait_ge(act_out, len(calls))

                work(ch, rows, act_in_place, t)
                dve.sem_inc(finished, 1)

            @block.scalar
            def _(act):
                for k, (ap, func) in enumerate(calls):
                    act.wait_ge(act_in, k + 1)
                    nc.scalar.activation(ap, ap, func).then_inc(act_out, 1)


def layers(nc, g, ins, out):
    bc = lambda ap, width: ap.unsqueeze(1).to_broadcast([P, NB, width])
    per_node = lambda ap, width: ap.unsqueeze(2).to_broadcast([P, NB, width])

    def elu(ch, act, to, tmp):
        ch.step(nc.vector.tensor_scalar(tmp, to, 0.0, None, ALU.min))
        act(tmp, ACT.Exp)
        ch.step(nc.vector.tensor_scalar(tmp, tmp, -1.0, None, ALU.add))
        ch.step(nc.vector.scalar_tensor_tensor(to, to, 0.0, tmp, ALU.max, ALU.add))

    def scope():
        c = ExitStack()
        return c, (lambda name, shape: c.enter_context(nc.sbuf_tensor(name, shape, F32)))

    stage_chunks(nc, g)

    stage_attention_inputs(nc, g, ins)
    stage_nodes(nc, g, "n_in", [], lambda ch, rows, act, t: layernorm(ch, nc, g, t, g.h[:], act))
    stage_dense(nc, g, "d_att", g.h, F, g.att_w[:], 8, g.att, [])
    stage_attention_tables(nc, g, ins)
    stage_spread(nc, g, "s_near", g.near_table, 4, g.near_chunk)
    stage_attention(nc, g)
    stage_attention_factors(nc, g)
    stage_attention_join(nc, g)
    c, sb = scope()
    with c:
        got, normed, w, mean = sb("l0_got", [P, NB, 4 * (F + 1)]), sb("l0_normed", [P, NB, 4 * F]), sb("l0_w", [4 * F, F]), sb("l0_mean", [P, NB, F])
        stage_collect(nc, g, "c_att", g.R, g.att_sums, 4 * (F + 1), got)
        stage_attention_mean(nc, g, got, normed)
        stage_dense(nc, g, "d_l0", normed, 4 * F, w[:], F, mean, [(w[:], ins["L0_gnn_w"].rearrange("h f o -> (h f) o"))])

        def work(ch, rows, act, t):
            ch.step(nc.vector.scalar_tensor_tensor(g.x[:], mean[:], 0.25, g.x[:], ALU.mult, ALU.add))
            ch.step(nc.vector.tensor_add(g.x[:], g.x[:], bc(rows[0][:], F)))
            layernorm(ch, nc, g, t, g.h[:], act)

        stage_nodes(nc, g, "n_l0", [ins["L0_gnn_bias"]], work, [(node_rows(g.table_32), g.h[:])])

    stage_aggregate(nc, g, "g_l1", g.table_32, g.sums_d)
    c, sb = scope()
    with c:
        got, cat, hid, both = (sb("l1_got", [P, NB, F]), sb("l1_cat", [P, NB, 2 * F]), sb("l1_hid", [P, NB, 64]), sb("l1_both", [P, NB, 64]))
        w1, w2, y = sb("l1_w1", [64, 64]), sb("l1_w2", [64, 64]), sb("l1_y", [P, NB, F])
        stage_collect(nc, g, "c_l1", g.D, g.sums_d, F, got)

        def work(ch, rows, act, t):
            ch.step(nc.vector.tensor_mul(cat[:, :, 0:F], got[:], per_node(g.D.inv_degree[:], F)))
            ch.step(nc.vector.tensor_copy(cat[:, :, F:2 * F], g.h[:]))

        stage_nodes(nc, g, "n_l1a", [], work)
        stage_dense(nc, g, "d_l1a", cat, 64, w1[:], 64, hid, [(w1[0:F, :], ins["L1_gnn_W1_l"]), (w1[F:2 * F, :], ins["L1_gnn_W1_r"])])

        def work(ch, rows, act, t):
            ch.step(nc.vector.tensor_add(hid[:], hid[:], bc(rows[0][:], 64)))
            ch.step(nc.vector.tensor_scalar(hid[:], hid[:], 0.0, None, ALU.max))

        stage_nodes(nc, g, "n_l1b", [ins["L1_gnn_b1"]], work)
        stage_dense(nc, g, "d_l1b", hid, 64, w2[:], 64, both, [(w2[:, 0:F], ins["L1_gnn_W2_l"]), (w2[:, F:2 * F], ins["L1_gnn_W2_r"])])

        def work(ch, rows, act, t):
            ch.step(nc.vector.tensor_mul(y[:], both[:, :, 0:F], per_node(g.valid[:], F)))

        stage_nodes(nc, g, "n_l1c", [], work, [(node_rows(g.table_32), y[:])])
        stage_aggregate(nc, g, "g_l1d", g.table_32, g.sums_d)
        stage_collect(nc, g, "c_l1d", g.D, g.sums_d, F, got)

        def work(ch, rows, act, t):
            ch.step(nc.vector.tensor_mul(got[:], got[:], per_node(g.D.inv_degree[:], F)))
            ch.step(nc.vector.tensor_add(got[:], got[:], bc(rows[0][:], F)))
            ch.step(nc.vector.tensor_add(got[:], got[:], both[:, :, F:2 * F]))
            ch.step(nc.vector.tensor_add(g.x[:], g.x[:], got[:]))
            layernorm(ch, nc, g, t, g.h[:], act)

        stage_nodes(nc, g, "n_l1d", [ins["L1_gnn_b2"]], work, [(node_rows(g.table_32), g.h[:])])

    stage_aggregate(nc, g, "g_l2", g.table_32, g.sums_d3, mix=(ins["L2_gnn_mu"], ins["L2_gnn_sigma"]))
    c, sb = scope()
    with c:
        got, cat, w, res = sb("l2_got", [P, NB, 3 * F]), sb("l2_cat", [P, NB, 4 * F]), sb("l2_w", [4 * F, F]), sb("l2_res", [P, NB, F])
        stage_collect(nc, g, "c_l2", g.D, g.sums_d3, 3 * F, got)

        def work(ch, rows, act, t):
            ch.step(nc.vector.tensor_mul(cat[:, :, 0:3 * F], got[:], per_node(g.D.inv_degree[:], 3 * F)))
            ch.step(nc.vector.tensor_copy(cat[:, :, 3 * F:4 * F], g.h[:]))

        stage_nodes(nc, g, "n_l2a", [], work)
        parts = [(w[k * F:(k + 1) * F, :], ins["L2_gnn_g"][:, k * F:(k + 1) * F]) for k in range(3)]
        stage_dense(nc, g, "d_l2", cat, 4 * F, w[:], F, res, parts + [(w[3 * F:4 * F, :], ins["L2_gnn_root"])])

        def work(ch, rows, act, t):
            ch.step(nc.vector.tensor_add(res[:], res[:], bc(rows[0][:], F)))
            ch.step(nc.vector.tensor_add(g.x[:], g.x[:], res[:]))
            layernorm(ch, nc, g, t, g.h[:], act)

        stage_nodes(nc, g, "n_l2b", [ins["L2_gnn_bias"]], work)

    c, sb = scope()
    with c:
        hid = sb("l3_hid", [P, NB, 64])

        def spline_mean(ch, to, bias, width):
            ch.step(nc.vector.tensor_mul(to, to, per_node(g.R.inv_degree[:], width)))
            ch.step(nc.vector.tensor_add(to, to, bc(bias, width)))

        stage_spline(nc, g, "p_1", ins["L3_gnn_stn1_w"], 1, 64, g.sums_r64)
        stage_collect(nc, g, "c_p1", g.R, g.sums_r64, 64, hid)
        c2, sb2 = scope()
        with c2:
            tmp = sb2("l3_tmp1", [P, NB, 64])

            def work(ch, rows, act, t):
                spline_mean(ch, hid[:], rows[0][:], 64)
                elu(ch, act, hid[:], tmp[:])
                ch.step(nc.vector.tensor_mul(hid[:], hid[:], per_node(g.valid[:], 64)))

            stage_nodes(nc, g, "n_p1", [ins["L3_gnn_stn1_b"]], work, [(node_rows(g.table_64), hid[:])])
        stage_spline(nc, g, "p_2", ins["L3_gnn_stn2_w"], 64, 64, g.sums_r64, table=g.table_64, width=64)
        stage_collect(nc, g, "c_p2", g.R, g.sums_r64, 64, hid)
        c2, sb2 = scope()
        with c2:
            tmp, hid2, w3, w4 = sb2("l3_tmp2", [P, NB, 64]), sb2("l3_hid2", [P, NB, 64]), sb2("l3_w3", [64, 64]), sb2("l3_w4", [64, 3])
            t3, row = sb2("l3_t3", [P, NB, 3]), sb2("l3_row", [P, NB, F + 3])

            def work(ch, rows, act, t):
                spline_mean(ch, hid[:], rows[0][:], 64)
                elu(ch, act, hid[:], tmp[:])

            stage_nodes(nc, g, "n_p2", [ins["L3_gnn_stn2_b"]], work)
            stage_dense(nc, g, "d_p3", hid, 64, w3[:], 64, hid2, [(w3[:], ins["L3_gnn_stn3_w"])])

            def work(ch, rows, act, t):
                ch.step(nc.vector.tensor_add(hid2[:], hid2[:], bc(rows[0][:], 64)))
                elu(ch, act, hid2[:], tmp[:])

            stage_nodes(nc, g, "n_p3", [ins["L3_gnn_stn3_b"]], work)
            stage_dense(nc, g, "d_p4", hid2, 64, w4[:], 3, t3, [(w4[:], ins["L3_gnn_stn4_w"])])

            def work(ch, rows, act, t):
                ch.step(nc.vector.tensor_add(t3[:], t3[:], bc(rows[0][:], 3)))
                ch.step(nc.vector.tensor_copy(row[:, :, 0:F], g.h[:]))
                ch.step(nc.vector.tensor_copy(row[:, :, F:F + 3], t3[:]))

            stage_nodes(nc, g, "n_p4", [ins["L3_gnn_stn4_b"]], work, [(node_rows(g.table_35), row[:]), (node_rows(g.shift_table), t3[:])])
        stage_spread(nc, g, "s_shift", g.shift_table, 3, g.shift_chunk)
        stage_spline(nc, g, "p_3", ins["L3_gnn_conv_w"], F, F, g.sums_r32, table=g.table_35, width=F + 3, near=g.shift_chunk)
        c2, sb2 = scope()
        with c2:
            got = sb2("l3_got", [P, NB, F])
            stage_collect(nc, g, "c_p3", g.R, g.sums_r32, F, got)

            def work(ch, rows, act, t):
                spline_mean(ch, got[:], rows[0][:], F)
                ch.step(nc.vector.tensor_add(got[:], got[:], g.x[:]))

            full = (NB - 1) * P
            stage_nodes(nc, g, "n_p5", [ins["L3_gnn_conv_b"]], work,
                        [(out[0:full, :].rearrange("(b p) f -> p b f", p=P), got[:, 0:NB - 1, :]),
                         (out[full:N, :], got[0:N - full, NB - 1, :])])


def build(nc, ins, out):
    g = Shared()
    g.R = Order("r", 16, 4, 19)
    g.D = Order("d", 8, 3, 16)
    g.orders = (g.R, g.D)
    with ExitStack() as c:
        dram = lambda name, shape, dt=F32: nc.dram_tensor(name, shape, dt, kind="Internal").ap()
        sb = lambda name, shape, dt=F32: c.enter_context(nc.sbuf_tensor(name, shape, dt))
        g.pad = {"src": dram("pad_src", [EP], I32), "dst": dram("pad_dst", [EP], I32),
                 "edge_attr_3": dram("pad_attr_3", [EP * 3]), "edge_attr_2": dram("pad_attr_2", [EP * 2])}
        for o, key, other, attr in ((g.R, "src", "dst", "edge_attr_3"), (g.D, "dst", "src", "edge_attr_2")):
            o.key, o.other, o.attr = key, other, attr
            o.rec = dram(f"rec_{o.name}", [o.slots, o.words], I32)
            o.first = dram(f"first_{o.name}", [o.chunks, 1])
            o.mask = sb(f"mask_{o.name}", [P, o.per_tile])
            o.slot0 = sb(f"slot0_{o.name}", [P, NH])
            o.last = sb(f"last_{o.name}", [P, NB], I32)
            o.inv_degree = sb(f"inv_degree_{o.name}", [P, NB])
        V = g.R.chunks
        for o in g.orders:
            o.keep = dram(f"keep_{o.name}", [o.chunks])
        g.chunk_node, g.chunk_row = dram("chunk_node", [V], I32), sb("chunk_row", [P, V // P], I32)
        g.att_table, g.near_table, g.near_chunk = dram("att_table", [NP, F + 5]), dram("near_table", [NP, 4]), dram("near_chunk", [V, 4])
        g.top, g.factor, g.decay = dram("top", [4, V]), dram("factor", [4, V]), dram("decay", [4, V])
        g.att_raw, g.att_sums = dram("att_raw", [F + 1, 4 * V]), dram("att_sums", [V, 4 * (F + 1)])
        g.table_32, g.table_64, g.table_35 = dram("table_32", [NP, F]), dram("table_64", [NP, 64]), dram("table_35", [NP, F + 3])
        g.sums_d, g.sums_d3 = dram("sums_d", [g.D.chunks, F]), dram("sums_d3", [g.D.chunks, 3 * F])
        g.sums_r64, g.sums_r32 = dram("sums_r64", [V, 64]), dram("sums_r32", [V, F])
        g.shift_table, g.shift_chunk = dram("shift_table", [NP, 3]), dram("shift_chunk", [V, 3])
        g.R.mask_t = sb("mask_t", [g.R.per_tile, P])
        g.iota_row, g.pidx = sb("iota_row", [P, P]), sb("pidx", [P, 1])
        g.ident, g.below, g.before = sb("ident", [P, P]), sb("below", [P, P]), sb("before", [P, P])
        g.ones, g.zero_bf = sb("ones", [P, P]), sb("zero_bf", [P, P], BF16)
        g.valid = sb("valid", [P, NB])
        g.degree = {k: sb(f"degree_{k}", [P, NH]) for k in ("src", "dst")}
        stage_setup(nc, g, ins)
        with ExitStack() as cs:
            sbs = lambda name, shape, dt=F32: cs.enter_context(nc.sbuf_tensor(name, shape, dt))
            cols = STEPS * HB
            g.key_i = {k: sbs(f"key_i_{k}", [P, cols], I32) for k in ("src", "dst")}
            g.key_f = {k: sbs(f"key_f_{k}", [P, cols]) for k in ("src", "dst")}
            g.lo = {k: sbs(f"lo_{k}", [P, cols]) for k in ("src", "dst")}
            g.hi = {k: sbs(f"hi_{k}", [P, cols]) for k in ("src", "dst")}
            g.attr = {"edge_attr_3": sbs("attr_3", [P, cols * 3]), "edge_attr_2": sbs("attr_2", [P, cols * 2])}
            stage_histogram(nc, g)
            stage_starts(nc, g)
            for o in g.orders:
                stage_sort(nc, g, o)
        g.x, g.h = sb("x_nodes", [P, NB, F]), sb("h_nodes", [P, NB, F])
        g.att_w, g.att = sb("att_w", [F, 8]), sb("att", [P, NB, 8])
        layers(nc, g, ins, out)


_INS = ["x", "src", "dst", "edge_attr_2", "edge_attr_3", "L0_gnn_w", "L0_gnn_fc_w", "L0_gnn_fc_b", "L0_gnn_bias",
        "L1_gnn_W1_l", "L1_gnn_b1", "L1_gnn_W1_r", "L1_gnn_W2_l", "L1_gnn_b2", "L1_gnn_W2_r",
        "L2_gnn_g", "L2_gnn_mu", "L2_gnn_sigma", "L2_gnn_root", "L2_gnn_bias",
        "L3_gnn_stn1_w", "L3_gnn_stn1_b", "L3_gnn_stn2_w", "L3_gnn_stn2_b", "L3_gnn_stn3_w", "L3_gnn_stn3_b",
        "L3_gnn_stn4_w", "L3_gnn_stn4_b", "L3_gnn_conv_w", "L3_gnn_conv_b"]


def kernel(**inputs):
    import numpy as _np
    import concourse.bacc as _bacc
    from concourse import mybir as _mybir
    from concourse.bass_utils import run_bass_kernel_spmd as _run

    nc = _bacc.Bacc("TRN2", target_bir_lowering=False, num_devices=1)
    arrays, args = {}, {}
    for name in _INS:
        a = _np.ascontiguousarray(inputs[name])
        arrays[f"in_{name}_dram"] = a
        args[name] = nc.dram_tensor(f"in_{name}_dram", a.shape, _mybir.dt.from_np(a.dtype), kind="ExternalInput").ap()
    out = nc.dram_tensor("out_dram", (N, F), F32, kind="ExternalOutput").ap()
    build(nc, args, out)
    r = _run(nc, [arrays], core_ids=[0])
    return r.results[0]["out_dram"]
```

```python
from contextlib import ExitStack

import concourse.bass as bass
from concourse import mybir

F32 = mybir.dt.float32
I32 = mybir.dt.int32
BF16 = mybir.dt.bfloat16
ALU = mybir.AluOpType
ACT = mybir.ActivationFunctionType
AX = mybir.AxisListType

P = 128
N = 3125
E = 103125
NB = -(-N // P)
NP = NB * P
NH = NB + 1
HB = 13
STEPS = E // (HB * P) + 1
EP = STEPS * HB * P
PAD_KEY = NB * P
PAD_START = 5.0e7
BIG = 1.0e30
TB = 32
QUARTERS = 4
F = 32
FAR = F + 5 + 64
EPS_LN = 1e-5


class Order:

    def __init__(self, name, chunk, words, pairs):
        self.name, self.chunk, self.words, self.pairs = name, chunk, words, pairs
        self.blocks = 2 * pairs
        self.shift = chunk.bit_length() - 1
        self.per_tile = P // chunk
        self.tiles = self.blocks * TB
        self.chunks = self.tiles * self.per_tile
        self.vb = TB * self.per_tile
        self.slots = self.tiles * P
        assert self.chunks >= N + E // chunk


class Shared:
    pass


class Chain:

    def __init__(self, eng, sem):
        self.eng, self.sem, self.n = eng, sem, 0

    def step(self, ins):
        ins.then_inc(self.sem, 1)
        self.n += 1
        self.eng.wait_ge(self.sem, self.n)

    def restart(self):
        self.eng.sem_clear(self.sem)
        self.n = 0


def new_sem(nc, c, name):
    handle = nc.alloc_semaphore(name)
    c.callback(nc.release_semaphore, handle)
    c.callback(nc.gpsimd.sem_clear, handle)
    return handle


def rows_sem(nc, name):
    return nc.alloc_semaphore(name)


def stage_setup(nc, g, ins):
    R, D = g.R, g.D
    with ExitStack() as c:
        sb = lambda name, shape, dt: c.enter_context(nc.sbuf_tensor(name, shape, dt))
        sem = lambda name: new_sem(nc, c, name)
        iota_i = sb("su_iota_i", [P, P], I32)
        pidx_i = sb("su_pidx_i", [P, 1], I32)
        node_i = sb("su_node_i", [P, NH], I32)
        node_f = sb("su_node_f", [P, NH], F32)
        pg_i = sb("su_pg_i", [P, 2], I32)
        pg_f = sb("su_pg_f", [P, 2], F32)
        cg_i = sb("su_cg_i", [P, P], I32)
        cg_f = sb("su_cg_f", [P, P], F32)
        fill_r = sb("su_fill_r", [P, R.tiles * R.words], I32)
        fill_d = sb("su_fill_d", [P, D.tiles * D.words], I32)
        zeros = sb("su_zeros", [P, 256], F32)
        pad_key = sb("su_pad_key", [1, EP - E], I32)
        iotas = sem("su_iotas")
        fills = sem("su_fills")
        copied = sem("su_copied")
        steps = sem("su_steps")
        with nc.Block() as block:
            @block.gpsimd
            def _(pool):
                nc.gpsimd.iota(iota_i[:], [[1, P]], base=0, channel_multiplier=0).then_inc(iotas, 1)
                nc.gpsimd.iota(pidx_i[:], [[0, 1]], base=0, channel_multiplier=1).then_inc(iotas, 1)
                nc.gpsimd.iota(node_i[:], [[P, NH]], base=0, channel_multiplier=1).then_inc(iotas, 1)
                nc.gpsimd.memset(zeros[:], 0.0).then_inc(fills, 1)
                nc.gpsimd.memset(pad_key[:], PAD_KEY).then_inc(fills, 1)

            @block.vector
            def _(dve):
                ch = Chain(dve, steps)
                for o, fill in ((R, fill_r), (D, fill_d)):
                    ch.step(nc.vector.memset(fill[:], 0))
                    nc.vector.memset(fill[:].rearrange("p (t w) -> p t w", w=o.words)[:, :, 0], N).then_inc(fills, 1)
                nc.vector.memset(g.ones[:], 1.0)
                nc.vector.memset(g.zero_bf[:], 0.0)
                dve.wait_ge(iotas, 3)
                nc.vector.tensor_copy(g.iota_row[:], iota_i[:])
                ch.step(nc.vector.tensor_copy(g.pidx[:], pidx_i[:]))
                ch.step(nc.vector.tensor_copy(node_f[:], node_i[:]))
                nc.vector.tensor_scalar(g.valid[:], node_f[:, 0:NB], float(N), None, ALU.is_lt)
                for k, o in enumerate((R, D)):
                    nc.vector.tensor_scalar(pg_i[:, k:k + 1], pidx_i[:], o.shift, None, ALU.logical_shift_right)
                ch.step(nc.vector.tensor_scalar(cg_i[:], iota_i[:], R.shift, None, ALU.logical_shift_right))
                nc.vector.tensor_copy(pg_f[:], pg_i[:])
                ch.step(nc.vector.tensor_copy(cg_f[:], cg_i[:]))
                nc.vector.tensor_scalar(g.ident[:], g.iota_row[:], g.pidx[:], None, ALU.is_equal)
                nc.vector.tensor_scalar(g.below[:], g.iota_row[:], g.pidx[:], None, ALU.is_gt)
                nc.vector.tensor_scalar(g.before[:], g.iota_row[:], g.pidx[:], None, ALU.is_lt)
                nc.vector.tensor_scalar(R.mask[:], g.iota_row[:, 0:R.per_tile], pg_f[:, 0:1], None, ALU.is_equal)
                nc.vector.tensor_scalar(D.mask[:], g.iota_row[:, 0:D.per_tile], pg_f[:, 1:2], None, ALU.is_equal)
                nc.vector.tensor_scalar(R.mask_t[:], cg_f[0:R.per_tile, :], g.pidx[0:R.per_tile, :], None, ALU.is_equal)

            @block.sync
            def _(sp):
                for name, width in (("src", 1), ("dst", 1), ("edge_attr_3", 3), ("edge_attr_2", 2)):
                    flat = ins[name] if width == 1 else ins[name].rearrange("e w -> (e w)")
                    sp.dma_start(g.pad[name][0:E * width].rearrange("(p f) -> p f", p=125),
                                 flat.rearrange("(p f) -> p f", p=125)).then_inc(copied, 16)
                sp.wait_ge(fills, 4)
                for name in ("src", "dst"):
                    sp.dma_start(g.pad[name][E:EP].rearrange("(p f) -> p f", p=1), pad_key[:]).then_inc(copied, 16)
                for name, width in (("edge_attr_3", 3), ("edge_attr_2", 2)):
                    sp.dma_start(g.pad[name][E * width:EP * width].rearrange("(p f) -> p f", p=1),
                                 zeros[0:1, 0:(EP - E) * width]).then_inc(copied, 16)
                for o, fill in ((R, fill_r), (D, fill_d)):
                    sp.dma_start(o.rec.rearrange("(p t) w -> p (t w)", p=P), fill[:]).then_inc(copied, 16)
                    sp.dma_start(o.first.rearrange("(p f) w -> p (f w)", p=P), zeros[:, 0:o.chunks // P]).then_inc(copied, 16)
                sp.wait_ge(copied, 12 * 16)


def stage_histogram(nc, g):
    keys = ("src", "dst")
    with ExitStack() as c:
        sb = lambda name, shape, dt: c.enter_context(nc.sbuf_tensor(name, shape, dt))
        sem = lambda name: new_sem(nc, c, name)
        lo_i = sb("hi_lo_i", [P, STEPS * HB], I32)
        hi_i = sb("hi_hi_i", [P, STEPS * HB], I32)
        lo1 = [sb(f"hi_lo1_{i}", [P, HB, P], BF16) for i in range(4)]
        hi1 = [sb(f"hi_hi1_{i}", [P, HB, NH], BF16) for i in range(4)]
        count = [c.enter_context(nc.psum_tensor(f"hi_count_{k}", [P, NH], F32)) for k in keys]
        loaded, steps = sem("hi_loaded"), sem("hi_steps")
        onehots, counted = sem("hi_onehots"), sem("hi_counted")
        with nc.Block() as block:
            @block.sync
            def _(sp):
                for k in keys:
                    sp.dma_start(g.key_i[k][:].rearrange("p (s j) -> p s j", j=HB),
                                 g.pad[k].rearrange("(s p j) -> p s j", p=P, j=HB)).then_inc(loaded, 16)
                for name, width in (("edge_attr_3", 3), ("edge_attr_2", 2)):
                    sp.dma_start(g.attr[name][:].rearrange("p (s j) -> p s j", j=HB * width),
                                 g.pad[name].rearrange("(s p j) -> p s j", p=P, j=HB * width)).then_inc(loaded, 16)
                sp.wait_ge(loaded, 64)

            @block.vector
            def _(dve):
                ch = Chain(dve, steps)
                dve.wait_ge(loaded, 64)
                for k in keys:
                    ch.step(nc.vector.tensor_copy(g.key_f[k][:], g.key_i[k][:]))
                    ch.step(nc.vector.tensor_scalar(lo_i[:], g.key_i[k][:], P - 1, None, ALU.bitwise_and))
                    ch.step(nc.vector.tensor_scalar(hi_i[:], g.key_i[k][:], 7, None, ALU.logical_shift_right))
                    ch.step(nc.vector.tensor_copy(g.lo[k][:], lo_i[:]))
                    ch.step(nc.vector.tensor_copy(g.hi[k][:], hi_i[:]))

                def half(step, slot, k):
                    cols = bass.ds(step * HB, HB)
                    nc.vector.tensor_tensor(lo1[slot][:], g.iota_row[:].unsqueeze(1).to_broadcast([P, HB, P]),
                                            g.lo[k][:, cols].unsqueeze(2).to_broadcast([P, HB, P]), ALU.is_equal)
                    nc.vector.tensor_tensor(hi1[slot][:], g.iota_row[:, 0:NH].unsqueeze(1).to_broadcast([P, HB, NH]),
                                            g.hi[k][:, cols].unsqueeze(2).to_broadcast([P, HB, NH]),
                                            ALU.is_equal).then_inc(onehots, 1)

                for slot in range(4):
                    half(slot // 2, slot, keys[slot % 2])
                with dve.Fori(1, STEPS // 2) as i:
                    for slot in range(4):
                        dve.wait_ge(counted, i * 4 + (slot - 3))
                        half(i * 2 + slot // 2, slot, keys[slot % 2])
                dve.wait_ge(counted, STEPS * 2 + 2)
                for k, cnt in zip(keys, count):
                    nc.vector.tensor_copy(g.degree[k][:], cnt[:])

            @block.tensor
            def _(pe):
                for cnt in count:
                    nc.tensor.matmul(cnt[:], g.zero_bf[:], g.zero_bf[:, 0:NH], start=True, stop=False)
                with pe.Fori(0, STEPS // 2) as i:
                    for slot in range(4):
                        pe.wait_ge(onehots, i * 4 + (slot + 1))
                        for j in range(HB):
                            last = nc.tensor.matmul(count[slot % 2][:], lo1[slot][:, j, :], hi1[slot][:, j, :],
                                                    start=False, stop=False)
                        last.then_inc(counted, 1)
                for cnt in count:
                    nc.tensor.matmul(cnt[:], g.zero_bf[:], g.zero_bf[:, 0:NH],
                                     start=False, stop=True).then_inc(counted, 1)


def stage_starts(nc, g):
    with ExitStack() as c:
        sb = lambda name, shape, dt: c.enter_context(nc.sbuf_tensor(name, shape, dt))
        sem = lambda name: new_sem(nc, c, name)
        tmp_i = sb("st_tmp_i", [P, NB], I32)
        need = sb("st_need", [P, NB], F32)
        total = sb("st_total", [P, NB], F32)
        upto = sb("st_upto", [P, NB], F32)
        start = sb("st_start", [P, NB], F32)
        marked = sb("st_marked", [P, NB], F32)
        place = sb("st_place", [P, NB], F32)
        mark = [sb(f"st_mark_{o.name}", [P, NB], I32) for o in g.orders]
        ps_in = c.enter_context(nc.psum_tensor("st_ps_in", [P, NB], F32))
        ps_tot = c.enter_context(nc.psum_tensor("st_ps_tot", [P, NB], F32))
        steps, needed, summed = sem("st_steps"), sem("st_needed"), sem("st_summed")
        ready, scattered = sem("st_ready"), rows_sem(nc, "st_scattered")
        with nc.Block() as block:
            @block.vector
            def _(dve):
                ch = Chain(dve, steps)
                for n, o in enumerate(g.orders):
                    deg = g.degree[o.key][:, 0:NB]
                    ch.step(nc.vector.tensor_scalar(o.inv_degree[:], deg, 1.0, None, ALU.max))
                    ch.step(nc.vector.reciprocal(o.inv_degree[:], o.inv_degree[:]))
                    ch.step(nc.vector.tensor_scalar(tmp_i[:], deg, float(o.chunk - 1), None, ALU.add))
                    ch.step(nc.vector.tensor_scalar(tmp_i[:], tmp_i[:], o.shift, None, ALU.logical_shift_right))
                    ch.step(nc.vector.tensor_copy(need[:], tmp_i[:]))
                    ch.step(nc.vector.scalar_tensor_tensor(need[:], need[:], 1.0, g.valid[:], ALU.max, ALU.mult))
                    dve.sem_inc(needed, 1)
                    dve.wait_ge(summed, n + 1)
                    ch.step(nc.vector.tensor_copy(total[:], ps_tot[:]))
                    ch.step(nc.vector.tensor_tensor_scan(upto[:], g.ones[:, 0:NB], total[:], 0.0, ALU.mult, ALU.add))
                    ch.step(nc.vector.tensor_sub(upto[:], upto[:], total[:]))
                    ch.step(nc.vector.tensor_add(start[:], ps_in[:], upto[:]))
                    nc.vector.memset(o.slot0[:, NB:NH], PAD_START)
                    ch.step(nc.vector.tensor_scalar(o.slot0[:, 0:NB], start[:], float(o.chunk), None, ALU.mult))
                    ch.step(nc.vector.tensor_add(marked[:], start[:], need[:]))
                    ch.step(nc.vector.tensor_scalar(marked[:], marked[:], -1.0, None, ALU.add))
                    if o is g.D:
                        quarter = o.chunks // QUARTERS
                        ch.step(nc.vector.memset(place[:], 0.0))
                        for q in range(1, QUARTERS):
                            cut = g.crossing[:, q - 1, :]
                            ch.step(nc.vector.tensor_scalar(cut, marked[:], float(q * quarter), None, ALU.is_ge))
                            ch.step(nc.vector.tensor_add(place[:], place[:], cut))
                            ch.step(nc.vector.scalar_tensor_tensor(cut, start[:], float(q * quarter), cut, ALU.is_lt, ALU.mult))
                        ch.step(nc.vector.scalar_tensor_tensor(marked[:], place[:], -float(quarter), marked[:], ALU.mult, ALU.add))
                        ch.step(nc.vector.scalar_tensor_tensor(marked[:], marked[:], float(QUARTERS), place[:], ALU.mult, ALU.add))
                    ch.step(nc.vector.tensor_copy(o.last[:], marked[:]))
                    ch.step(nc.vector.tensor_scalar(marked[:], g.valid[:], -PAD_START, PAD_START, ALU.mult, ALU.add))
                    ch.step(nc.vector.tensor_add(marked[:], marked[:], start[:]))
                    nc.vector.tensor_copy(mark[n][:], marked[:]).then_inc(ready, 1)

            @block.tensor
            def _(pe):
                for n, o in enumerate(g.orders):
                    pe.wait_ge(needed, n + 1)
                    nc.tensor.matmul(ps_in[:], g.below[:], need[:], start=True, stop=True)
                    nc.tensor.matmul(ps_tot[:], g.ones[:], need[:], start=True, stop=True).then_inc(summed, 1)

            @block.gpsimd
            def _(pool):
                for n, o in enumerate(g.orders):
                    pool.wait_ge(ready, n + 1)
                    for b in range(NB):
                        pool.indirect_dma_start(
                            out=o.first[:, :], out_offset=bass.IndirectOffsetOnAxis(ap=mark[n][:, b:b + 1], axis=0),
                            in_=g.ones[:, 0:1], in_offset=None, bounds_check=o.chunks - 1,
                            oob_is_err=False).then_inc(scattered, 16)
                pool.wait_ge(scattered, 2 * NB * 16)


def stage_sort(nc, g, o):
    W = o.words
    A = W - 1
    with ExitStack() as c:
        sb = lambda name, shape, dt: c.enter_context(nc.sbuf_tensor(f"so_{o.name}_{name}", shape, dt))
        ps = lambda name, shape: c.enter_context(nc.psum_tensor(f"so_{o.name}_{name}", shape, F32))
        sem = lambda name: new_sem(nc, c, f"so_{o.name}_{name}")
        two = range(2)
        row = [sb(f"row{i}", [P, P * HB], I32) for i in two]
        row_lo = sb("row_lo", [P, P * HB], I32)
        lo_t = [sb(f"lo_t{i}", [P, P, HB], F32) for i in two]
        lo1 = [sb(f"lo1{i}", [P, HB, P], BF16) for i in two]
        hi1 = [sb(f"hi1{i}", [P, HB, NH], BF16) for i in two]
        same = sb("same", [P, HB, P], BF16)
        rank = [sb(f"rank{i}", [P, HB], F32) for i in two]
        table = [sb(f"table{i}", [P, HB + 1, NH], F32) for i in two]
        pick = sb("pick", [P, HB, NH], F32)
        slot = sb("slot", [P, HB], F32)
        slot_i = sb("slot_i", [P, HB], I32)
        part_i = sb("part_i", [P, HB], I32)
        part = sb("part", [P, HB], F32)
        place = [sb(f"place{i}", [P, HB], I32) for i in two]
        rec = [sb(f"rec{i}", [P, HB, W], I32) for i in two]
        ps_hist = [ps(f"hist{i}", [P, HB, NH]) for i in two]
        ps_look = [ps(f"look{i}", [P, HB, NH]) for i in two]
        row_in = [sem(f"row_in{i}") for i in two]
        row_used, onehots, hist, tables, looked = sem("row_used"), sem("onehots"), sem("hist"), sem("tables"), sem("looked")
        looks_read, placed, taken = sem("looks_read"), sem("placed"), sem("taken")
        scattered = [rows_sem(nc, f"so_{o.name}_scattered{i}") for i in two]
        steps = sem("steps")
        half = STEPS // 2
        with nc.Block() as block:
            @block.sync
            def _(sp):
                def load(step, b):
                    src = g.pad[o.key][bass.ds(step * (P * HB), P * HB)]
                    sp.dma_start(row[b][:], src.rearrange("(a f) -> a f", a=1).to_broadcast([P, P * HB])).then_inc(row_in[b], 16)

                for b in two:
                    load(b, b)
                with sp.Fori(1, half) as i:
                    for b in two:
                        sp.wait_ge(row_used, i * 2 + (b - 1))
                        load(i * 2 + b, b)
                sp.wait_ge(row_in[0], 16 * half)
                sp.wait_ge(row_in[1], 16 * half)

            @block.vector
            def _(dve):
                ch = Chain(dve, steps)

                def digits(step, b, turn, first):
                    cols = bass.ds(step * HB, HB)
                    dve.wait_ge(row_in[b], turn * 16 + 16)
                    nc.vector.tensor_tensor(lo1[b][:], g.iota_row[:].unsqueeze(1).to_broadcast([P, HB, P]),
                                            g.lo[o.key][:, cols].unsqueeze(2).to_broadcast([P, HB, P]), ALU.is_equal)
                    nc.vector.tensor_tensor(hi1[b][:], g.iota_row[:, 0:NH].unsqueeze(1).to_broadcast([P, HB, NH]),
                                            g.hi[o.key][:, cols].unsqueeze(2).to_broadcast([P, HB, NH]),
                                            ALU.is_equal).then_inc(onehots, 1)
                    ch.step(nc.vector.tensor_scalar(row_lo[:], row[b][:], P - 1, None, ALU.bitwise_and))
                    nc.vector.tensor_scalar(lo_t[b][:].rearrange("p e j -> p (e j)"), row_lo[:], g.pidx[:], None, ALU.is_equal)
                    keys = row[b][:].rearrange("p (e j) -> p e j", j=HB)
                    for j in range(HB):
                        last = nc.vector.scalar_tensor_tensor(same[:, j, :], keys[:, :, j], g.key_f[o.key][:, bass.ds(step * HB + j, 1)],
                                                              g.before[:], ALU.is_equal, ALU.mult, accum_out=rank[b][:, j:j + 1])
                    last.then_inc(row_used, 1)
                    dve.wait_ge(hist, step + 1)
                    if first:
                        ch.step(nc.vector.tensor_copy(table[b][:, 0, :], o.slot0[:]))
                    else:
                        ch.step(nc.vector.tensor_copy(table[b][:, 0, :], table[1 - b][:, HB, :]))
                    for j in range(HB):
                        ins = nc.vector.tensor_add(table[b][:, j + 1, :], table[b][:, j, :], ps_hist[b][:, j, :])
                        ch.step(ins)
                    dve.sem_inc(tables, 1)

                def places(step, b, turn, first):
                    cols = bass.ds(step * HB, HB)
                    dve.wait_ge(looked, step + 1)
                    nc.vector.tensor_mul(pick[:], ps_look[b][:], hi1[b][:]).then_inc(looks_read, 1)
                    dve.wait_ge(looks_read, step + 1)
                    ch.step(nc.vector.tensor_reduce(slot[:], pick[:], AX.X, ALU.add))
                    ch.step(nc.vector.tensor_add(slot[:], slot[:], rank[b][:]))
                    ch.step(nc.vector.tensor_copy(slot_i[:], slot[:]))
                    ch.step(nc.vector.tensor_scalar(part_i[:], slot_i[:], P - 1, None, ALU.bitwise_and))
                    ch.step(nc.vector.tensor_copy(part[:], part_i[:]))
                    ch.step(nc.vector.tensor_scalar(slot_i[:], slot_i[:], 7, None, ALU.logical_shift_right))
                    ch.step(nc.vector.tensor_copy(slot[:], slot_i[:]))
                    if not first:
                        dve.wait_ge(scattered[b], turn * (16 * HB))
                    nc.vector.scalar_tensor_tensor(place[b][:], part[:], float(o.tiles), slot[:], ALU.mult, ALU.add)
                    nc.vector.tensor_copy(rec[b][:, :, 0], g.key_i[o.other][:, cols])
                    nc.vector.tensor_copy(rec[b][:, :, 1:W].bitcast(F32),
                                          g.attr[o.attr][:, bass.ds(step * (HB * A), HB * A)].rearrange("p (j a) -> p j a", a=A)).then_inc(placed, 1)

                digits(0, 0, 0, True)
                digits(1, 1, 0, False)
                places(0, 0, 0, True)
                ch.restart()
                digits(2, 0, 1, False)
                places(1, 1, 0, True)
                with dve.Fori(1, half - 1) as i:
                    ch.restart()
                    digits(i * 2 + 1, 1, i, False)
                    places(i * 2, 0, i, False)
                    digits(i * 2 + 2, 0, i + 1, False)
                    places(i * 2 + 1, 1, i, False)
                ch.restart()
                digits(STEPS - 1, 1, half - 1, False)
                places(STEPS - 2, 0, half - 1, False)
                places(STEPS - 1, 1, half - 1, False)

            @block.tensor
            def _(pe):
                def histograms(step, b):
                    pe.wait_ge(onehots, step + 1)
                    for j in range(HB):
                        last = nc.tensor.matmul(ps_hist[b][:, j, :], lo1[b][:, j, :], hi1[b][:, j, :], start=True, stop=True)
                    last.then_inc(hist, 1)

                def lookups(step, b):
                    pe.wait_ge(tables, step + 1)
                    for j in range(HB):
                        last = nc.tensor.matmul(ps_look[b][:, j, :], lo_t[b][:, :, j], table[b][:, j, :], start=True, stop=True)
                    last.then_inc(looked, 1)

                histograms(0, 0)
                lookups(0, 0)
                with pe.Fori(0, half - 1) as i:
                    histograms(i * 2 + 1, 1)
                    lookups(i * 2 + 1, 1)
                    histograms(i * 2 + 2, 0)
                    lookups(i * 2 + 2, 0)
                histograms(STEPS - 1, 1)
                lookups(STEPS - 1, 1)

            @block.gpsimd
            def _(pool):
                bound = pool.to_reg(o.slots - 1)
                with pool.Fori(0, half) as i:
                    for b in two:
                        pool.wait_ge(placed, i * 2 + (b + 1))
                        pool.sem_inc(taken, 1)
                        for j in range(HB):
                            pool.indirect_dma_start(
                                out=o.rec[:, :], out_offset=bass.IndirectOffsetOnAxis(ap=place[b][:, j:j + 1], axis=0),
                                in_=rec[b][:, j, :], in_offset=None, bounds_check=bound,
                                oob_is_err=False).then_inc(scattered[b], 16)
                for b in two:
                    pool.wait_ge(scattered[b], half * 16 * HB)



def stage_chunks(nc, g):
    with ExitStack() as c:
        sb = lambda name, shape, dt=F32: c.enter_context(nc.sbuf_tensor(name, shape, dt))
        sem = lambda name: new_sem(nc, c, name)
        first = {o.name: sb(f"ck_first_{o.name}", [P, o.chunks // P]) for o in g.orders}
        keep = {o.name: sb(f"ck_keep_{o.name}", [P, o.chunks // P]) for o in g.orders}
        line = sb("ck_line", [1, g.R.chunks])
        line_one = sb("ck_line_one", [1, g.R.chunks])
        nodes = sb("ck_nodes", [1, g.R.chunks])
        nodes_i = sb("ck_nodes_i", [1, g.R.chunks], I32)
        loaded, steps, made, stored = sem("ck_loaded"), sem("ck_steps"), sem("ck_made"), sem("ck_stored")
        with nc.Block() as block:
            @block.sync
            def _(sp):
                for o in g.orders:
                    sp.dma_start(first[o.name][:], o.first.rearrange("(p f) w -> p (f w)", p=P)).then_inc(loaded, 16)
                sp.dma_start(line[:], g.R.first.rearrange("v w -> w v")).then_inc(loaded, 16)
                sp.wait_ge(made, 2)
                for o in g.orders:
                    sp.dma_start(o.keep[0:o.chunks].rearrange("(p f) -> p f", p=P), keep[o.name][:]).then_inc(stored, 16)
                sp.wait_ge(made, 3)
                sp.dma_start(g.chunk_node.rearrange("(a v) -> a v", a=1), nodes_i[:]).then_inc(stored, 16)
                sp.dma_start(g.R.keep[g.R.chunks:g.R.chunks + g.R.vb].rearrange("(a v) -> a v", a=1), line_one[:, 0:g.R.vb]).then_inc(stored, 16)
                sp.wait_ge(stored, 64)
                sp.dma_start(g.chunk_row[:], g.chunk_node.rearrange("(p f) -> p f", p=P)).then_inc(loaded, 16)
                sp.wait_ge(loaded, 64)

            @block.vector
            def _(dve):
                ch = Chain(dve, steps)
                ch.step(nc.vector.memset(line_one[:], 1.0))
                dve.wait_ge(loaded, 48)
                for o in g.orders:
                    nc.vector.tensor_scalar(keep[o.name][:], first[o.name][:], -1.0, 1.0, ALU.mult, ALU.add).then_inc(made, 1)
                ch.step(nc.vector.tensor_tensor_scan(nodes[:], line_one[:], line[:], -1.0, ALU.mult, ALU.add))
                nc.vector.tensor_copy(nodes_i[:], nodes[:]).then_inc(made, 1)


def stage_spread(nc, g, name, table, width, to):
    per = g.R.chunks // P
    with ExitStack() as c:
        rows = c.enter_context(nc.sbuf_tensor(f"{name}_rows", [P, per, width], F32))
        got, stored = rows_sem(nc, f"{name}_got"), new_sem(nc, c, f"{name}_stored")
        with nc.Block() as block:
            @block.gpsimd
            def _(pool):
                for j in range(per):
                    pool.indirect_dma_start(out=rows[:, j, :], out_offset=None, in_=table[:, :],
                                            in_offset=bass.IndirectOffsetOnAxis(ap=g.chunk_row[:, j:j + 1], axis=0)).then_inc(got, 16)

            @block.sync
            def _(sp):
                sp.wait_ge(got, 16 * per)
                sp.dma_start(to.rearrange("(p f) w -> p (f w)", p=P), rows[:].rearrange("p f w -> p (f w)")).then_inc(stored, 16)
                sp.wait_ge(stored, 16)


def stage_collect(nc, g, name, o, sums, width, to):
    with ExitStack() as c:
        got = rows_sem(nc, f"{name}_got")
        with nc.Block() as block:
            @block.gpsimd
            def _(pool):
                for b in range(NB):
                    pool.indirect_dma_start(out=to[:, b, :], out_offset=None, in_=sums[:, :],
                                            in_offset=bass.IndirectOffsetOnAxis(ap=o.last[:, b:b + 1], axis=0)).then_inc(got, 16)
                pool.wait_ge(got, 16 * NB)


def stage_collect_quarters(nc, g, name, sums, to):
    o = g.D
    last_row = (o.chunks // QUARTERS - 1) * QUARTERS
    with ExitStack() as c:
        ends = c.enter_context(nc.sbuf_tensor(f"{name}_ends", [P, QUARTERS - 1, F], F32))
        part = c.enter_context(nc.sbuf_tensor(f"{name}_part", [P, NB, F], F32))
        got = rows_sem(nc, f"{name}_got")
        loaded, steps = new_sem(nc, c, f"{name}_loaded"), new_sem(nc, c, f"{name}_steps")
        b3 = [P, NB, F]
        with nc.Block() as block:
            @block.gpsimd
            def _(pool):
                for b in range(NB):
                    pool.indirect_dma_start(out=to[:, b, :], out_offset=None, in_=sums[:, :],
                                            in_offset=bass.IndirectOffsetOnAxis(ap=o.last[:, b:b + 1], axis=0)).then_inc(got, 16)

            @block.sync
            def _(sp):
                sp.dma_start(ends[:].rearrange("p q f -> p (q f)"), sums[last_row:last_row + QUARTERS - 1, :]
                             .rearrange("q f -> (q f)").unsqueeze(0).to_broadcast([P, (QUARTERS - 1) * F])).then_inc(loaded, 16)

            @block.vector
            def _(dve):
                ch = Chain(dve, steps)
                dve.wait_ge(loaded, 16)
                for q in range(QUARTERS - 1):
                    ch.step(nc.vector.tensor_mul(part[:], g.crossing[:, q, :].unsqueeze(2).to_broadcast(b3),
                                                 ends[:, q, :].unsqueeze(1).to_broadcast(b3)))
                    if q == 0:
                        dve.wait_ge(got, 16 * NB)
                    ch.step(nc.vector.tensor_add(to[:], to[:], part[:]))


def stage_gaussians(nc, g, mu_in, sigma_in, gauss):
    o = g.D
    per = o.tiles // QUARTERS
    with ExitStack() as c:
        sb = lambda nm, shape, dt=F32: c.enter_context(nc.sbuf_tensor(f"ga_{nm}", shape, dt))
        sem = lambda nm: new_sem(nc, c, f"ga_{nm}")
        rec = sb("rec", [P, o.tiles, o.words], I32)
        mu, scale, diff = sb("mu", [P, 3, 2]), sb("scale", [P, 3, 2]), sb("diff", [P, per, 3, 2])
        loaded, steps, dists, done = sem("loaded"), sem("steps"), sem("dists"), sem("done")
        b4 = [P, per, 3, 2]
        with nc.Block() as block:
            @block.sync
            def _(sp):
                sp.dma_start(rec[:].rearrange("p t w -> p (t w)"), o.rec.rearrange("(p t) w -> p (t w)", p=P)).then_inc(loaded, 16)
                for to, view in ((mu, mu_in), (scale, sigma_in)):
                    sp.dma_start(to[:].rearrange("p k d -> p (k d)"),
                                 view.rearrange("k d -> (k d)").unsqueeze(0).to_broadcast([P, 6])).then_inc(loaded, 16)
                sp.wait_ge(loaded, 48)

            @block.vector
            def _(dve):
                ch = Chain(dve, steps)
                dve.wait_ge(loaded, 48)
                ch.step(nc.vector.tensor_mul(scale[:], scale[:], scale[:]))
                ch.step(nc.vector.tensor_scalar(scale[:], scale[:], 1e-15, None, ALU.add))
                ch.step(nc.vector.reciprocal(scale[:], scale[:]))
                for q in range(QUARTERS):
                    attr = rec[:, q * per:(q + 1) * per, 1:3].bitcast(F32)
                    ch.step(nc.vector.tensor_sub(diff[:], attr.unsqueeze(2).to_broadcast(b4), mu[:].unsqueeze(1).to_broadcast(b4)))
                    ch.step(nc.vector.tensor_mul(diff[:], diff[:], diff[:]))
                    ch.step(nc.vector.tensor_mul(diff[:], diff[:], scale[:].unsqueeze(1).to_broadcast(b4)))
                    ch.step(nc.vector.tensor_reduce(gauss[:, :, q, :], diff[:], AX.X, ALU.add))
                dve.sem_inc(dists, 1)

            @block.scalar
            def _(act):
                act.wait_ge(dists, 1)
                flat = gauss[:].rearrange("p t q k -> p (t q k)")
                nc.scalar.activation(flat, flat, ACT.Exp, scale=-0.5).then_inc(done, 1)
                act.wait_ge(done, 1)


def stage_dense(nc, g, name, src, k, weights, width, dst, weight_parts):
    G5 = 5
    with ExitStack() as c:
        sb = lambda nm, shape, dt=F32: c.enter_context(nc.sbuf_tensor(f"{name}_{nm}", shape, dt))
        sem = lambda nm: new_sem(nc, c, f"{name}_{nm}")
        rows = sb("rows", [P, G5, k])
        cols = sb("cols", [k, G5, P])
        ps_t = [c.enter_context(nc.psum_tensor(f"{name}_ps_t{i}", [k, 4, P], F32)) for i in range(2)]
        ps_o = c.enter_context(nc.psum_tensor(f"{name}_ps_o", [P, G5, width], F32))
        loaded, staged, turned, copied, done, taken, seen = (
            sem(n) for n in ("loaded", "staged", "turned", "copied", "done", "taken", "seen"))
        with nc.Block() as block:
            @block.sync
            def _(sp):
                for to, view in weight_parts:
                    sp.dma_start(to, view).then_inc(loaded, 16)
                if weight_parts:
                    sp.wait_ge(loaded, 16 * len(weight_parts))

            @block.vector
            def _(dve):
                with dve.Fori(0, NB // G5) as i:
                    nc.vector.tensor_copy(rows[:], src[:, bass.ds(i * G5, G5), 0:k]).then_inc(staged, 1)
                    dve.wait_ge(done, i + 1)
                    nc.vector.tensor_copy(dst[:, bass.ds(i * G5, G5), :], ps_o[:]).then_inc(taken, 1)
                    dve.wait_ge(taken, i + 1)

            @block.tensor
            def _(pe):
                if weight_parts:
                    pe.wait_ge(loaded, 16 * len(weight_parts))
                with pe.Fori(0, NB // G5) as i:
                    pe.wait_ge(staged, i + 1)
                    pe.sem_inc(seen, 1)
                    for j in range(G5):
                        last = nc.tensor.transpose(ps_t[j // 4][:, j % 4, :], rows[:, j, :], g.ident[:])
                    last.then_inc(turned, 1)
                    pe.wait_ge(copied, i + 1)
                    for j in range(G5):
                        last = nc.tensor.matmul(ps_o[:, j, :], cols[:, j, :], weights, start=True, stop=True)
                    last.then_inc(done, 1)

            @block.scalar
            def _(act):
                with act.Fori(0, NB // G5) as i:
                    act.wait_ge(turned, i + 1)
                    nc.scalar.copy(cols[:, 0:4, :], ps_t[0][:])
                    nc.scalar.copy(cols[:, 4:5, :], ps_t[1][:, 0:1, :]).then_inc(copied, 1)


def layernorm(ch, nc, g, t, out, act):
    b3 = lambda ap: ap.unsqueeze(2).to_broadcast([P, NB, F])
    ch.step(nc.vector.tensor_reduce(t.mean[:], g.x[:], AX.X, ALU.add))
    ch.step(nc.vector.tensor_scalar(t.mean[:], t.mean[:], 1.0 / F, None, ALU.mult))
    ch.step(nc.vector.tensor_sub(t.centred[:], g.x[:], b3(t.mean[:])))
    ch.step(nc.vector.tensor_mul(t.square[:], t.centred[:], t.centred[:]))
    ch.step(nc.vector.tensor_reduce(t.var[:], t.square[:], AX.X, ALU.add))
    ch.step(nc.vector.tensor_scalar(t.var[:], t.var[:], 1.0 / F, EPS_LN, ALU.mult, ALU.add))
    act(t.var[:], ACT.Sqrt)
    ch.step(nc.vector.reciprocal(t.var[:], t.var[:]))
    ch.step(nc.vector.tensor_mul(t.centred[:], t.centred[:], b3(t.var[:])))
    ch.step(nc.vector.tensor_scalar(t.centred[:], t.centred[:], 0.0, None, ALU.max))
    ch.step(nc.vector.tensor_mul(out, t.centred[:], b3(g.valid[:])))


class NormBuffers:
    def __init__(self, nc, c, name):
        sb = lambda nm, shape: c.enter_context(nc.sbuf_tensor(f"{name}_{nm}", shape, F32))
        self.mean, self.var = sb("mean", [P, NB]), sb("var", [P, NB])
        self.centred, self.square = sb("centred", [P, NB, F]), sb("square", [P, NB, F])


def node_rows(table):
    return table.rearrange("(b p) w -> p b w", p=P)



def stage_attention_inputs(nc, g, ins):
    with ExitStack() as c:
        sb = lambda name, shape, dt=F32: c.enter_context(nc.sbuf_tensor(name, shape, dt))
        sem = lambda name: new_sem(nc, c, name)
        w = sb("a0_w", [F, 4, F])
        fc = sb("a0_fc", [F, 2 * F])
        prod = sb("a0_prod", [F, 4, F])
        loaded, steps, zeroed = sem("a0_loaded"), sem("a0_steps"), sem("a0_zeroed")
        full = (NB - 1) * P
        with nc.Block() as block:
            @block.gpsimd
            def _(pool):
                nc.gpsimd.memset(g.x[:], 0.0).then_inc(zeroed, 1)

            @block.sync
            def _(sp):
                sp.dma_start(w[:], ins["L0_gnn_w"].rearrange("h f o -> f h o")).then_inc(loaded, 16)
                sp.dma_start(fc[:], ins["L0_gnn_fc_w"].to_broadcast([F, 2 * F])).then_inc(loaded, 16)
                sp.wait_ge(zeroed, 1)
                sp.dma_start(g.x[:, 0:NB - 1, :], ins["x"][0:full, :].rearrange("(b p) f -> p b f", p=P)).then_inc(loaded, 16)
                sp.dma_start(g.x[0:N - full, NB - 1, :], ins["x"][full:N, :]).then_inc(loaded, 16)
                sp.wait_ge(loaded, 64)

            @block.vector
            def _(dve):
                ch = Chain(dve, steps)
                dve.wait_ge(loaded, 64)
                for half in range(2):
                    ch.step(nc.vector.tensor_mul(prod[:], w[:], fc[:, half * F:(half + 1) * F].unsqueeze(1).to_broadcast([F, 4, F])))
                    ch.step(nc.vector.tensor_reduce(g.att_w[:, half * 4:half * 4 + 4], prod[:], AX.X, ALU.add))


def stage_attention_tables(nc, g, ins):
    with ExitStack() as c:
        sb = lambda name, shape, dt=F32: c.enter_context(nc.sbuf_tensor(name, shape, dt))
        sem = lambda name: new_sem(nc, c, name)
        row = sb("a1_row", [P, NB, FAR])
        near = sb("a1_near", [P, NB, 4])
        off = sb("a1_off", [P, NB])
        fc_b = sb("a1_fc_b", [P, 1])
        loaded, steps, made, stored = sem("a1_loaded"), sem("a1_steps"), sem("a1_made"), sem("a1_stored")
        with nc.Block() as block:
            @block.sync
            def _(sp):
                sp.dma_start(fc_b[:], ins["L0_gnn_fc_b"].rearrange("(a b) -> a b", a=1).to_broadcast([P, 1])).then_inc(loaded, 16)
                sp.wait_ge(made, 1)
                sp.dma_start(node_rows(g.att_table), row[:]).then_inc(stored, 16)
                sp.dma_start(node_rows(g.near_table), near[:]).then_inc(stored, 16)
                sp.wait_ge(stored, 32)

            @block.vector
            def _(dve):
                ch = Chain(dve, steps)
                nc.vector.tensor_copy(row[:, :, 0:F], g.h[:])
                nc.vector.tensor_copy(row[:, :, F], g.valid[:])
                nc.vector.tensor_copy(row[:, :, F + 5:FAR], g.spline_h[:])
                ch.step(nc.vector.tensor_scalar(off[:], g.valid[:], BIG, -BIG, ALU.mult, ALU.add))
                ch.step(nc.vector.tensor_add(row[:, :, F + 1:F + 5], g.att[:, :, 4:8], off[:].unsqueeze(2).to_broadcast([P, NB, 4])))
                dve.wait_ge(loaded, 16)
                nc.vector.tensor_scalar(near[:], g.att[:, :, 0:4], fc_b[:], None, ALU.add).then_inc(made, 1)


def stage_attention(nc, g):
    o = g.R
    C8, S = o.per_tile, o.chunk
    with ExitStack() as c:
        sb = lambda name, shape, dt=F32: c.enter_context(nc.sbuf_tensor(f"at_{name}", shape, dt))
        ps = lambda name, shape: c.enter_context(nc.psum_tensor(f"at_{name}", shape, F32))
        sem = lambda name: new_sem(nc, c, f"at_{name}")
        two = range(2)
        rec = [sb(f"rec{b}", [P, TB, o.words], I32) for b in two]
        far = [sb(f"far{b}", [P, TB, FAR]) for b in two]
        near = [sb(f"near{b}", [P, C8]) for b in two]
        score = sb("score", [P, C8, S])
        leaky = sb("leaky", [P, C8, S])
        shifted = sb("shifted", [P, C8, S])
        top = [sb(f"top{b}", [P, C8]) for b in two]
        prob = sb("prob", [P, P])
        term = sb("term", [P, 4, TB])
        spread = sb("spread", [P, TB, 4, C8])
        sums = [sb(f"sums{b}", [F + 1, 4, TB, C8]) for b in two]
        ps_far, ps_prob = ps("ps_far", [P, C8, S]), ps("ps_prob", [P, 4, TB])
        ps_sum = [ps(f"ps_sum{k}", [F + 1, TB // 2, 4, C8]) for k in two]
        rec_in, near_in = [sem(f"rec_in{b}") for b in two], [sem(f"near_in{b}") for b in two]
        far_in = [rows_sem(nc, f"at_far_in{b}") for b in two]
        stored = [sem(f"stored{b}") for b in two]
        sums_out, top_out = [sem(f"sums_out{b}") for b in two], [sem(f"top_out{b}") for b in two]
        steps, taken, terms = sem("steps"), sem("taken"), sem("terms")
        turned, shifts, probs, turned_back, spreads, summed, copied = (
            sem(n) for n in ("turned", "shifts", "probs", "turned_back", "spreads", "summed", "copied"))
        rec_v = o.rec.rearrange("(p t) w -> p t w", p=P)
        near_v = g.near_chunk.rearrange("(t c) h -> h t c", c=C8)
        with nc.Block() as block:
            @block.sync
            def _(sp):
                def load(n, b):
                    sp.dma_start(rec[b][:], rec_v[:, bass.ds(n * TB, TB), :]).then_inc(rec_in[b], 16)
                    for h in range(4):
                        sp.dma_start(near[b][h * TB:(h + 1) * TB, :], near_v[h, bass.ds(n * TB, TB), :],
                                     allow_slow_non_contiguous=True).then_inc(near_in[b], 16)

                for b in two:
                    load(b, b)
                def store(n, b, turn):
                    sp.wait_ge(far_in[b], turn * (16 * TB) + 16 * TB)
                    sp.dma_start(g.far_64[:, bass.ds(n * TB, TB), :], far[b][:, :, F + 5:FAR]).then_inc(stored[b], 16)

                with sp.Fori(0, o.pairs - 1) as i:
                    for b in two:
                        store(i * 2 + b, b, i)
                        sp.wait_ge(summed, i * 2 + (b + 2))
                        sp.wait_ge(stored[b], i * 16 + 16)
                        load(i * 2 + (b + 2), b)
                for b in two:
                    store(o.blocks - 2 + b, b, o.pairs - 1)
                for b in two:
                    sp.wait_ge(stored[b], 16 * o.pairs)

            @block.gpsimd
            def _(pool):
                with pool.Fori(0, o.pairs) as i:
                    for b in two:
                        pool.wait_ge(rec_in[b], i * 16 + 16)
                        pool.sem_inc(taken, 1)
                        for t in range(TB):
                            pool.indirect_dma_start(out=far[b][:, t, :], out_offset=None, in_=g.att_table[:, :],
                                                    in_offset=bass.IndirectOffsetOnAxis(ap=rec[b][:, t, 0:1], axis=0)).then_inc(far_in[b], 16)

            @block.tensor
            def _(pe):
                pe.sem_inc(summed, 1)
                pe.sem_inc(turned, 1)
                pe.sem_inc(turned_back, 1)
                with pe.Fori(0, o.pairs) as i:
                    for b in two:
                        n = i * 2 + b
                        pe.wait_ge(terms, n + 1)
                        pe.wait_ge(shifts, n + 1)
                        nc.tensor.transpose(ps_far[:].rearrange("p c s -> p (c s)"),
                                            term[:].rearrange("p h t -> p (h t)"), g.ident[:]).then_inc(turned, 1)
                        pe.wait_ge(probs, n + 2)
                        nc.tensor.transpose(ps_prob[:].rearrange("p h t -> p (h t)"), prob[:], g.ident[:]).then_inc(turned_back, 1)
                        pe.wait_ge(spreads, n + 1)
                        pe.wait_ge(copied, n + 1)
                        for t in range(TB):
                            last = nc.tensor.matmul(ps_sum[t // (TB // 2)][:, t % (TB // 2), :, :], far[b][:, t, 0:F + 1],
                                                    spread[:, t, :, :], start=True, stop=True)
                        last.then_inc(summed, 1)

            @block.vector
            def _(dve):
                dve.sem_inc(shifts, 1)
                ch = Chain(dve, steps)
                with dve.Fori(0, o.pairs) as i:
                    ch.restart()
                    for b in two:
                        n = i * 2 + b
                        dve.wait_ge(turned, n + 2)
                        dve.wait_ge(near_in[b], i * 64 + 64)
                        ch.step(nc.vector.tensor_add(score[:], ps_far[:], near[b][:].unsqueeze(2).to_broadcast([P, C8, S])))
                        ch.step(nc.vector.scalar_tensor_tensor(leaky[:], score[:], 0.2, score[:], ALU.mult, ALU.max))
                        dve.wait_ge(top_out[b], i * 64 + 64)
                        ch.step(nc.vector.tensor_reduce(top[b][:], leaky[:], AX.X, ALU.max))
                        dve.wait_ge(probs, n + 1)
                        nc.vector.tensor_sub(shifted[:], leaky[:], top[b][:].unsqueeze(2).to_broadcast([P, C8, S])).then_inc(shifts, 1)
                        dve.wait_ge(turned_back, n + 2)
                        dve.wait_ge(summed, n + 1)
                        nc.vector.tensor_mul(spread[:], ps_prob[:].rearrange("p h t -> p t h").unsqueeze(3).to_broadcast([P, TB, 4, C8]),
                                             o.mask[:].unsqueeze(1).unsqueeze(1).to_broadcast([P, TB, 4, C8])).then_inc(spreads, 1)

            @block.scalar
            def _(act):
                act.sem_inc(copied, 1)
                act.sem_inc(probs, 1)
                for b in two:
                    act.sem_inc(top_out[b], 64)
                for b in two:
                    act.sem_inc(sums_out[b], 16)
                with act.Fori(0, o.pairs) as i:
                    for b in two:
                        n = i * 2 + b
                        act.wait_ge(far_in[b], i * (16 * TB) + 16 * TB)
                        act.wait_ge(turned, n + 1)
                        nc.scalar.copy(term[:], far[b][:, :, F + 1:F + 5].rearrange("p t h -> p h t")).then_inc(terms, 1)
                        act.wait_ge(shifts, n + 2)
                        act.wait_ge(turned_back, n + 1)
                        nc.scalar.activation(prob[:], shifted[:].rearrange("p c s -> p (c s)"), ACT.Exp).then_inc(probs, 1)
                        for h in range(4):
                            act.dma_start(g.top[h, bass.ds(n * o.vb, o.vb)].rearrange("(t c) -> t c", c=C8),
                                          top[b][h * TB:(h + 1) * TB, :]).then_inc(top_out[b], 16)
                        act.wait_ge(summed, n + 2)
                        act.wait_ge(sums_out[b], i * 16 + 16)
                        for k in two:
                            half = slice(k * (TB // 2), (k + 1) * (TB // 2))
                            last = nc.scalar.copy(sums[b][:, :, half, :].rearrange("f h t c -> f t h c"), ps_sum[k][:])
                        last.then_inc(copied, 1)
                        act.wait_ge(copied, n + 2)
                        act.dma_start(g.att_raw[:, bass.ds(n * (4 * o.vb), 4 * o.vb)],
                                      sums[b][:].rearrange("f h t c -> f (h t c)")).then_inc(sums_out[b], 16)
                for b in two:
                    act.wait_ge(sums_out[b], 16 * o.pairs + 16)
                    act.wait_ge(top_out[b], 64 * o.pairs + 64)


def stage_attention_factors(nc, g):
    o = g.R
    V = o.chunks
    with ExitStack() as c:
        sb = lambda name, shape, dt=F32: c.enter_context(nc.sbuf_tensor(f"af_{name}", shape, dt))
        sem = lambda name: new_sem(nc, c, f"af_{name}")
        top, keep, upto = sb("top", [4, V]), sb("keep", [4, V]), sb("upto", [4, V])
        decay = sb("decay", [4, V])
        loaded, steps, differences, exps, made, stored = (sem(n) for n in ("loaded", "steps", "differences", "exps", "made", "stored"))
        with nc.Block() as block:
            @block.sync
            def _(sp):
                sp.dma_start(top[:], g.top).then_inc(loaded, 16)
                sp.dma_start(keep[:], o.keep[0:V].rearrange("(a v) -> a v", a=1).to_broadcast([4, V])).then_inc(loaded, 16)
                sp.wait_ge(exps, 1)
                sp.dma_start(g.factor, top[:]).then_inc(stored, 16)
                sp.wait_ge(made, 1)
                sp.dma_start(g.decay, decay[:]).then_inc(stored, 16)
                sp.wait_ge(stored, 32)

            @block.vector
            def _(dve):
                ch = Chain(dve, steps)
                dve.wait_ge(loaded, 32)
                ch.step(nc.vector.tensor_scalar(decay[:], keep[:], 1.0e38, -1.0e38, ALU.mult, ALU.add))
                ch.step(nc.vector.tensor_tensor_scan(upto[:], decay[:], top[:], 0.0, ALU.add, ALU.max))
                nc.vector.tensor_sub(top[:], top[:], upto[:]).then_inc(differences, 1)
                ch.step(nc.vector.memset(decay[:, 0:1], 0.0))
                ch.step(nc.vector.tensor_sub(decay[:, 1:V], upto[:, 0:V - 1], upto[:, 1:V]))
                nc.vector.tensor_scalar(decay[:], decay[:], 0.0, None, ALU.min).then_inc(differences, 1)
                dve.wait_ge(exps, 2)
                nc.vector.tensor_mul(decay[:], decay[:], keep[:]).then_inc(made, 1)

            @block.scalar
            def _(act):
                act.wait_ge(differences, 1)
                nc.scalar.activation(top[:], top[:], ACT.Exp).then_inc(exps, 1)
                act.wait_ge(differences, 2)
                nc.scalar.activation(decay[:], decay[:], ACT.Exp).then_inc(exps, 1)


def stage_attention_join(nc, g):
    o = g.R
    V, W = o.vb, 4 * (F + 1)
    parts = V // P
    with ExitStack() as c:
        sb = lambda name, shape, dt=F32: c.enter_context(nc.sbuf_tensor(f"aj_{name}", shape, dt))
        sem = lambda name: new_sem(nc, c, f"aj_{name}")
        two = range(2)
        raw = [sb(f"raw{b}", [F + 1, 4, V]) for b in two]
        factor = [sb(f"factor{b}", [F + 1, 4, V]) for b in two]
        decay = [sb(f"decay{b}", [F + 1, 4, V]) for b in two]
        run = [sb(f"run{b}", [F + 1, 4, V]) for b in two]
        rows = [sb(f"rows{b}", [P, parts, W]) for b in two]
        ps_rows = c.enter_context(nc.psum_tensor("aj_ps_rows", [P, parts, 256], F32))
        loaded, out = [sem(f"loaded{b}") for b in two], [sem(f"out{b}") for b in two]
        steps, scanned, turned, copied, seen = (sem(n) for n in ("steps", "scanned", "turned", "copied", "seen"))
        with nc.Block() as block:
            @block.sync
            def _(sp):
                def load(n, b):
                    sp.dma_start(raw[b][:].rearrange("f h v -> f (h v)"),
                                 g.att_raw[:, bass.ds(n * (4 * V), 4 * V)]).then_inc(loaded[b], 16)
                    for src, to in ((g.factor, factor), (g.decay, decay)):
                        sp.dma_start(to[b][:], src[:, bass.ds(n * V, V)].unsqueeze(0).to_broadcast([F + 1, 4, V])).then_inc(loaded[b], 16)

                for b in two:
                    load(b, b)
                with sp.Fori(1, o.pairs) as i:
                    for b in two:
                        sp.wait_ge(scanned, i * 2 + (b - 1))
                        load(i * 2 + b, b)

            @block.vector
            def _(dve):
                ch = Chain(dve, steps)
                ch.step(nc.vector.memset(run[1][:], 0.0))
                with dve.Fori(0, o.pairs) as i:
                    ch.restart()
                    for b in two:
                        n = i * 2 + b
                        dve.wait_ge(loaded[b], i * 48 + 48)
                        ch.step(nc.vector.tensor_mul(raw[b][:], raw[b][:], factor[b][:]))
                        dve.wait_ge(turned, i * 2 + 1)
                        for h in range(4):
                            ins = nc.vector.tensor_tensor_scan(run[b][:, h, :], decay[b][:, h, :], raw[b][:, h, :],
                                                               run[1 - b][:, h, V - 1:V], ALU.mult, ALU.add)
                            ch.step(ins)
                        dve.sem_inc(scanned, 1)

            @block.tensor
            def _(pe):
                pe.sem_inc(turned, 1)
                with pe.Fori(0, o.pairs) as i:
                    for b in two:
                        n = i * 2 + b
                        pe.wait_ge(scanned, n + 1)
                        pe.wait_ge(copied, n + 1)
                        pe.sem_inc(seen, 1)
                        for q in range(parts):
                            for h in range(4):
                                last = nc.tensor.transpose(ps_rows[:, q, h * (F + 1):(h + 1) * (F + 1)],
                                                           run[b][:, h, q * P:(q + 1) * P], g.ident[0:F + 1, 0:F + 1])
                        last.then_inc(turned, 1)

            @block.scalar
            def _(act):
                act.sem_inc(copied, 1)
                for b in two:
                    act.sem_inc(out[b], 16)
                with act.Fori(0, o.pairs) as i:
                    for b in two:
                        n = i * 2 + b
                        act.wait_ge(turned, n + 2)
                        act.wait_ge(out[b], i * 16 + 16)
                        nc.scalar.copy(rows[b][:], ps_rows[:, :, 0:W]).then_inc(copied, 1)
                        act.wait_ge(copied, n + 2)
                        act.dma_start(g.att_sums[bass.ds(n * V, V), :].rearrange("(q p) w -> p q w", p=P), rows[b][:]).then_inc(out[b], 16)
                for b in two:
                    act.wait_ge(out[b], 16 * o.pairs + 16)


def stage_attention_mean(nc, g, got, normed):
    with ExitStack() as c:
        weight = c.enter_context(nc.sbuf_tensor("am_weight", [P, NB, 4], F32))
        steps = new_sem(nc, c, "am_steps")
        with nc.Block() as block:
            @block.vector
            def _(dve):
                ch = Chain(dve, steps)
                v = got[:].rearrange("p b (h f) -> p b h f", f=F + 1)
                ch.step(nc.vector.tensor_scalar(weight[:], v[:, :, :, F], 1e-30, None, ALU.max))
                ch.step(nc.vector.reciprocal(weight[:], weight[:]))
                ch.step(nc.vector.tensor_mul(normed[:].rearrange("p b (h f) -> p b h f", f=F), v[:, :, :, 0:F],
                                             weight[:].unsqueeze(3).to_broadcast([P, NB, 4, F])))



class Spline:
    K = 125

    def __init__(self, nc, c, g, name, fin, fout, sums, stored=None, near=None):
        o = g.R
        self.nc, self.g, self.o, self.fin, self.fout, self.sums = nc, g, o, fin, fout, sums
        self.stored, self.near = stored, near
        self.C8, self.V = o.per_tile, o.vb
        self.parts = self.V // P
        self.XT = 4 if fin > 1 else TB
        self.XS = TB // self.XT
        self.HT = TB // 2
        self.bufs = 2 if near is not None else 1
        width = fin + 3 if near is not None else fin
        sb = lambda nm, shape, dt=F32: c.enter_context(nc.sbuf_tensor(f"{name}_{nm}", shape, dt))
        ps = lambda nm, shape: c.enter_context(nc.psum_tensor(f"{name}_{nm}", shape, F32))
        sem = lambda nm: new_sem(nc, c, f"{name}_{nm}")
        K, C8, V = self.K, self.C8, self.V
        self.w = sb("w", [K, fin, fout])
        self.rec = [sb(f"rec{b}", [P, TB, o.words], I32) for b in range(self.bufs)]
        self.far = [sb(f"far{b}", [P, TB, width]) for b in range(self.bufs)]
        self.shift = [sb(f"shift{b}", [C8, TB, 3]) for b in range(self.bufs)] if near is not None else []
        self.keep = sb("keep", [fout, V])
        self.pos = sb("pos", [P, TB, 3])
        self.up, self.down = sb("up", [P, TB * 3, 5]), sb("down", [P, TB * 3, 5])
        self.pair = sb("pair", [P, TB, 25])
        self.basis = [sb(f"basis{k}", [P, self.HT, K]) for k in range(2)]
        self.lows, self.highs, self.floor, self.roof = (sb(n, [P, 5]) for n in ("lows", "highs", "floor", "roof"))
        self.spread_to = [sb(f"spread{k}", [P, self.XT, fin, C8]) for k in range(2)]
        self.outer = sb("outer", [K, fin, V])
        self.run, self.carry = sb("run", [fout, V]), sb("carry", [fout, 1])
        self.rows = sb("rows", [P, self.parts, fout])
        if fin > 1:
            self.ps_outer = [ps(f"ps_outer{k}", [K, fin, C8]) for k in range(3)]
        else:
            self.ps_outer = [ps("ps_outer", [K, fin, V])]
        self.ps_out = ps("ps_out", [fout, V])
        self.ps_rows = ps("ps_rows", [P, self.parts, fout])
        if near is not None:
            self.ps_shift = ps("ps_shift", [P, TB, 3])
            self.gathered = [rows_sem(nc, f"{name}_gathered{b}") for b in range(2)]
        self.loaded = [sem(f"loaded{b}") for b in range(self.bufs)]
        self.loads = 16 * (1 + (stored is not None) + (near is not None))
        self.const, self.keep_in, self.out = sem("const"), sem("keep_in"), sem("out")
        self.shifts, self.positions, self.bases, self.spreads = sem("shifts"), sem("positions"), sem("bases"), sem("spreads")
        self.products, self.outers, self.made, self.scanned = sem("products"), sem("outers"), sem("made"), sem("scanned")
        self.turned, self.copied, self.seen = sem("turned"), sem("copied"), sem("seen")
        self.rec_v = o.rec.rearrange("(p t) w -> p t w", p=P)
        self.keep_v = o.keep.rearrange("(a v) -> a v", a=1)


    def begin_sync(self, sp, weights):
        sp.dma_start(self.w[:], weights).then_inc(self.const, 16)

    def load(self, sp, m, b):
        sp.dma_start(self.rec[b][:], self.rec_v[:, bass.ds(m * TB, TB), :]).then_inc(self.loaded[b], 16)
        if self.stored is not None:
            sp.dma_start(self.far[b][:], self.stored[:, bass.ds(m * TB, TB), :]).then_inc(self.loaded[b], 16)
        if self.near is not None:
            sp.dma_start(self.shift[b][:], self.near[bass.ds(m * self.V, self.V), :].rearrange("(t c) d -> c t d", c=self.C8)).then_inc(self.loaded[b], 16)


    def begin_vector(self, dve, ch):
        nc = self.nc
        ends = 3.0e38
        for k, (lo, hi) in enumerate(((ends, 0.0), (-ends, 0.0), (0.0, 0.0), (0.0, -ends), (0.0, ends))):
            nc.vector.memset(self.lows[:, k:k + 1], float(k - 1))
            nc.vector.memset(self.highs[:, k:k + 1], float(k + 1))
            nc.vector.memset(self.floor[:, k:k + 1], lo)
            nc.vector.memset(self.roof[:, k:k + 1], hi)
        ch.step(nc.vector.memset(self.carry[:], 0.0))
        dve.sem_inc(self.scanned, 1)
        dve.sem_inc(self.positions, 1)
        dve.sem_inc(self.spreads, 1)

    def points(self, dve, ch, m, b, turn):
        nc, far = self.nc, self.far[b]
        dve.wait_ge(self.loaded[b], turn * self.loads + self.loads)
        pseudo = self.rec[b][:, :, 1:4].bitcast(F32)
        if self.near is not None:
            dve.wait_ge(self.shifts, m + 1)
            dve.wait_ge(self.gathered[b], turn * (16 * TB) + 16 * TB)
            ch.step(nc.vector.tensor_add(self.pos[:], pseudo, far[:, :, self.fin:self.fin + 3]))
            nc.vector.tensor_sub(self.pos[:], self.pos[:], self.ps_shift[:]).then_inc(self.positions, 1)
            dve.wait_ge(self.positions, m + 2)
            ch.step(nc.vector.tensor_scalar(self.pos[:], self.pos[:], 0.0, 1.0, ALU.max, ALU.min))
            ch.step(nc.vector.tensor_scalar(self.pos[:], self.pos[:], 4.0, None, ALU.mult))
        else:
            ch.step(nc.vector.tensor_scalar(self.pos[:], pseudo, 4.0, None, ALU.mult))
        b5, b55, b255 = [P, TB * 3, 5], [P, TB, 5, 5], [P, self.HT, 25, 5]
        wide = lambda ap: ap.unsqueeze(1).to_broadcast(b5)
        x = self.pos[:].rearrange("p t d -> p (t d)").unsqueeze(2).to_broadcast(b5)
        up, down = self.up, self.down
        ch.step(nc.vector.tensor_sub(up[:], x, wide(self.lows[:])))
        ch.step(nc.vector.tensor_tensor(up[:], up[:], wide(self.floor[:]), ALU.max))
        ch.step(nc.vector.tensor_sub(down[:], wide(self.highs[:]), x))
        ch.step(nc.vector.tensor_tensor(down[:], down[:], wide(self.roof[:]), ALU.max))
        ch.step(nc.vector.tensor_tensor(up[:], up[:], down[:], ALU.min))
        v = up[:].rearrange("p (t d) k -> p t d k", d=3)
        ch.step(nc.vector.tensor_mul(self.pair[:].rearrange("p t (a b) -> p t a b", a=5),
                                     v[:, :, 0, :].unsqueeze(3).to_broadcast(b55), v[:, :, 1, :].unsqueeze(2).to_broadcast(b55)))
        dve.wait_ge(self.products, m * TB + 1)
        for k in range(2):
            ts = slice(k * self.HT, (k + 1) * self.HT)
            nc.vector.tensor_mul(self.basis[k][:].rearrange("p t (a b) -> p t a b", b=5),
                                 self.pair[:, ts, :].unsqueeze(3).to_broadcast(b255),
                                 v[:, ts, 2, :].unsqueeze(2).to_broadcast(b255)).then_inc(self.bases, 1)
        if self.fin == 1:
            ch.step(nc.vector.tensor_scalar(far[:, :, 0], self.rec[b][:, :, 0], float(N), None, ALU.is_lt))

    def spread(self, dve, m, b, steps):
        nc = self.nc
        bx = [P, self.XT, self.fin, self.C8]
        for s in steps:
            if s >= 2:
                dve.wait_ge(self.products, m * TB + ((s - 1) * self.XT + 1))
            nc.vector.tensor_mul(self.spread_to[s % 2][:], self.far[b][:, s * self.XT:(s + 1) * self.XT, 0:self.fin].unsqueeze(3).to_broadcast(bx),
                                 self.o.mask[:].unsqueeze(1).unsqueeze(1).to_broadcast(bx)).then_inc(self.spreads, 1)

    def scan(self, dve, ch, m):
        nc = self.nc
        dve.wait_ge(self.made, m + 2)
        dve.wait_ge(self.keep_in, m * 16 + 16)
        dve.wait_ge(self.turned, m + 1)
        nc.vector.tensor_tensor_scan(self.run[:], self.keep[:], self.ps_out[:], self.carry[:], ALU.mult, ALU.add).then_inc(self.scanned, 1)
        dve.wait_ge(self.scanned, m + 2)
        ch.step(nc.vector.tensor_copy(self.carry[:], self.run[:, self.V - 1:self.V]))


    def begin_tensor(self, pe):
        pe.wait_ge(self.const, 16)
        pe.sem_inc(self.products, 1)
        pe.sem_inc(self.made, 1)
        pe.sem_inc(self.turned, 1)

    def near_shifts(self, pe, m, b, turn):
        pe.wait_ge(self.loaded[b], turn * self.loads + self.loads)
        pe.wait_ge(self.positions, m + 1)
        self.nc.tensor.matmul(self.ps_shift[:].rearrange("p t d -> p (t d)"), self.o.mask_t[:],
                              self.shift[b][:].rearrange("c t d -> c (t d)"), start=True, stop=True).then_inc(self.shifts, 1)

    def outer_products(self, pe, m):
        ring = len(self.ps_outer)
        for t in range(TB):
            if t % self.HT == 0:
                pe.wait_ge(self.bases, m * 2 + (t // self.HT + 1))
            if t % self.XT == 0:
                pe.wait_ge(self.spreads, m * self.XS + (t // self.XT + 2))
            if self.fin == 1:
                if t == 0:
                    pe.wait_ge(self.outers, m + 1)
                to = self.ps_outer[0][:, 0, t * self.C8:(t + 1) * self.C8]
            else:
                if t >= ring:
                    pe.wait_ge(self.outers, m * TB + (t - ring + 2))
                to = self.ps_outer[t % ring][:].rearrange("k f c -> k (f c)")
            self.nc.tensor.matmul(to, self.basis[t // self.HT][:, t % self.HT, :],
                                  self.spread_to[(t // self.XT) % 2][:, t % self.XT, :, :].rearrange("p f c -> p (f c)"),
                                  start=True, stop=True).then_inc(self.products, 1)

    def through_weights(self, pe, m):
        pe.wait_ge(self.outers, m + 2 if self.fin == 1 else m * TB + (TB + 1))
        pe.wait_ge(self.scanned, m + 1)
        for f in range(self.fin):
            last = self.nc.tensor.matmul(self.ps_out[:], self.w[:, f, :], self.outer[:, f, :], start=(f == 0), stop=(f == self.fin - 1))
        last.then_inc(self.made, 1)

    def turn(self, pe, m):
        pe.wait_ge(self.scanned, m + 2)
        pe.wait_ge(self.copied, m + 1)
        pe.sem_inc(self.seen, 1)
        for q in range(self.parts):
            last = self.nc.tensor.transpose(self.ps_rows[:, q, :], self.run[:, q * P:(q + 1) * P], self.g.ident[0:self.fout, 0:self.fout])
        last.then_inc(self.turned, 1)


    def load_marks(self, act, m):
        act.dma_start(self.keep[:], self.keep_v[:, bass.ds(m * self.V, self.V)].to_broadcast([self.fout, self.V])).then_inc(self.keep_in, 16)

    def begin_scalar(self, act):
        self.load_marks(act, 0)
        act.sem_inc(self.outers, 1)
        act.sem_inc(self.copied, 1)
        act.sem_inc(self.out, 16)

    def copy_products(self, act, m):
        act.wait_ge(self.made, m + 1)
        if self.fin == 1:
            act.wait_ge(self.products, m * TB + (TB + 1))
            self.nc.scalar.copy(self.outer[:], self.ps_outer[0][:]).then_inc(self.outers, 1)
            return
        for t in range(TB):
            act.wait_ge(self.products, m * TB + (t + 2))
            self.nc.scalar.copy(self.outer[:, :, t * self.C8:(t + 1) * self.C8], self.ps_outer[t % len(self.ps_outer)][:]).then_inc(self.outers, 1)

    def store_rows(self, act, m):
        act.wait_ge(self.turned, m + 2)
        act.wait_ge(self.out, m * 16 + 16)
        self.nc.scalar.copy(self.rows[:], self.ps_rows[:]).then_inc(self.copied, 1)
        act.wait_ge(self.copied, m + 2)
        act.dma_start(self.sums[bass.ds(m * self.V, self.V), :].rearrange("(q p) w -> p q w", p=P), self.rows[:]).then_inc(self.out, 16)
        self.load_marks(act, m + 1)

    def end_scalar(self, act):
        act.wait_ge(self.out, 16 * self.o.blocks + 16)
        act.wait_ge(self.keep_in, 16 * self.o.blocks + 16)


def stage_spline_ones(nc, g, name, weights, fout, sums):
    with ExitStack() as c:
        sl = Spline(nc, c, g, name, 1, fout, sums)
        steps = new_sem(nc, c, f"{name}_steps")
        blocks = g.R.blocks
        with nc.Block() as block:
            @block.sync
            def _(sp):
                sl.begin_sync(sp, weights)
                sl.load(sp, 0, 0)
                with sp.Fori(1, blocks) as m:
                    sp.wait_ge(sl.spreads, m + 1)
                    sl.load(sp, m, 0)

            @block.vector
            def _(dve):
                ch = Chain(dve, steps)
                sl.begin_vector(dve, ch)
                sl.points(dve, ch, 0, 0, 0)
                sl.spread(dve, 0, 0, [0])
                with dve.Fori(1, blocks) as m:
                    ch.restart()
                    sl.points(dve, ch, m, 0, m)
                    sl.spread(dve, m, 0, [0])
                    sl.scan(dve, ch, m - 1)
                ch.restart()
                sl.scan(dve, ch, blocks - 1)

            @block.tensor
            def _(pe):
                sl.begin_tensor(pe)
                with pe.Fori(0, blocks) as m:
                    sl.outer_products(pe, m)
                    sl.through_weights(pe, m)
                    sl.turn(pe, m)

            @block.scalar
            def _(act):
                sl.begin_scalar(act)
                with act.Fori(0, blocks) as m:
                    sl.copy_products(act, m)
                    sl.store_rows(act, m)
                sl.end_scalar(act)


def stage_spline_gathered(nc, g, name, weights, fin, fout, sums, table, near):
    with ExitStack() as c:
        sl = Spline(nc, c, g, name, fin, fout, sums, near=near)
        steps, taken = new_sem(nc, c, f"{name}_steps"), new_sem(nc, c, f"{name}_taken")
        o, two = g.R, range(2)
        with nc.Block() as block:
            @block.sync
            def _(sp):
                sl.begin_sync(sp, weights)
                for b in two:
                    sl.load(sp, b, b)
                with sp.Fori(1, o.pairs) as i:
                    for b in two:
                        sp.wait_ge(sl.spreads, i * (2 * sl.XS) + ((b - 1) * sl.XS + 1))
                        sl.load(sp, i * 2 + b, b)

            @block.gpsimd
            def _(pool):
                with pool.Fori(0, o.pairs) as i:
                    for b in two:
                        pool.wait_ge(sl.loaded[b], i * sl.loads + sl.loads)
                        pool.sem_inc(taken, 1)
                        for t in range(TB):
                            pool.indirect_dma_start(out=sl.far[b][:, t, :], out_offset=None, in_=table[:, :],
                                                    in_offset=bass.IndirectOffsetOnAxis(ap=sl.rec[b][:, t, 0:1], axis=0)).then_inc(sl.gathered[b], 16)

            @block.vector
            def _(dve):
                ch = Chain(dve, steps)
                first, rest = range(2), range(2, sl.XS)
                sl.begin_vector(dve, ch)
                sl.points(dve, ch, 0, 0, 0)
                sl.spread(dve, 0, 0, range(sl.XS))
                sl.points(dve, ch, 1, 1, 0)
                sl.spread(dve, 1, 1, first)
                sl.scan(dve, ch, 0)
                sl.spread(dve, 1, 1, rest)
                with dve.Fori(1, o.pairs) as i:
                    ch.restart()
                    for b in two:
                        n = i * 2 + b
                        sl.points(dve, ch, n, b, i)
                        sl.spread(dve, n, b, first)
                        sl.scan(dve, ch, i * 2 + (b - 1))
                        sl.spread(dve, n, b, rest)
                ch.restart()
                sl.scan(dve, ch, o.blocks - 1)

            @block.tensor
            def _(pe):
                sl.begin_tensor(pe)
                sl.near_shifts(pe, 0, 0, 0)
                sl.outer_products(pe, 0)
                sl.near_shifts(pe, 1, 1, 0)
                sl.through_weights(pe, 0)
                sl.turn(pe, 0)
                with pe.Fori(0, o.pairs - 1) as i:
                    for b in two:
                        sl.outer_products(pe, i * 2 + (b + 1))
                        sl.near_shifts(pe, i * 2 + (b + 2), b, i + 1)
                        sl.through_weights(pe, i * 2 + (b + 1))
                        sl.turn(pe, i * 2 + (b + 1))
                sl.outer_products(pe, o.blocks - 1)
                sl.through_weights(pe, o.blocks - 1)
                sl.turn(pe, o.blocks - 1)

            @block.scalar
            def _(act):
                sl.begin_scalar(act)
                with act.Fori(0, o.blocks) as n:
                    sl.copy_products(act, n)
                    sl.store_rows(act, n)
                sl.end_scalar(act)



def stage_aggregate(nc, g, name, table, sums, gauss=None, sl=None, sl_from=0, sl_count=0, sl_weights=None):
    o = g.D
    Q = QUARTERS
    GT = TB // Q
    V = GT * o.per_tile
    parts = V // P
    width = 3 * F if gauss is not None else F
    per = o.tiles // Q
    with ExitStack() as c:
        sb = lambda nm, shape, dt=F32: c.enter_context(nc.sbuf_tensor(f"{name}_{nm}", shape, dt))
        ps = lambda nm, shape: c.enter_context(nc.psum_tensor(f"{name}_{nm}", shape, F32))
        sem = lambda nm: new_sem(nc, c, f"{name}_{nm}")
        two = range(2)
        rec = [sb(f"rec{b}", [P, Q, GT, o.words], I32) for b in two]
        keep = [sb(f"keep{b}", [Q * F, V]) for b in two]
        got = [sb(f"got{b}", [P, GT, Q, width]) for b in two]
        mixed = [sb(f"mixed{b}", [P, GT, Q, F]) for b in two] if gauss is not None else got
        run = [sb(f"run{b}", [Q * F, V]) for b in two]
        rows = [sb(f"rows{b}", [P, parts, Q * F]) for b in two]
        ps_sum = [ps(f"ps_sum{b}", [Q * F, V]) for b in two]
        ps_rows = ps("ps_rows", [P, parts, Q * F])
        loaded, out = ([sem(f"{n}{b}") for b in two] for n in ("loaded", "out"))
        gathered = [rows_sem(nc, f"{name}_gathered{b}") for b in two]
        steps, taken, seen = sem("steps"), sem("taken"), sem("seen")
        mixes, summed, scanned, turned, copied = (sem(n) for n in ("mixes", "summed", "scanned", "turned", "copied"))
        rec_v = o.rec.rearrange("(p q t) w -> p q t w", p=P, q=Q)
        loads = 16 * (1 + Q)
        with nc.Block() as block:
            @block.sync
            def _(sp):
                def load(n, b):
                    sp.dma_start(rec[b][:].rearrange("p q t w -> p q (t w)"),
                                 rec_v[:, :, bass.ds(n * GT, GT), :].rearrange("p q t w -> p q (t w)")).then_inc(loaded[b], 16)
                    for q in range(Q):
                        marks = o.keep[bass.ds(n * V + q * (o.chunks // Q), V)]
                        sp.dma_start(keep[b][q * F:(q + 1) * F, :], marks.rearrange("(a v) -> a v", a=1).to_broadcast([F, V])).then_inc(loaded[b], 16)

                def next_pair(i):
                    for b in two:
                        sp.wait_ge(scanned, i * 2 + b)
                        load(i * 2 + b, b)

                for b in two:
                    load(b, b)
                if sl_count:
                    if sl_from == 0:
                        sl.begin_sync(sp, sl_weights)
                        sl.load(sp, 0, 0)
                    else:
                        sl.load(sp, sl_from, 0)
                    with sp.Fori(1, sl_count) as i:
                        sp.wait_ge(sl.spreads, i * sl.XS + (sl_from * sl.XS + 1))
                        sl.load(sp, i + sl_from, 0)
                        next_pair(i)
                if max(sl_count, 1) < o.pairs:
                    with sp.Fori(max(sl_count, 1), o.pairs) as i:
                        next_pair(i)

            @block.gpsimd
            def _(pool):
                with pool.Fori(0, o.pairs) as i:
                    for b in two:
                        pool.wait_ge(loaded[b], i * loads + loads)
                        pool.sem_inc(taken, 1)
                        for t in range(GT):
                            for q in range(Q):
                                pool.indirect_dma_start(out=got[b][:, t, q, :], out_offset=None, in_=table[:, :],
                                                        in_offset=bass.IndirectOffsetOnAxis(ap=rec[b][:, q, t, 0:1], axis=0)).then_inc(gathered[b], 16)

            @block.tensor
            def _(pe):
                def products(i, b):
                    if gauss is not None:
                        pe.wait_ge(mixes, i * 2 + (b + 1))
                    else:
                        pe.wait_ge(gathered[b], i * (16 * TB) + 16 * TB)
                    pe.wait_ge(scanned, i * 2 + 1)
                    for t in range(GT):
                        last = nc.tensor.matmul(ps_sum[b][:, t * o.per_tile:(t + 1) * o.per_tile],
                                                mixed[b][:, t, :, :].rearrange("p q f -> p (q f)"), o.mask[:], start=True, stop=True)
                    last.then_inc(summed, 1)

                def transposes(i, b):
                    pe.wait_ge(scanned, i * 2 + (b + 2))
                    pe.wait_ge(copied, i * 2 + (b + 1))
                    pe.sem_inc(seen, 1)
                    for k in range(parts):
                        last = nc.tensor.transpose(ps_rows[:, k, :], run[b][:, k * P:(k + 1) * P], g.ident[:])
                    last.then_inc(turned, 1)

                pe.sem_inc(turned, 1)
                if sl_count:
                    if sl_from == 0:
                        sl.begin_tensor(pe)
                    with pe.Fori(0, sl_count) as i:
                        sl.outer_products(pe, i + sl_from)
                        products(i, 0)
                        sl.through_weights(pe, i + sl_from)
                        transposes(i, 0)
                        sl.turn(pe, i + sl_from)
                        products(i, 1)
                        transposes(i, 1)
                if sl_count < o.pairs:
                    with pe.Fori(sl_count, o.pairs) as i:
                        for b in two:
                            products(i, b)
                            transposes(i, b)

            @block.vector
            def _(dve):
                ch = Chain(dve, steps)

                def sums_of(i, b):
                    if gauss is not None:
                        dve.wait_ge(gathered[b], i * (16 * TB) + 16 * TB)
                        rows3 = got[b][:].rearrange("p t q (k f) -> p (t q) k f", k=3)
                        by = gauss[:, bass.ds(i * (2 * GT) + b * GT, GT), :, :].rearrange("p t q k -> p (t q) k")
                        ch.step(nc.vector.tensor_mul(rows3, rows3, by.unsqueeze(3).to_broadcast([P, TB, 3, F])))
                        to = mixed[b][:].rearrange("p t q f -> p (t q) f")
                        ch.step(nc.vector.tensor_add(to, rows3[:, :, 0, :], rows3[:, :, 1, :]))
                        nc.vector.tensor_add(to, to, rows3[:, :, 2, :]).then_inc(mixes, 1)
                    dve.wait_ge(summed, i * 2 + (b + 1))
                    dve.wait_ge(loaded[b], i * loads + loads)
                    dve.wait_ge(turned, i * 2 + 1)
                    nc.vector.tensor_tensor_scan(run[b][:], keep[b][:], ps_sum[b][:], run[1 - b][:, V - 1:V],
                                                 ALU.mult, ALU.add).then_inc(scanned, 1)
                    dve.wait_ge(scanned, i * 2 + (b + 2))

                ch.step(nc.vector.memset(run[1][:], 0.0))
                dve.sem_inc(scanned, 1)
                if sl_count:
                    first, rest = range(2), range(2, sl.XS)
                    if sl_from == 0:
                        sl.begin_vector(dve, ch)
                    sl.points(dve, ch, sl_from, 0, sl_from)
                    sl.spread(dve, sl_from, 0, range(sl.XS))
                    sums_of(0, 0)
                    with dve.Fori(1, sl_count) as i:
                        ch.restart()
                        m = i + sl_from
                        sl.points(dve, ch, m, 0, m)
                        sl.spread(dve, m, 0, first)
                        sl.scan(dve, ch, i + (sl_from - 1))
                        sums_of(i - 1, 1)
                        sl.spread(dve, m, 0, rest)
                        sums_of(i, 0)
                    ch.restart()
                    sl.scan(dve, ch, sl_from + sl_count - 1)
                    sums_of(sl_count - 1, 1)
                if sl_count < o.pairs:
                    with dve.Fori(sl_count, o.pairs) as i:
                        ch.restart()
                        for b in two:
                            sums_of(i, b)

            @block.scalar
            def _(act):
                def store(i, b):
                    act.wait_ge(turned, i * 2 + (b + 2))
                    act.wait_ge(out[b], i * 16 + 16)
                    nc.scalar.copy(rows[b][:], ps_rows[:]).then_inc(copied, 1)
                    act.wait_ge(copied, i * 2 + (b + 2))
                    act.dma_start(sums.rearrange("(v q) f -> v (q f)", q=Q)[bass.ds(i * (2 * V) + b * V, V), :]
                                  .rearrange("(k p) w -> p k w", p=P), rows[b][:]).then_inc(out[b], 16)

                act.sem_inc(copied, 1)
                for b in two:
                    act.sem_inc(out[b], 16)
                if sl_count:
                    if sl_from == 0:
                        sl.begin_scalar(act)
                    with act.Fori(0, sl_count) as i:
                        sl.copy_products(act, i + sl_from)
                        store(i, 0)
                        sl.store_rows(act, i + sl_from)
                        store(i, 1)
                if sl_count < o.pairs:
                    with act.Fori(sl_count, o.pairs) as i:
                        for b in two:
                            store(i, b)
                for b in two:
                    act.wait_ge(out[b], 16 * o.pairs + 16)
                if sl_count and sl_from + sl_count == g.R.blocks:
                    sl.end_scalar(act)



def stage_nodes(nc, g, name, biases, work, stores=()):
    with ExitStack() as c:
        sb = lambda nm, shape: c.enter_context(nc.sbuf_tensor(f"{name}_{nm}", shape, F32))
        sem = lambda nm: new_sem(nc, c, f"{name}_{nm}")
        rows = [sb(f"bias{k}", [P, view.shape[0]]) for k, view in enumerate(biases)]
        t = NormBuffers(nc, c, name)
        loaded, steps, finished, stored, act_in, act_out = (
            sem(n) for n in ("loaded", "steps", "finished", "stored", "act_in", "act_out"))
        calls = []

        with nc.Block() as block:
            @block.sync
            def _(sp):
                for to, view in zip(rows, biases):
                    sp.dma_start(to[:], view.unsqueeze(0).to_broadcast([P, view.shape[0]])).then_inc(loaded, 16)
                sp.wait_ge(finished, 1)
                for table, tile in stores:
                    sp.dma_start(table, tile).then_inc(stored, 16)
                if stores:
                    sp.wait_ge(stored, 16 * len(stores))

            @block.vector
            def _(dve):
                ch = Chain(dve, steps)
                if biases:
                    dve.wait_ge(loaded, 16 * len(biases))

                def act_in_place(ap, func):
                    calls.append((ap, func))
                    dve.sem_inc(act_in, 1)
                    dve.wait_ge(act_out, len(calls))

                work(ch, rows, act_in_place, t)
                dve.sem_inc(finished, 1)

            @block.scalar
            def _(act):
                for k, (ap, func) in enumerate(calls):
                    act.wait_ge(act_in, k + 1)
                    nc.scalar.activation(ap, ap, func).then_inc(act_out, 1)


def layers(nc, g, ins, out):
    bc = lambda ap, width: ap.unsqueeze(1).to_broadcast([P, NB, width])
    per_node = lambda ap, width: ap.unsqueeze(2).to_broadcast([P, NB, width])

    def elu(ch, act, to, tmp):
        ch.step(nc.vector.tensor_scalar(tmp, to, 0.0, None, ALU.min))
        act(tmp, ACT.Exp)
        ch.step(nc.vector.tensor_scalar(tmp, tmp, -1.0, None, ALU.add))
        ch.step(nc.vector.scalar_tensor_tensor(to, to, 0.0, tmp, ALU.max, ALU.add))

    def scope():
        c = ExitStack()
        return c, (lambda name, shape: c.enter_context(nc.sbuf_tensor(name, shape, F32)))

    stage_chunks(nc, g)

    def spline_mean(ch, to, bias, width):
        ch.step(nc.vector.tensor_mul(to, to, per_node(g.R.inv_degree[:], width)))
        ch.step(nc.vector.tensor_add(to, to, bc(bias, width)))

    c, sb = scope()
    with c:
        g.spline_h, tmp = sb("l3_h1", [P, NB, 64]), sb("l3_tmp1", [P, NB, 64])
        stage_spline_ones(nc, g, "p_1", ins["L3_gnn_stn1_w"], 64, g.sums_r64)
        stage_collect(nc, g, "c_p1", g.R, g.sums_r64, 64, g.spline_h)

        def work(ch, rows, act, t):
            spline_mean(ch, g.spline_h[:], rows[0][:], 64)
            elu(ch, act, g.spline_h[:], tmp[:])
            ch.step(nc.vector.tensor_mul(g.spline_h[:], g.spline_h[:], per_node(g.valid[:], 64)))

        stage_nodes(nc, g, "n_p1", [ins["L3_gnn_stn1_b"]], work)

        stage_attention_inputs(nc, g, ins)
        stage_nodes(nc, g, "n_in", [], lambda ch, rows, act, t: layernorm(ch, nc, g, t, g.h[:], act))
        stage_dense(nc, g, "d_att", g.h, F, g.att_w[:], 8, g.att, [])
        stage_attention_tables(nc, g, ins)
        stage_spread(nc, g, "s_near", g.near_table, 4, g.near_chunk)
    stage_attention(nc, g)
    stage_attention_factors(nc, g)
    stage_attention_join(nc, g)
    c, sb = scope()
    with c:
        got, normed, w, mean = sb("l0_got", [P, NB, 4 * (F + 1)]), sb("l0_normed", [P, NB, 4 * F]), sb("l0_w", [4 * F, F]), sb("l0_mean", [P, NB, F])
        stage_collect(nc, g, "c_att", g.R, g.att_sums, 4 * (F + 1), got)
        stage_attention_mean(nc, g, got, normed)
        stage_dense(nc, g, "d_l0", normed, 4 * F, w[:], F, mean, [(w[:], ins["L0_gnn_w"].rearrange("h f o -> (h f) o"))])

        def work(ch, rows, act, t):
            ch.step(nc.vector.scalar_tensor_tensor(g.x[:], mean[:], 0.25, g.x[:], ALU.mult, ALU.add))
            ch.step(nc.vector.tensor_add(g.x[:], g.x[:], bc(rows[0][:], F)))
            layernorm(ch, nc, g, t, g.h[:], act)

        stage_nodes(nc, g, "n_l0", [ins["L0_gnn_bias"]], work, [(node_rows(g.table_32), g.h[:])])

    cs = ExitStack()
    with cs:
        sl = Spline(nc, cs, g, "p_2", 64, 64, g.sums_r64, stored=g.far_64)
        beside = [min(g.D.pairs, g.R.blocks - k * g.D.pairs) for k in range(3)]
        assert sum(beside) == g.R.blocks and min(beside) > 0
        stage_aggregate(nc, g, "g_l1", g.table_32, g.sums_d, sl=sl, sl_from=0, sl_count=beside[0], sl_weights=ins["L3_gnn_stn2_w"])
        c, sb = scope()
        with c:
            got, hid, both = sb("l1_got", [P, NB, F]), sb("l1_hid", [P, NB, 64]), sb("l1_both", [P, NB, 64])
            c2, sb2 = scope()
            with c2:
                cat, w1, w2, y = sb2("l1_cat", [P, NB, 2 * F]), sb2("l1_w1", [64, 64]), sb2("l1_w2", [64, 64]), sb2("l1_y", [P, NB, F])
                stage_collect_quarters(nc, g, "c_l1", g.sums_d, got)

                def work(ch, rows, act, t):
                    ch.step(nc.vector.tensor_mul(cat[:, :, 0:F], got[:], per_node(g.D.inv_degree[:], F)))
                    ch.step(nc.vector.tensor_copy(cat[:, :, F:2 * F], g.h[:]))

                stage_nodes(nc, g, "n_l1a", [], work)
                stage_dense(nc, g, "d_l1a", cat, 64, w1[:], 64, hid, [(w1[0:F, :], ins["L1_gnn_W1_l"]), (w1[F:2 * F, :], ins["L1_gnn_W1_r"])])

                def work(ch, rows, act, t):
                    ch.step(nc.vector.tensor_add(hid[:], hid[:], bc(rows[0][:], 64)))
                    ch.step(nc.vector.tensor_scalar(hid[:], hid[:], 0.0, None, ALU.max))

                stage_nodes(nc, g, "n_l1b", [ins["L1_gnn_b1"]], work)
                stage_dense(nc, g, "d_l1b", hid, 64, w2[:], 64, both, [(w2[:, 0:F], ins["L1_gnn_W2_l"]), (w2[:, F:2 * F], ins["L1_gnn_W2_r"])])

                def work(ch, rows, act, t):
                    ch.step(nc.vector.tensor_mul(y[:], both[:, :, 0:F], per_node(g.valid[:], F)))

                stage_nodes(nc, g, "n_l1c", [], work, [(node_rows(g.table_32), y[:])])
            stage_aggregate(nc, g, "g_l1d", g.table_32, g.sums_d, sl=sl, sl_from=beside[0], sl_count=beside[1])
            stage_collect_quarters(nc, g, "c_l1d", g.sums_d, got)

            def work(ch, rows, act, t):
                ch.step(nc.vector.tensor_mul(got[:], got[:], per_node(g.D.inv_degree[:], F)))
                ch.step(nc.vector.tensor_add(got[:], got[:], bc(rows[0][:], F)))
                ch.step(nc.vector.tensor_add(got[:], got[:], both[:, :, F:2 * F]))
                ch.step(nc.vector.tensor_add(g.x[:], g.x[:], got[:]))
                layernorm(ch, nc, g, t, g.h[:], act)

            stage_nodes(nc, g, "n_l1d", [ins["L1_gnn_b2"]], work)

        c, sb = scope()
        with c:
            gauss = sb("l2_gauss", [P, g.D.tiles // QUARTERS, QUARTERS, 3])
            stage_gaussians(nc, g, ins["L2_gnn_mu"], ins["L2_gnn_sigma"], gauss)
            c2, sb2 = scope()
            with c2:
                three, w = sb2("l2_three", [P, NB, 3 * F]), sb2("l2_w", [F, 3 * F])
                stage_dense(nc, g, "d_l2", g.h, F, w[:], 3 * F, three, [(w[:], ins["L2_gnn_g"])])
                stage_nodes(nc, g, "n_l2", [], lambda ch, rows, act, t: None, [(node_rows(g.table_96), three[:])])
            stage_aggregate(nc, g, "g_l2", g.table_96, g.sums_d, gauss=gauss, sl=sl, sl_from=beside[0] + beside[1], sl_count=beside[2])
    c, sb = scope()
    with c:
        got, w, res = sb("l2_got", [P, NB, F]), sb("l2_w2", [F, F]), sb("l2_res", [P, NB, F])
        stage_collect_quarters(nc, g, "c_l2", g.sums_d, got)
        stage_dense(nc, g, "d_l2b", g.h, F, w[:], F, res, [(w[:], ins["L2_gnn_root"])])

        def work(ch, rows, act, t):
            ch.step(nc.vector.tensor_mul(got[:], got[:], per_node(g.D.inv_degree[:], F)))
            ch.step(nc.vector.tensor_add(got[:], got[:], res[:]))
            ch.step(nc.vector.tensor_add(got[:], got[:], bc(rows[0][:], F)))
            ch.step(nc.vector.tensor_add(g.x[:], g.x[:], got[:]))
            layernorm(ch, nc, g, t, g.h[:], act)

        stage_nodes(nc, g, "n_l2b", [ins["L2_gnn_bias"]], work)

    c, sb = scope()
    with c:
        hid = sb("l3_hid", [P, NB, 64])
        stage_collect(nc, g, "c_p2", g.R, g.sums_r64, 64, hid)
        c2, sb2 = scope()
        with c2:
            tmp, hid2, w3, w4 = sb2("l3_tmp2", [P, NB, 64]), sb2("l3_hid2", [P, NB, 64]), sb2("l3_w3", [64, 64]), sb2("l3_w4", [64, 3])
            t3, row = sb2("l3_t3", [P, NB, 3]), sb2("l3_row", [P, NB, F + 3])

            def work(ch, rows, act, t):
                spline_mean(ch, hid[:], rows[0][:], 64)
                elu(ch, act, hid[:], tmp[:])

            stage_nodes(nc, g, "n_p2", [ins["L3_gnn_stn2_b"]], work)
            stage_dense(nc, g, "d_p3", hid, 64, w3[:], 64, hid2, [(w3[:], ins["L3_gnn_stn3_w"])])

            def work(ch, rows, act, t):
                ch.step(nc.vector.tensor_add(hid2[:], hid2[:], bc(rows[0][:], 64)))
                elu(ch, act, hid2[:], tmp[:])

            stage_nodes(nc, g, "n_p3", [ins["L3_gnn_stn3_b"]], work)
            stage_dense(nc, g, "d_p4", hid2, 64, w4[:], 3, t3, [(w4[:], ins["L3_gnn_stn4_w"])])

            def work(ch, rows, act, t):
                ch.step(nc.vector.tensor_add(t3[:], t3[:], bc(rows[0][:], 3)))
                ch.step(nc.vector.tensor_copy(row[:, :, 0:F], g.h[:]))
                ch.step(nc.vector.tensor_copy(row[:, :, F:F + 3], t3[:]))

            stage_nodes(nc, g, "n_p4", [ins["L3_gnn_stn4_b"]], work, [(node_rows(g.table_35), row[:]), (node_rows(g.shift_table), t3[:])])
        stage_spread(nc, g, "s_shift", g.shift_table, 3, g.shift_chunk)
        stage_spline_gathered(nc, g, "p_3", ins["L3_gnn_conv_w"], F, F, g.sums_r32, g.table_35, g.shift_chunk)
        c2, sb2 = scope()
        with c2:
            got = sb2("l3_got", [P, NB, F])
            stage_collect(nc, g, "c_p3", g.R, g.sums_r32, F, got)

            def work(ch, rows, act, t):
                spline_mean(ch, got[:], rows[0][:], F)
                ch.step(nc.vector.tensor_add(got[:], got[:], g.x[:]))

            full = (NB - 1) * P
            stage_nodes(nc, g, "n_p5", [ins["L3_gnn_conv_b"]], work,
                        [(out[0:full, :].rearrange("(b p) f -> p b f", p=P), got[:, 0:NB - 1, :]),
                         (out[full:N, :], got[0:N - full, NB - 1, :])])


def build(nc, ins, out):
    g = Shared()
    g.R = Order("r", 16, 4, 19)
    g.D = Order("d", 4, 3, 15)
    g.orders = (g.R, g.D)
    with ExitStack() as c:
        dram = lambda name, shape, dt=F32: nc.dram_tensor(name, shape, dt, kind="Internal").ap()
        sb = lambda name, shape, dt=F32: c.enter_context(nc.sbuf_tensor(name, shape, dt))
        g.pad = {"src": dram("pad_src", [EP], I32), "dst": dram("pad_dst", [EP], I32),
                 "edge_attr_3": dram("pad_attr_3", [EP * 3]), "edge_attr_2": dram("pad_attr_2", [EP * 2])}
        for o, key, other, attr in ((g.R, "src", "dst", "edge_attr_3"), (g.D, "dst", "src", "edge_attr_2")):
            o.key, o.other, o.attr = key, other, attr
            o.rec = dram(f"rec_{o.name}", [o.slots, o.words], I32)
            o.first = dram(f"first_{o.name}", [o.chunks, 1])
            o.mask = sb(f"mask_{o.name}", [P, o.per_tile])
            o.slot0 = sb(f"slot0_{o.name}", [P, NH])
            o.last = sb(f"last_{o.name}", [P, NB], I32)
            o.inv_degree = sb(f"inv_degree_{o.name}", [P, NB])
        V = g.R.chunks
        for o in g.orders:
            o.keep = dram(f"keep_{o.name}", [o.chunks + o.vb])
        g.chunk_node, g.chunk_row = dram("chunk_node", [V], I32), sb("chunk_row", [P, V // P], I32)
        g.att_table, g.near_table, g.near_chunk = dram("att_table", [NP, FAR]), dram("near_table", [NP, 4]), dram("near_chunk", [V, 4])
        g.top, g.factor, g.decay = dram("top", [4, V]), dram("factor", [4, V]), dram("decay", [4, V])
        g.att_raw, g.att_sums = dram("att_raw", [F + 1, 4 * V]), dram("att_sums", [V, 4 * (F + 1)])
        g.table_32, g.table_35 = dram("table_32", [NP, F]), dram("table_35", [NP, F + 3])
        g.sums_d, g.table_96 = dram("sums_d", [g.D.chunks, F]), dram("table_96", [NP, 3 * F])
        g.far_64 = dram("far_64", [P, g.R.tiles, 64])
        g.sums_r64, g.sums_r32 = dram("sums_r64", [V, 64]), dram("sums_r32", [V, F])
        g.shift_table, g.shift_chunk = dram("shift_table", [NP, 3]), dram("shift_chunk", [V, 3])
        g.R.mask_t = sb("mask_t", [g.R.per_tile, P])
        g.iota_row, g.pidx = sb("iota_row", [P, P]), sb("pidx", [P, 1])
        g.ident, g.below, g.before = sb("ident", [P, P]), sb("below", [P, P]), sb("before", [P, P])
        g.ones, g.zero_bf = sb("ones", [P, P]), sb("zero_bf", [P, P], BF16)
        g.valid = sb("valid", [P, NB])
        g.crossing = sb("crossing", [P, QUARTERS - 1, NB])
        g.degree = {k: sb(f"degree_{k}", [P, NH]) for k in ("src", "dst")}
        stage_setup(nc, g, ins)
        with ExitStack() as cs:
            sbs = lambda name, shape, dt=F32: cs.enter_context(nc.sbuf_tensor(name, shape, dt))
            cols = STEPS * HB
            g.key_i = {k: sbs(f"key_i_{k}", [P, cols], I32) for k in ("src", "dst")}
            g.key_f = {k: sbs(f"key_f_{k}", [P, cols]) for k in ("src", "dst")}
            g.lo = {k: sbs(f"lo_{k}", [P, cols]) for k in ("src", "dst")}
            g.hi = {k: sbs(f"hi_{k}", [P, cols]) for k in ("src", "dst")}
            g.attr = {"edge_attr_3": sbs("attr_3", [P, cols * 3]), "edge_attr_2": sbs("attr_2", [P, cols * 2])}
            stage_histogram(nc, g)
            stage_starts(nc, g)
            for o in g.orders:
                stage_sort(nc, g, o)
        g.x, g.h = sb("x_nodes", [P, NB, F]), sb("h_nodes", [P, NB, F])
        g.att_w, g.att = sb("att_w", [F, 8]), sb("att", [P, NB, 8])
        layers(nc, g, ins, out)


_INS = ["x", "src", "dst", "edge_attr_2", "edge_attr_3", "L0_gnn_w", "L0_gnn_fc_w", "L0_gnn_fc_b", "L0_gnn_bias",
        "L1_gnn_W1_l", "L1_gnn_b1", "L1_gnn_W1_r", "L1_gnn_W2_l", "L1_gnn_b2", "L1_gnn_W2_r",
        "L2_gnn_g", "L2_gnn_mu", "L2_gnn_sigma", "L2_gnn_root", "L2_gnn_bias",
        "L3_gnn_stn1_w", "L3_gnn_stn1_b", "L3_gnn_stn2_w", "L3_gnn_stn2_b", "L3_gnn_stn3_w", "L3_gnn_stn3_b",
        "L3_gnn_stn4_w", "L3_gnn_stn4_b", "L3_gnn_conv_w", "L3_gnn_conv_b"]


def kernel(**inputs):
    import numpy as _np
    import concourse.bacc as _bacc
    from concourse import mybir as _mybir
    from concourse.bass_utils import run_bass_kernel_spmd as _run

    nc = _bacc.Bacc("TRN2", target_bir_lowering=False, num_devices=1)
    arrays, args = {}, {}
    for name in _INS:
        a = _np.ascontiguousarray(inputs[name])
        arrays[f"in_{name}_dram"] = a
        args[name] = nc.dram_tensor(f"in_{name}_dram", a.shape, _mybir.dt.from_np(a.dtype), kind="ExternalInput").ap()
    out = nc.dram_tensor("out_dram", (N, F), F32, kind="ExternalOutput").ap()
    build(nc, args, out)
    r = _run(nc, [arrays], core_ids=[0])
    return r.results[0]["out_dram"]
```

```python
from contextlib import ExitStack

import concourse.bass as bass
from concourse import mybir

F32 = mybir.dt.float32
I32 = mybir.dt.int32
BF16 = mybir.dt.bfloat16
ALU = mybir.AluOpType
ACT = mybir.ActivationFunctionType
AX = mybir.AxisListType

P = 128
N = 3125
E = 103125
NB = -(-N // P)
NP = NB * P
NH = NB + 1
HB = 13
STEPS = E // (HB * P) + 1
EP = STEPS * HB * P
PAD_KEY = NB * P
PAD_START = 5.0e7
BIG = 1.0e30
TB = 32
TB_D = 32
QUARTERS = 4
F = 32
FAR = F + 5 + 64
EPS_LN = 1e-5


class Order:

    def __init__(self, name, chunk, words, pairs, block_tiles, empty):
        self.name, self.chunk, self.words, self.pairs = name, chunk, words, pairs
        self.block_tiles, self.empty = block_tiles, empty
        self.blocks = 2 * pairs
        self.shift = chunk.bit_length() - 1
        self.per_tile = P // chunk
        self.tiles = self.blocks * block_tiles
        self.chunks = self.tiles * self.per_tile
        self.vb = block_tiles * self.per_tile
        self.slots = self.tiles * P
        assert self.chunks >= (N + E // chunk if empty else (E + (chunk - 1) * N) // chunk)


class Shared:
    pass


class Chain:

    def __init__(self, eng, sem):
        self.eng, self.sem, self.n = eng, sem, 0

    def step(self, ins):
        ins.then_inc(self.sem, 1)
        self.n += 1
        self.eng.wait_ge(self.sem, self.n)

    def put(self, ins):
        ins.then_inc(self.sem, 1)
        self.n += 1

    def wait(self):
        self.eng.wait_ge(self.sem, self.n)

    def restart(self):
        self.eng.sem_clear(self.sem)
        self.n = 0


def new_sem(nc, c, name):
    handle = nc.alloc_semaphore(name)
    c.callback(nc.release_semaphore, handle)
    c.callback(nc.gpsimd.sem_clear, handle)
    return handle


def rows_sem(nc, name):
    return nc.alloc_semaphore(name)


def stage_setup(nc, g, ins):
    R, D = g.R, g.D
    with ExitStack() as c:
        sb = lambda name, shape, dt: c.enter_context(nc.sbuf_tensor(name, shape, dt))
        sem = lambda name: new_sem(nc, c, name)
        iota_i = sb("su_iota_i", [P, P], I32)
        pidx_i = sb("su_pidx_i", [P, 1], I32)
        node_i = sb("su_node_i", [P, NH], I32)
        node_f = sb("su_node_f", [P, NH], F32)
        pg_i = sb("su_pg_i", [P, 2], I32)
        pg_f = sb("su_pg_f", [P, 2], F32)
        cg_i = sb("su_cg_i", [P, P], I32)
        cg_f = sb("su_cg_f", [P, P], F32)
        fill_r = sb("su_fill_r", [P, R.tiles * R.words], I32)
        fill_d = sb("su_fill_d", [P, D.tiles * D.words], I32)
        zeros = sb("su_zeros", [P, 4 * R.chunks // P], F32)
        goes_on = sb("su_goes_on", [P, max(o.marks.shape[0] for o in g.orders) // P], F32)
        edges = {"src": (g.key_i["src"], 1, PAD_KEY), "dst": (g.key_i["dst"], 1, PAD_KEY),
                 "edge_attr_3": (g.attr["edge_attr_3"], 3, 0.0), "edge_attr_2": (g.attr["edge_attr_2"], 2, 0.0)}
        assert E > (STEPS - 1) * HB * P and E % HB
        pad_key = sb("su_pad_key", [1, EP - E], I32)
        iotas = sem("su_iotas")
        fills = sem("su_fills")
        copied = sem("su_copied")
        steps = sem("su_steps")
        with nc.Block() as block:
            @block.gpsimd
            def _(pool):
                nc.gpsimd.iota(iota_i[:], [[1, P]], base=0, channel_multiplier=0).then_inc(iotas, 1)
                nc.gpsimd.iota(pidx_i[:], [[0, 1]], base=0, channel_multiplier=1).then_inc(iotas, 1)
                nc.gpsimd.iota(node_i[:], [[P, NH]], base=0, channel_multiplier=1).then_inc(iotas, 1)
                nc.gpsimd.memset(zeros[:], 0.0).then_inc(fills, 1)
                nc.gpsimd.memset(goes_on[:], 1.0).then_inc(fills, 1)
                for tile, width, value in edges.values():
                    nc.gpsimd.memset(tile[:, (STEPS - 1) * HB * width:], value).then_inc(fills, 1)
                nc.gpsimd.memset(pad_key[:], PAD_KEY).then_inc(fills, 1)

            @block.vector
            def _(dve):
                ch = Chain(dve, steps)
                for o, fill in ((R, fill_r), (D, fill_d)):
                    ch.step(nc.vector.memset(fill[:], 0))
                    nc.vector.memset(fill[:].rearrange("p (t w) -> p t w", w=o.words)[:, :, 0], N).then_inc(fills, 1)
                nc.vector.memset(g.ones[:], 1.0)
                nc.vector.memset(g.zero[:], 0.0)
                nc.vector.memset(g.zero_bf[:], 0.0)
                ch.step(nc.vector.memset(g.later[:], 1.0))
                nc.vector.memset(g.later[:, :, 0], 0.0)
                dve.wait_ge(iotas, 3)
                nc.vector.tensor_copy(g.iota_row[:], iota_i[:])
                ch.step(nc.vector.tensor_copy(g.pidx[:], pidx_i[:]))
                nc.vector.tensor_copy(g.digits[:], iota_i[:].unsqueeze(2).to_broadcast([P, P, HB]))
                nc.vector.tensor_scalar(g.minus_pidx[:], g.pidx[:], -1.0, None, ALU.mult)
                ch.step(nc.vector.tensor_copy(node_f[:], node_i[:]))
                nc.vector.tensor_scalar(g.valid[:], node_f[:, 0:NB], float(N), None, ALU.is_lt)
                for k, o in enumerate((R, D)):
                    nc.vector.tensor_scalar(pg_i[:, k:k + 1], pidx_i[:], o.shift, None, ALU.logical_shift_right)
                ch.step(nc.vector.tensor_scalar(cg_i[:], iota_i[:], R.shift, None, ALU.logical_shift_right))
                nc.vector.tensor_copy(pg_f[:], pg_i[:])
                ch.step(nc.vector.tensor_copy(cg_f[:], cg_i[:]))
                nc.vector.tensor_scalar(g.ident[:], g.iota_row[:], g.pidx[:], None, ALU.is_equal)
                nc.vector.tensor_scalar(g.below[:], g.iota_row[:], g.pidx[:], None, ALU.is_gt)
                nc.vector.tensor_scalar(g.before[:], g.iota_row[:], g.pidx[:], None, ALU.is_lt)
                nc.vector.tensor_scalar(R.mask[:], g.iota_row[:, 0:R.per_tile], pg_f[:, 0:1], None, ALU.is_equal)
                nc.vector.tensor_scalar(D.mask[:], g.iota_row[:, 0:D.per_tile], pg_f[:, 1:2], None, ALU.is_equal)
                nc.vector.tensor_scalar(R.mask_t[:], cg_f[0:R.per_tile, :], g.pidx[0:R.per_tile, :], None, ALU.is_equal)

            @block.sync
            def _(sp):
                whole = (STEPS - 1) * HB
                full, left = divmod(E - whole * P, HB)
                flat = {name: ins[name] if width == 1 else ins[name].rearrange("e w -> (e w)") for name, (_, width, _) in edges.items()}
                for name, (tile, width, _) in edges.items():
                    sp.dma_start(tile[:, 0:whole * width].rearrange("p (s j) -> p s j", j=HB * width),
                                 flat[name][0:whole * P * width].rearrange("(s p j) -> p s j", p=P, j=HB * width)).then_inc(copied, 16)
                for name in ("src", "dst"):
                    sp.dma_start(g.pad[name][0:E].rearrange("(p f) -> p f", p=125),
                                 ins[name].rearrange("(p f) -> p f", p=125)).then_inc(copied, 16)
                for name, tile in g.bias.items():
                    sp.dma_start(tile[:], ins[name].unsqueeze(0).to_broadcast([P, tile.shape[1]])).then_inc(copied, 16)
                sp.wait_ge(fills, 5 + len(edges))
                for name, (tile, width, _) in edges.items():
                    at, done = whole * width, (whole * P + full * HB) * width
                    sp.dma_start(tile[0:full, at:at + HB * width],
                                 flat[name][whole * P * width:done].rearrange("(p f) -> p f", p=full)).then_inc(copied, 16)
                    sp.dma_start(tile[full:full + 1, at:at + left * width],
                                 flat[name][done:E * width].rearrange("(p f) -> p f", p=1)).then_inc(copied, 16)
                for name in ("src", "dst"):
                    sp.dma_start(g.pad[name][E:EP].rearrange("(p f) -> p f", p=1), pad_key[:]).then_inc(copied, 16)
                for o, fill in ((R, fill_r), (D, fill_d)):
                    sp.dma_start(o.rec.rearrange("(p t) w -> p (t w)", p=P), fill[:]).then_inc(copied, 16)
                    sp.dma_start(o.keep.rearrange("(p f) -> p f", p=P), goes_on[:, 0:o.marks.shape[0] // P]).then_inc(copied, 16)
                for marks in (g.near_marks, g.shift_marks):
                    words = marks.shape[1] * R.chunks // P
                    sp.dma_start(marks.rearrange("(p f) w -> p (f w)", p=P), zeros[:, 0:words]).then_inc(copied, 16)
                sp.wait_ge(copied, (10 + 3 * len(edges) + len(g.bias)) * 16)


def one_hot(nc, g, to, digit):
    shape = [P, to.shape[1], HB]
    return nc.vector.tensor_tensor(to[:], g.digits[:, 0:shape[1], :], digit.unsqueeze(1).to_broadcast(shape), ALU.is_equal)


def stage_histogram(nc, g):
    keys = ("src", "dst")
    k, two = g.R.key, range(2)
    with ExitStack() as c:
        sb = lambda name, shape, dt: c.enter_context(nc.sbuf_tensor(name, shape, dt))
        sem = lambda name: new_sem(nc, c, name)
        lo_i = sb("hi_lo_i", [P, STEPS * HB], I32)
        hi_i = sb("hi_hi_i", [P, STEPS * HB], I32)
        lo1 = [sb(f"hi_lo1_{i}", [P, P, HB], BF16) for i in two]
        hi1 = [sb(f"hi_hi1_{i}", [P, NH, HB], BF16) for i in two]
        count = c.enter_context(nc.psum_tensor("hi_count", [P, NH], F32))
        stored, steps, split = sem("hi_stored"), sem("hi_steps"), sem("hi_split")
        onehots, counted = sem("hi_onehots"), sem("hi_counted")
        with nc.Block() as block:
            @block.sync
            def _(sp):
                for n, key in enumerate(keys):
                    sp.wait_ge(split, n + 1)
                    sp.dma_start(g.pad_lo[key].rearrange("(s p j) -> p s j", p=P, j=HB),
                                 g.lo[key][:].rearrange("p (s j) -> p s j", j=HB)).then_inc(stored, 16)
                sp.wait_ge(stored, 32)

            @block.vector
            def _(dve):
                ch = Chain(dve, steps)
                for key in keys:
                    ch.step(nc.vector.tensor_copy(g.key_f[key][:], g.key_i[key][:]))
                    ch.step(nc.vector.tensor_scalar(lo_i[:], g.key_i[key][:], P - 1, None, ALU.bitwise_and))
                    ch.step(nc.vector.tensor_scalar(hi_i[:], g.key_i[key][:], 7, None, ALU.logical_shift_right))
                    ch.step(nc.vector.tensor_copy(g.lo[key][:], lo_i[:]))
                    ch.step(nc.vector.tensor_copy(g.hi[key][:], hi_i[:]))
                    dve.sem_inc(split, 1)

                def half(step, slot):
                    cols = bass.ds(step * HB, HB)
                    one_hot(nc, g, lo1[slot], g.lo[k][:, cols])
                    one_hot(nc, g, hi1[slot], g.hi[k][:, cols]).then_inc(onehots, 1)

                for slot in two:
                    half(slot, slot)
                with dve.Fori(1, STEPS // 2) as i:
                    for slot in two:
                        dve.wait_ge(counted, i * 2 + (slot - 1))
                        half(i * 2 + slot, slot)
                dve.wait_ge(counted, STEPS + 1)
                nc.vector.tensor_copy(g.degree[k][:], count[:])

            @block.tensor
            def _(pe):
                nc.tensor.matmul(count[:], g.zero_bf[:], g.zero_bf[:, 0:NH], start=True, stop=False)
                with pe.Fori(0, STEPS // 2) as i:
                    for slot in two:
                        pe.wait_ge(onehots, i * 2 + (slot + 1))
                        for j in range(HB):
                            last = nc.tensor.matmul(count[:], lo1[slot][:, :, j], hi1[slot][:, :, j], start=False, stop=False)
                        last.then_inc(counted, 1)
                nc.tensor.matmul(count[:], g.zero_bf[:], g.zero_bf[:, 0:NH], start=False, stop=True).then_inc(counted, 1)


def stage_starts(nc, g, o):
    with ExitStack() as c:
        sb = lambda name, shape, dt: c.enter_context(nc.sbuf_tensor(f"{name}_{o.name}", shape, dt))
        sem = lambda name: new_sem(nc, c, f"{name}_{o.name}")
        tmp_i = sb("st_tmp_i", [P, NB], I32)
        need = sb("st_need", [P, NB], F32)
        total = sb("st_total", [P, NB], F32)
        upto = sb("st_upto", [P, NB], F32)
        start = sb("st_start", [P, NB], F32)
        marked = sb("st_marked", [P, NB], F32)
        place = sb("st_place", [P, NB], F32)
        ps_in = c.enter_context(nc.psum_tensor(f"st_ps_in_{o.name}", [P, NB], F32))
        ps_tot = c.enter_context(nc.psum_tensor(f"st_ps_tot_{o.name}", [P, NB], F32))
        steps, needed, summed = sem("st_steps"), sem("st_needed"), sem("st_summed")
        with nc.Block() as block:
            @block.vector
            def _(dve):
                ch = Chain(dve, steps)
                deg = g.degree[o.key][:, 0:NB]
                ch.step(nc.vector.tensor_scalar(o.inv_degree[:], deg, 1.0, None, ALU.max))
                ch.step(nc.vector.reciprocal(o.inv_degree[:], o.inv_degree[:]))
                ch.step(nc.vector.scalar_tensor_tensor(o.inv_degree[:], deg, 1.0, o.inv_degree[:], ALU.min, ALU.mult))
                ch.step(nc.vector.tensor_scalar(tmp_i[:], deg, float(o.chunk - 1), None, ALU.add))
                ch.step(nc.vector.tensor_scalar(tmp_i[:], tmp_i[:], o.shift, None, ALU.logical_shift_right))
                ch.step(nc.vector.tensor_copy(need[:], tmp_i[:]))
                ch.step(nc.vector.scalar_tensor_tensor(need[:], need[:], 1.0 if o.empty else 0.0, g.valid[:], ALU.max, ALU.mult))
                dve.sem_inc(needed, 1)
                dve.wait_ge(summed, 1)
                ch.step(nc.vector.tensor_copy(total[:], ps_tot[:]))
                ch.step(nc.vector.tensor_tensor_scan(upto[:], g.ones[:, 0:NB], total[:], 0.0, ALU.mult, ALU.add))
                ch.step(nc.vector.tensor_sub(upto[:], upto[:], total[:]))
                ch.step(nc.vector.tensor_add(start[:], ps_in[:], upto[:]))
                nc.vector.memset(o.slot0[:, NB:NH], PAD_START)
                ch.step(nc.vector.tensor_scalar(o.slot0[:, 0:NB], start[:], float(o.chunk), None, ALU.mult))
                ch.step(nc.vector.tensor_add(marked[:], start[:], need[:]))
                ch.step(nc.vector.tensor_scalar(marked[:], marked[:], -1.0, 0.0, ALU.add, ALU.max))
                if o is g.D:
                    quarter = o.chunks // QUARTERS
                    ch.step(nc.vector.memset(place[:], 0.0))
                    for q in range(1, QUARTERS):
                        cut = g.crossing[:, q - 1, :]
                        ch.step(nc.vector.tensor_scalar(cut, marked[:], float(q * quarter), None, ALU.is_ge))
                        ch.step(nc.vector.tensor_add(place[:], place[:], cut))
                        ch.step(nc.vector.scalar_tensor_tensor(cut, start[:], float(q * quarter), cut, ALU.is_lt, ALU.mult))
                    ch.step(nc.vector.scalar_tensor_tensor(marked[:], place[:], -float(quarter), marked[:], ALU.mult, ALU.add))
                    ch.step(nc.vector.scalar_tensor_tensor(marked[:], marked[:], float(QUARTERS), place[:], ALU.mult, ALU.add))
                ch.step(nc.vector.tensor_copy(o.last[:], marked[:]))
                ch.step(nc.vector.tensor_scalar(marked[:], need[:], 1.0, -PAD_START, ALU.min, ALU.mult))
                ch.step(nc.vector.tensor_scalar(marked[:], marked[:], PAD_START, None, ALU.add))
                ch.step(nc.vector.tensor_add(marked[:], marked[:], start[:]))
                nc.vector.tensor_copy(o.start[:], marked[:])

            @block.tensor
            def _(pe):
                pe.wait_ge(needed, 1)
                nc.tensor.matmul(ps_in[:], g.below[:], need[:], start=True, stop=True)
                nc.tensor.matmul(ps_tot[:], g.ones[:], need[:], start=True, stop=True).then_inc(summed, 1)



def mark_first_chunks(pool, g, o, scattered):
    for b in range(NB):
        pool.indirect_dma_start(
            out=o.marks[:, :], out_offset=bass.IndirectOffsetOnAxis(ap=o.start[:, b:b + 1], axis=0),
            in_=g.zero[:], in_offset=None, bounds_check=o.chunks - 1, oob_is_err=False).then_inc(scattered, 16)


def stage_sort(nc, g, o, tally=None, ones_weights=None):
    W = o.words
    A = W - 1
    with ExitStack() as c:
        sb = lambda name, shape, dt: c.enter_context(nc.sbuf_tensor(f"so_{o.name}_{name}", shape, dt))
        ps = lambda name, shape: c.enter_context(nc.psum_tensor(f"so_{o.name}_{name}", shape, F32))
        sem = lambda name: new_sem(nc, c, f"so_{o.name}_{name}")
        two = range(2)
        row = [sb(f"row{i}", [P, P * HB], I32) for i in two]
        low = [sb(f"low{i}", [P, P * HB], BF16) for i in two]
        apart = sb("apart", [P, P * HB], BF16)
        lo_t = [sb(f"lo_t{i}", [P, P, HB], F32) for i in two]
        lo1 = [sb(f"lo1{i}", [P, P, HB], BF16) for i in two]
        hi1 = [sb(f"hi1{i}", [P, NH, HB], BF16) for i in two]
        same = sb("same", [P, HB, P], BF16)
        rank = [sb(f"rank{i}", [P, HB], F32) for i in two]
        counts = sb("counts", [P, NH, HB + 1], F32)
        table = [sb(f"table{i}", [P, NH, HB + 1], F32) for i in two]
        pick = sb("pick", [P, HB, NH], F32)
        slot = sb("slot", [P, HB], F32)
        slot_i = sb("slot_i", [P, HB], I32)
        part_i = sb("part_i", [P, HB], I32)
        tile_i = sb("tile_i", [P, HB], I32)
        place = [sb(f"place{i}", [P, HB], I32) for i in two]
        rec = [sb(f"rec{i}", [P, HB, W], I32) for i in two]
        ps_hist = [ps(f"hist{i}", [P, HB, NH]) for i in two]
        looks = 1 if ones_weights is not None else 2
        ps_look = [ps(f"look{i}", [P, HB, NH]) for i in range(looks)]
        row_in = [sem(f"row_in{i}") for i in two]
        row_used, onehots, hist, tables, looked = sem("row_used"), sem("onehots"), sem("hist"), sem("tables"), sem("looked")
        looks_read, placed, taken = sem("looks_read"), sem("placed"), sem("taken")
        low_in = [sem(f"low_in{i}") for i in two]
        apart_made, lows_made = sem("apart_made"), sem("lows_made")
        scattered = [rows_sem(nc, f"so_{o.name}_scattered{i}") for i in two]
        marked = rows_sem(nc, f"so_{o.name}_marked")
        steps = sem("steps")
        half = STEPS // 2
        if tally is not None:
            lo2 = [sb(f"lo2{i}", [P, P, HB], BF16) for i in two]
            hi2 = [sb(f"hi2{i}", [P, NH, HB], BF16) for i in two]
            ps_count = ps("count", [P, NH])
            onehots2, counted = sem("onehots2"), sem("counted")
        sl = None
        spans = [(1, half - 1, 0)]
        if ones_weights is not None:
            sl = Spline(nc, c, g, "p_1", 1, ones_weights.shape[2], g.sums_r64)
            by_third = ones_weights.rearrange("(k t) i o -> k (t i) o", t=sl.J)
            sl.banks(c, "p_1")
            both = sl.o.blocks - 2 - (half - 2)
            assert 0 < both < half - 2
            spans = [(1, 1 + both, 2), (1 + both, half - 1, 1)]

        def block_of(i, b, per, first):
            return i * 2 + b if per == 2 else i + (first + 1)

        with nc.Block() as block:
            @block.sync
            def _(sp):
                def load(step, b):
                    along = lambda of: of[bass.ds(step * (P * HB), P * HB)].rearrange("(a f) -> a f", a=1).to_broadcast([P, P * HB])
                    sp.dma_start(low[b][:], along(g.pad_lo[o.key])).then_inc(low_in[b], 16)
                    sp.dma_start(row[b][:], along(g.pad[o.key])).then_inc(row_in[b], 16)

                def next_load(step, b):
                    sp.wait_ge(row_used, step - 1)
                    sp.wait_ge(apart_made, step - 1)
                    load(step, b)

                for b in two:
                    load(b, b)
                if sl:
                    sl.begin_sync(sp, by_third)
                    sl.load(sp, 0, 0)
                for b in two:
                    next_load(b + 2, b)
                if sl:
                    sp.wait_ge(sl.spreads, 2)
                    sl.load(sp, 1, 0)
                for lo, hi, per in spans:
                    with sp.Fori(lo, hi) as i:
                        for b in two:
                            next_load(i * 2 + (b + 2), b)
                            if b < per:
                                sp.wait_ge(sl.spreads, block_of(i, b, per, both) + 1)
                                sl.load(sp, block_of(i, b, per, both), 0)
                sp.wait_ge(row_in[0], 16 * half)
                sp.wait_ge(row_in[1], 16 * half)

            @block.vector
            def _(dve):
                ch = Chain(dve, steps)

                def others(step, b, reused):
                    if reused:
                        dve.wait_ge(counted, step - 1)
                    cols = bass.ds(step * HB, HB)
                    one_hot(nc, g, lo2[b], g.lo[tally.key][:, cols])
                    one_hot(nc, g, hi2[b], g.hi[tally.key][:, cols]).then_inc(onehots2, 1)

                def digits(step, b, turn, first, reused=True):
                    cols = bass.ds(step * HB, HB)
                    dve.wait_ge(row_in[b], turn * 16 + 16)
                    one_hot(nc, g, lo1[b], g.lo[o.key][:, cols])
                    one_hot(nc, g, hi1[b], g.hi[o.key][:, cols]).then_inc(onehots, 1)
                    keys = row[b][:].rearrange("p (e j) -> p e j", j=HB)
                    for j in range(HB):
                        last = nc.vector.scalar_tensor_tensor(same[:, j, :], keys[:, :, j], g.key_f[o.key][:, bass.ds(step * HB + j, 1)],
                                                              g.before[:], ALU.is_equal, ALU.mult, accum_out=rank[b][:, j:j + 1])
                    last.then_inc(row_used, 1)
                    if tally is not None:
                        others(step, b, reused)
                    dve.wait_ge(hist, step + 1)
                    before = o.slot0[:] if first else table[1 - b][:, :, HB]
                    nc.vector.tensor_copy(counts[:, :, 0], before)
                    ch.step(nc.vector.tensor_copy(counts[:, :, 1:HB + 1], ps_hist[b][:].rearrange("p j k -> p k j")))
                    flat = lambda t: t[:].rearrange("p k j -> p (k j)")
                    nc.vector.tensor_tensor_scan(flat(table[b]), flat(g.later), flat(counts), 0.0, ALU.mult, ALU.add).then_inc(tables, 1)
                    dve.wait_ge(tables, step + 1)

                def places(step, b, turn, first):
                    cols = bass.ds(step * HB, HB)
                    dve.wait_ge(looked, step + 1)
                    nc.vector.tensor_mul(pick[:], ps_look[b % looks][:], hi1[b][:].rearrange("p k j -> p j k")).then_inc(looks_read, 1)
                    dve.wait_ge(looks_read, step + 1)
                    ch.step(nc.vector.tensor_reduce(slot[:], pick[:], AX.X, ALU.add))
                    ch.step(nc.vector.tensor_add(slot_i[:], slot[:], rank[b][:]))
                    nc.vector.tensor_scalar(part_i[:], slot_i[:], P - 1, None, ALU.bitwise_and)
                    ch.step(nc.vector.tensor_scalar(tile_i[:], slot_i[:], 7, None, ALU.logical_shift_right))
                    if not first:
                        dve.wait_ge(scattered[b], turn * (16 * HB))
                    nc.vector.scalar_tensor_tensor(place[b][:], part_i[:], float(o.tiles), tile_i[:], ALU.mult, ALU.add)
                    nc.vector.tensor_copy(rec[b][:, :, 0], g.key_i[o.other][:, cols])
                    nc.vector.tensor_copy(rec[b][:, :, 1:W].bitcast(F32),
                                          g.attr[o.attr][:, bass.ds(step * (HB * A), HB * A)].rearrange("p (j a) -> p j a", a=A)).then_inc(placed, 1)

                def spline_block(m):
                    sl.scan(dve, ch, m - 2)
                    sl.points(dve, ch, m, 0, m)
                    sl.spread(dve, m, 0, [0])

                digits(0, 0, 0, True, reused=False)
                digits(1, 1, 0, False, reused=False)
                places(0, 0, 0, True)
                ch.restart()
                digits(2, 0, 1, False)
                places(1, 1, 0, True)
                if sl:
                    sl.begin_vector(dve, ch)
                    for m in two:
                        sl.points(dve, ch, m, 0, m, first=m == 0)
                        sl.spread(dve, m, 0, [0])
                for lo, hi, per in spans:
                    with dve.Fori(lo, hi) as i:
                        ch.restart()
                        for b in two:
                            digits(i * 2 + (b + 1), 1 - b, i + b, False)
                            places(i * 2 + b, b, i, False)
                            if b < per:
                                spline_block(block_of(i, b, per, both))
                ch.restart()
                digits(STEPS - 1, 1, half - 1, False)
                places(STEPS - 2, 0, half - 1, False)
                if sl:
                    sl.scan(dve, ch, sl.o.blocks - 2)
                    sl.scan(dve, ch, sl.o.blocks - 1)
                places(STEPS - 1, 1, half - 1, False)
                if tally is not None:
                    dve.wait_ge(counted, STEPS + 1)
                    nc.vector.tensor_copy(g.degree[tally.key][:], ps_count[:])

            @block.tensor
            def _(pe):
                def histograms(step, b):
                    pe.wait_ge(onehots, step + 1)
                    for j in range(HB):
                        last = nc.tensor.matmul(ps_hist[b][:, j, :], lo1[b][:, :, j], hi1[b][:, :, j], start=True, stop=True)
                    last.then_inc(hist, 1)
                    if tally is not None:
                        pe.wait_ge(onehots2, step + 1)
                        for j in range(HB):
                            last = nc.tensor.matmul(ps_count[:], lo2[b][:, :, j], hi2[b][:, :, j], start=False, stop=False)
                        last.then_inc(counted, 1)

                def lookups(step, b, first=False):
                    pe.wait_ge(tables, step + 1)
                    pe.wait_ge(lows_made, step + 1)
                    if looks == 1 and not first:
                        pe.wait_ge(looks_read, step)
                    for j in range(HB):
                        last = nc.tensor.matmul(ps_look[b % looks][:, j, :], lo_t[b][:, :, j], table[b][:, :, j], start=True, stop=True)
                    last.then_inc(looked, 1)

                if tally is not None:
                    nc.tensor.matmul(ps_count[:], g.zero_bf[:], g.zero_bf[:, 0:NH], start=True, stop=False)
                for step in range(3):
                    histograms(step, step % 2)
                    lookups(step, step % 2, first=step == 0)
                if sl:
                    sl.begin_tensor(pe)
                    sl.outer_products(pe, 0)
                    sl.through_weights(pe, 0)
                for lo, hi, per in spans:
                    with pe.Fori(lo, hi) as i:
                        for b in two:
                            histograms(i * 2 + (b + 1), 1 - b)
                            if b < per:
                                sl.outer_products(pe, block_of(i, b, per, both) - 1)
                            lookups(i * 2 + (b + 1), 1 - b)
                            if b < per:
                                sl.turn(pe, block_of(i, b, per, both) - 2)
                                sl.through_weights(pe, block_of(i, b, per, both) - 1)
                histograms(STEPS - 1, 1)
                if sl:
                    sl.outer_products(pe, sl.o.blocks - 1)
                lookups(STEPS - 1, 1)
                if sl:
                    sl.turn(pe, sl.o.blocks - 2)
                    sl.through_weights(pe, sl.o.blocks - 1)
                    sl.turn(pe, sl.o.blocks - 1)
                if tally is not None:
                    nc.tensor.matmul(ps_count[:], g.zero_bf[:], g.zero_bf[:, 0:NH], start=False, stop=True).then_inc(counted, 1)

            @block.scalar
            def _(act):
                def lows(step, b, turn, before=2):
                    act.wait_ge(low_in[b], turn * 16 + 16)
                    if before >= 1:
                        act.wait_ge(lows_made, step)
                    nc.scalar.activation(apart[:], low[b][:], ACT.Abs, bias=g.minus_pidx[:]).then_inc(apart_made, 1)
                    act.wait_ge(apart_made, step + 1)
                    if before >= 2:
                        act.wait_ge(looked, step - 1)
                    nc.scalar.activation(lo_t[b][:].rearrange("p e j -> p (e j)"), apart[:], ACT.Relu, bias=g.ones[:, 0:1], scale=-1.0).then_inc(lows_made, 1)

                for step in range(4):
                    lows(step, step % 2, step // 2, min(step, 2))
                if sl:
                    sl.begin_scalar(act)
                    sl.copy_products(act, 0)
                for lo, hi, per in spans:
                    with act.Fori(lo, hi) as i:
                        for b in two:
                            lows(i * 2 + (b + 2), b, i + 1)
                            if b < per:
                                sl.copy_products(act, block_of(i, b, per, both) - 1)
                                sl.store_rows(act, block_of(i, b, per, both) - 2)
                if sl:
                    sl.copy_products(act, sl.o.blocks - 1)
                    sl.store_rows(act, sl.o.blocks - 2)
                    sl.store_rows(act, sl.o.blocks - 1)
                    sl.end_scalar(act)

            @block.gpsimd
            def _(pool):
                mark_first_chunks(pool, g, o, marked)
                bound = pool.to_reg(o.slots - 1)
                with pool.Fori(0, half) as i:
                    for b in two:
                        pool.wait_ge(placed, i * 2 + (b + 1))
                        pool.sem_inc(taken, 1)
                        for j in range(HB):
                            pool.indirect_dma_start(
                                out=o.rec[:, :], out_offset=bass.IndirectOffsetOnAxis(ap=place[b][:, j:j + 1], axis=0),
                                in_=rec[b][:, j, :], in_offset=None, bounds_check=bound,
                                oob_is_err=False).then_inc(scattered[b], 16)
                for b in two:
                    pool.wait_ge(scattered[b], half * 16 * HB)
                pool.wait_ge(marked, 16 * NB)



def stage_chunks(nc, g):
    per = g.R.chunks // P
    with ExitStack() as c:
        sb = lambda name, shape: c.enter_context(nc.sbuf_tensor(name, shape, F32))
        sem = lambda name: new_sem(nc, c, name)
        keep, firsts, node = sb("ck_keep", [P, per]), sb("ck_firsts", [P, 1]), sb("ck_node", [P, 1])
        ps_before = c.enter_context(nc.psum_tensor("ck_ps_before", [P, 1], F32))
        loaded, steps, counted, summed = sem("ck_loaded"), sem("ck_steps"), sem("ck_counted"), sem("ck_summed")
        with nc.Block() as block:
            @block.sync
            def _(sp):
                sp.dma_start(keep[:], g.R.keep[0:g.R.chunks].rearrange("(p f) -> p f", p=P)).then_inc(loaded, 16)

            @block.vector
            def _(dve):
                ch = Chain(dve, steps)
                dve.wait_ge(loaded, 16)
                ch.step(nc.vector.tensor_reduce(firsts[:], keep[:], AX.X, ALU.add))
                nc.vector.tensor_scalar(firsts[:], firsts[:], -1.0, float(per), ALU.mult, ALU.add).then_inc(counted, 1)
                dve.wait_ge(summed, 1)
                ch.step(nc.vector.tensor_sub(node[:], ps_before[:], keep[:, 0:1]))
                nc.vector.tensor_copy(g.chunk_row[:], node[:])

            @block.tensor
            def _(pe):
                pe.wait_ge(counted, 1)
                nc.tensor.matmul(ps_before[:], g.below[:], firsts[:], start=True, stop=True).then_inc(summed, 1)


def stage_spread(nc, g, name, rows, table, width, marks, to):
    o = g.R
    per = o.chunks // P
    with ExitStack() as c:
        sb = lambda nm, shape: c.enter_context(nc.sbuf_tensor(f"{name}_{nm}", shape, F32))
        before, keep, marked, spread = sb("before", [P, width]), sb("keep", [P, per]), sb("marked", [P, per, width]), sb("spread", [P, per, width])
        scattered, got = rows_sem(nc, f"{name}_scattered"), rows_sem(nc, f"{name}_got")
        loaded, held, stored = (new_sem(nc, c, f"{name}_{n}") for n in ("loaded", "held", "stored"))
        with nc.Block() as block:
            @block.gpsimd
            def _(pool):
                pool.indirect_dma_start(out=before[:], out_offset=None, in_=table[:, :],
                                        in_offset=bass.IndirectOffsetOnAxis(ap=g.chunk_row[:, 0:1], axis=0)).then_inc(got, 16)
                for b in range(NB):
                    pool.indirect_dma_start(out=marks[:, :], out_offset=bass.IndirectOffsetOnAxis(ap=o.start[:, b:b + 1], axis=0),
                                            in_=rows[:, b, :], in_offset=None, bounds_check=o.chunks - 1,
                                            oob_is_err=False).then_inc(scattered, 16)

            @block.sync
            def _(sp):
                sp.dma_start(keep[:], o.keep[0:o.chunks].rearrange("(p f) -> p f", p=P)).then_inc(loaded, 16)
                sp.wait_ge(scattered, 16 * NB)
                sp.dma_start(marked[:].rearrange("p f w -> p (f w)"), marks.rearrange("(p f) w -> p (f w)", p=P)).then_inc(loaded, 16)
                sp.wait_ge(held, width)
                sp.dma_start(to.rearrange("(p f) w -> p (f w)", p=P), spread[:].rearrange("p f w -> p (f w)")).then_inc(stored, 16)
                sp.wait_ge(stored, 16)

            @block.vector
            def _(dve):
                dve.wait_ge(got, 16)
                dve.wait_ge(loaded, 32)
                for k in range(width):
                    nc.vector.tensor_tensor_scan(spread[:, :, k], keep[:], marked[:, :, k], before[:, k:k + 1],
                                                 ALU.mult, ALU.add).then_inc(held, 1)


def collect_rows(pool, o, sums, to, got, blocks=range(NB)):
    for b in blocks:
        pool.indirect_dma_start(out=to[:, b, :], out_offset=None, in_=sums[:, :],
                                in_offset=bass.IndirectOffsetOnAxis(ap=o.last[:, b:b + 1], axis=0)).then_inc(got, 16)
    pool.wait_ge(got, 16 * len(blocks))


def stage_collect(nc, g, name, o, sums, to):
    with ExitStack() as c:
        got = rows_sem(nc, f"{name}_got")
        with nc.Block() as block:
            @block.gpsimd
            def _(pool):
                collect_rows(pool, o, sums, to, got)


class Gaussians:

    def __init__(self, nc, c, g, mu_in, sigma_in, gauss):
        o = g.D
        self.nc, self.o, self.mu_in, self.sigma_in, self.gauss = nc, o, mu_in, sigma_in, gauss
        self.per = o.tiles // QUARTERS
        sb = lambda nm, shape, dt=F32: c.enter_context(nc.sbuf_tensor(f"ga_{nm}", shape, dt))
        sem = lambda nm: new_sem(nc, c, f"ga_{nm}")
        self.rec = sb("rec", [P, o.tiles, o.words], I32)
        self.mu, self.scale, self.diff = sb("mu", [P, 3, 2]), sb("scale", [P, 3, 2]), sb("diff", [P, self.per, 3, 2])
        self.loaded, self.dists, self.done = sem("loaded"), sem("dists"), sem("done")

    def load(self, sp):
        o = self.o
        sp.dma_start(self.rec[:].rearrange("p t w -> p (t w)"), o.rec.rearrange("(p t) w -> p (t w)", p=P)).then_inc(self.loaded, 16)
        for to, view in ((self.mu, self.mu_in), (self.scale, self.sigma_in)):
            sp.dma_start(to[:].rearrange("p k d -> p (k d)"),
                         view.rearrange("k d -> (k d)").unsqueeze(0).to_broadcast([P, 6])).then_inc(self.loaded, 16)

    def distances(self, dve, ch):
        nc, scale, diff, b4 = self.nc, self.scale, self.diff, [P, self.per, 3, 2]
        dve.wait_ge(self.loaded, 48)
        ch.step(nc.vector.tensor_mul(scale[:], scale[:], scale[:]))
        ch.step(nc.vector.tensor_scalar(scale[:], scale[:], 1e-15, None, ALU.add))
        ch.step(nc.vector.reciprocal(scale[:], scale[:]))
        for q in range(QUARTERS):
            attr = self.rec[:, q * self.per:(q + 1) * self.per, 1:3].bitcast(F32)
            ch.step(nc.vector.tensor_sub(diff[:], attr.unsqueeze(2).to_broadcast(b4), self.mu[:].unsqueeze(1).to_broadcast(b4)))
            ch.step(nc.vector.tensor_mul(diff[:], diff[:], diff[:]))
            ch.step(nc.vector.tensor_mul(diff[:], diff[:], scale[:].unsqueeze(1).to_broadcast(b4)))
            ch.step(nc.vector.tensor_reduce(self.gauss[:, :, q, :], diff[:], AX.X, ALU.add))
        dve.sem_inc(self.dists, 1)

    def exponentials(self, act):
        act.wait_ge(self.dists, 1)
        flat = self.gauss[:].rearrange("p t q k -> p (t q k)")
        self.nc.scalar.activation(flat, flat, ACT.Exp, scale=-0.5).then_inc(self.done, 1)
        act.wait_ge(self.done, 1)


def stage_collect_quarters(nc, g, name, sums, to, gaussians=None, collected=False):
    o = g.D
    last_row = (o.chunks // QUARTERS - 1) * QUARTERS
    with ExitStack() as c:
        ends = c.enter_context(nc.sbuf_tensor(f"{name}_ends", [P, QUARTERS - 1, F], F32))
        part = c.enter_context(nc.sbuf_tensor(f"{name}_part", [P, NB, F], F32))
        got = rows_sem(nc, f"{name}_got")
        loaded, steps = new_sem(nc, c, f"{name}_loaded"), new_sem(nc, c, f"{name}_steps")
        b3 = [P, NB, F]
        beside = Gaussians(nc, c, g, *gaussians) if gaussians is not None else None
        with nc.Block() as block:
            if not collected:
                @block.gpsimd
                def _(pool):
                    collect_rows(pool, o, sums, to, got)

            @block.sync
            def _(sp):
                sp.dma_start(ends[:].rearrange("p q f -> p (q f)"), sums[last_row:last_row + QUARTERS - 1, :]
                             .rearrange("q f -> (q f)").unsqueeze(0).to_broadcast([P, (QUARTERS - 1) * F])).then_inc(loaded, 16)

                if beside:
                    beside.load(sp)

            @block.scalar
            def _(act):
                if beside:
                    beside.exponentials(act)

            @block.vector
            def _(dve):
                ch = Chain(dve, steps)
                if beside:
                    beside.distances(dve, ch)
                dve.wait_ge(loaded, 16)
                for q in range(QUARTERS - 1):
                    ch.step(nc.vector.tensor_mul(part[:], g.crossing[:, q, :].unsqueeze(2).to_broadcast(b3),
                                                 ends[:, q, :].unsqueeze(1).to_broadcast(b3)))
                    if q == 0 and not collected:
                        dve.wait_ge(got, 16 * NB)
                    ch.step(nc.vector.tensor_add(to[:], to[:], part[:]))


def stage_dense(nc, g, name, src, k, width, dst, weight_parts, collect=None):
    per = P // k
    groups = -(-NB // per)
    wave = min(4, 512 // (per * width))
    waves = [range(a, min(a + wave, groups)) for a in range(0, groups, wave)]
    RING = 3
    blocks = lambda q: min(per, NB - q * per)
    with ExitStack() as c:
        sb = lambda nm, shape, dt=F32: c.enter_context(nc.sbuf_tensor(f"{name}_{nm}", shape, dt))
        sem = lambda nm: new_sem(nc, c, f"{name}_{nm}")
        wide = sb("wide", [per * k, per * width])
        cols = sb("cols", [per * k, groups, P])
        ps_t = [c.enter_context(nc.psum_tensor(f"{name}_ps_t{i}", [per * k, wave, P], F32)) for i in range(RING)]
        ps_o = [c.enter_context(nc.psum_tensor(f"{name}_ps_o{i}", [P, wave, per * width], F32)) for i in range(RING)]
        zeroed, loaded, turned, copied, done, taken = (
            sem(n) for n in ("zeroed", "loaded", "turned", "copied", "done", "taken"))
        with nc.Block() as block:
            if collect is not None:
                collected = rows_sem(nc, f"{name}_collected")

                @block.gpsimd
                def _(pool):
                    collect_rows(pool, collect[0], collect[1], collect[2], collected, *collect[3:])

            @block.sync
            def _(sp):
                sp.wait_ge(zeroed, 1)
                for r in range(per):
                    for row, col, view in weight_parts:
                        h, w = view.shape
                        sp.dma_start(wide[r * k + row:r * k + row + h, r * width + col:r * width + col + w], view).then_inc(loaded, 16)
                sp.wait_ge(loaded, 16 * per * len(weight_parts))

            @block.vector
            def _(dve):
                nc.vector.memset(wide[:], 0.0).then_inc(zeroed, 1)
                flat = dst[:].rearrange("p b w -> p (b w)")
                for n, qs in enumerate(waves):
                    dve.wait_ge(done, n + 1)
                    full = [q for q in qs if blocks(q) == per]
                    if full:
                        last = nc.vector.tensor_copy(flat[:, full[0] * per * width:(full[-1] + 1) * per * width],
                                                     ps_o[n % RING][:, 0:len(full), :].rearrange("p q w -> p (q w)"))
                    if len(full) < len(qs):
                        q = qs[-1]
                        last = nc.vector.tensor_copy(flat[:, q * per * width:NB * width],
                                                     ps_o[n % RING][:, len(full), 0:blocks(q) * width])
                    last.then_inc(taken, 1)

            @block.tensor
            def _(pe):
                rows = src[:].rearrange("p b k -> p (b k)")

                def transposes(n):
                    if n >= RING:
                        pe.wait_ge(copied, n - RING + 1)
                    for at, q in enumerate(waves[n]):
                        words = blocks(q) * k
                        last = nc.tensor.transpose(ps_t[n % RING][0:words, at, :], rows[:, q * per * k:q * per * k + words], g.ident[:])
                    last.then_inc(turned, 1)

                def products(n):
                    pe.wait_ge(copied, n + 1)
                    if n >= RING:
                        pe.wait_ge(taken, n - RING + 1)
                    for at, q in enumerate(waves[n]):
                        m = blocks(q)
                        last = nc.tensor.matmul(ps_o[n % RING][:, at, 0:m * width], cols[0:m * k, q, :], wide[0:m * k, 0:m * width],
                                                start=True, stop=True)
                    last.then_inc(done, 1)

                for n in range(min(2, len(waves))):
                    transposes(n)
                pe.wait_ge(loaded, 16 * per * len(weight_parts))
                for n in range(len(waves)):
                    products(n)
                    if n + 2 < len(waves):
                        transposes(n + 2)

            @block.scalar
            def _(act):
                for n, qs in enumerate(waves):
                    act.wait_ge(turned, n + 1)
                    full = [q for q in qs if blocks(q) == per]
                    if full:
                        last = nc.scalar.copy(cols[:, full[0]:full[-1] + 1, :], ps_t[n % RING][:, 0:len(full), :])
                    if len(full) < len(qs):
                        words = blocks(qs[-1]) * k
                        last = nc.scalar.copy(cols[0:words, qs[-1], :], ps_t[n % RING][0:words, len(full), :])
                    last.then_inc(copied, 1)


def layernorm(ch, nc, g, t, out, act):
    b3 = lambda ap: ap.unsqueeze(2).to_broadcast([P, NB, F])
    ch.step(nc.vector.tensor_reduce(t.mean[:], g.x[:], AX.X, ALU.add))
    ch.step(nc.vector.tensor_scalar(t.mean[:], t.mean[:], 1.0 / F, None, ALU.mult))
    ch.step(nc.vector.tensor_sub(t.centred[:], g.x[:], b3(t.mean[:])))
    ch.step(nc.vector.tensor_mul(t.square[:], t.centred[:], t.centred[:]))
    ch.step(nc.vector.tensor_reduce(t.var[:], t.square[:], AX.X, ALU.add))
    ch.step(nc.vector.tensor_scalar(t.var[:], t.var[:], 1.0 / F, EPS_LN, ALU.mult, ALU.add))
    act(t.var[:], ACT.Sqrt)
    ch.step(nc.vector.reciprocal(t.var[:], t.var[:]))
    ch.step(nc.vector.tensor_mul(t.centred[:], t.centred[:], b3(t.var[:])))
    ch.step(nc.vector.tensor_scalar(t.centred[:], t.centred[:], 0.0, None, ALU.max))
    ch.step(nc.vector.tensor_mul(out, t.centred[:], b3(g.valid[:])))


class NormBuffers:
    def __init__(self, nc, c, name):
        sb = lambda nm, shape: c.enter_context(nc.sbuf_tensor(f"{name}_{nm}", shape, F32))
        self.mean, self.var = sb("mean", [P, NB]), sb("var", [P, NB])
        self.centred, self.square = sb("centred", [P, NB, F]), sb("square", [P, NB, F])


def node_rows(table):
    return table.rearrange("(b p) w -> p b w", p=P)



def stage_attention_inputs(nc, g, ins):
    with ExitStack() as c:
        sb = lambda name, shape, dt=F32: c.enter_context(nc.sbuf_tensor(name, shape, dt))
        sem = lambda name: new_sem(nc, c, name)
        w = sb("a0_w", [F, 4, F])
        fc = sb("a0_fc", [F, 2 * F])
        prod = sb("a0_prod", [F, 4, F])
        loaded, steps, zeroed = sem("a0_loaded"), sem("a0_steps"), sem("a0_zeroed")
        full = (NB - 1) * P
        with nc.Block() as block:
            @block.gpsimd
            def _(pool):
                nc.gpsimd.memset(g.x[:], 0.0).then_inc(zeroed, 1)

            @block.sync
            def _(sp):
                sp.dma_start(w[:], ins["L0_gnn_w"].rearrange("h f o -> f h o")).then_inc(loaded, 16)
                sp.dma_start(fc[:], ins["L0_gnn_fc_w"].to_broadcast([F, 2 * F])).then_inc(loaded, 16)
                sp.wait_ge(zeroed, 1)
                sp.dma_start(g.x[:, 0:NB - 1, :], ins["x"][0:full, :].rearrange("(b p) f -> p b f", p=P)).then_inc(loaded, 16)
                sp.dma_start(g.x[0:N - full, NB - 1, :], ins["x"][full:N, :]).then_inc(loaded, 16)
                sp.wait_ge(loaded, 64)

            @block.vector
            def _(dve):
                ch = Chain(dve, steps)
                dve.wait_ge(loaded, 64)
                for half in range(2):
                    ch.step(nc.vector.tensor_mul(prod[:], w[:], fc[:, half * F:(half + 1) * F].unsqueeze(1).to_broadcast([F, 4, F])))
                    ch.step(nc.vector.tensor_reduce(g.att_w[:, half * 4:half * 4 + 4], prod[:], AX.X, ALU.add))


def stage_attention_tables(nc, g, ins):
    with ExitStack() as c:
        sb = lambda name, shape, dt=F32: c.enter_context(nc.sbuf_tensor(name, shape, dt))
        sem = lambda name: new_sem(nc, c, name)
        row = sb("a1_row", [P, NB, FAR])
        near = g.near
        off = sb("a1_off", [P, NB])
        fc_b = sb("a1_fc_b", [P, 1])
        loaded, steps, made, stored = sem("a1_loaded"), sem("a1_steps"), sem("a1_made"), sem("a1_stored")
        with nc.Block() as block:
            @block.sync
            def _(sp):
                sp.dma_start(fc_b[:], ins["L0_gnn_fc_b"].rearrange("(a b) -> a b", a=1).to_broadcast([P, 1])).then_inc(loaded, 16)
                sp.wait_ge(made, 1)
                sp.dma_start(node_rows(g.att_table), row[:]).then_inc(stored, 16)
                sp.dma_start(node_rows(g.near_table), near[:]).then_inc(stored, 16)
                sp.wait_ge(stored, 32)

            @block.vector
            def _(dve):
                ch = Chain(dve, steps)
                nc.vector.tensor_copy(row[:, :, 0:F], g.h[:])
                nc.vector.tensor_copy(row[:, :, F], g.valid[:])
                nc.vector.tensor_copy(row[:, :, F + 5:FAR], g.spline_h[:])
                ch.step(nc.vector.tensor_scalar(off[:], g.valid[:], BIG, -BIG, ALU.mult, ALU.add))
                ch.step(nc.vector.tensor_add(row[:, :, F + 1:F + 5], g.att[:, :, 4:8], off[:].unsqueeze(2).to_broadcast([P, NB, 4])))
                dve.wait_ge(loaded, 16)
                nc.vector.tensor_scalar(near[:], g.att[:, :, 0:4], fc_b[:], None, ALU.add).then_inc(made, 1)


def stage_attention(nc, g):
    o = g.R
    C8, S, V = o.per_tile, o.chunk, o.vb
    W, parts = 4 * (F + 1), V // P
    with ExitStack() as c:
        sb = lambda name, shape, dt=F32: c.enter_context(nc.sbuf_tensor(f"at_{name}", shape, dt))
        ps = lambda name, shape: c.enter_context(nc.psum_tensor(f"at_{name}", shape, F32))
        sem = lambda name: new_sem(nc, c, f"at_{name}")
        two = range(2)
        rec = [sb(f"rec{b}", [P, TB, o.words], I32) for b in two]
        far = [sb(f"far{b}", [P, TB, FAR]) for b in two]
        near = [sb(f"near{b}", [P, C8]) for b in two]
        score = sb("score", [P, C8, S])
        leaky = sb("leaky", [P, C8, S])
        shifted = sb("shifted", [P, C8, S])
        top = [sb(f"top{b}", [P, C8]) for b in two]
        prob = sb("prob", [P, P])
        term = sb("term", [P, 4, TB])
        spread = sb("spread", [P, TB, 4, C8])
        sums = [sb(f"sums{b}", [F + 1, 4, TB, C8]) for b in two]
        line, keep = ([sb(f"{n}{b}", [4, V]) for b in two] for n in ("line", "keep"))
        upto, fade = ([sb(f"{n}{b}", [4, V]) for b in two] for n in ("upto", "fade"))
        factor, decay, run = ([sb(f"{n}{b}", [F + 1, 4, V]) for b in two] for n in ("factor", "decay", "run"))
        rows = [sb(f"rows{b}", [P, parts, W]) for b in two]
        ps_rows = ps("ps_rows", [P, parts, 256])
        ps_far, ps_prob = ps("ps_far", [P, C8, S]), ps("ps_prob", [P, 4, TB])
        ps_sum = [ps(f"ps_sum{k}", [F + 1, TB // 2, 4, C8]) for k in two]
        rec_in, near_in = [sem(f"rec_in{b}") for b in two], [sem(f"near_in{b}") for b in two]
        far_in = [rows_sem(nc, f"at_far_in{b}") for b in two]
        stored = [sem(f"stored{b}") for b in two]
        top_out, line_in, factors_out, factors_in, rows_out = (
            [sem(f"{n}{b}") for b in two] for n in ("top_out", "line_in", "factors_out", "factors_in", "rows_out"))
        differences, exps, made, scanned, rows_turned, rows_copied, seen = (
            sem(n) for n in ("differences", "exps", "made", "scanned", "rows_turned", "rows_copied", "seen"))
        steps, taken, terms = sem("steps"), sem("taken"), sem("terms")
        turned, shifts, probs, turned_back, spreads, summed, copied = (
            sem(n) for n in ("turned", "shifts", "probs", "turned_back", "spreads", "summed", "copied"))
        rec_v = o.rec.rearrange("(p t) w -> p t w", p=P)
        near_v = g.near_chunk.rearrange("(t c) h -> h t c", c=C8)
        with nc.Block() as block:
            @block.sync
            def _(sp):
                def load(n, b):
                    sp.dma_start(rec[b][:], rec_v[:, bass.ds(n * TB, TB), :]).then_inc(rec_in[b], 16)
                    for h in range(4):
                        sp.dma_start(near[b][h * TB:(h + 1) * TB, :], near_v[h, bass.ds(n * TB, TB), :],
                                     allow_slow_non_contiguous=True).then_inc(near_in[b], 16)

                for b in two:
                    load(b, b)
                def store(n, b, turn):
                    sp.wait_ge(far_in[b], turn * (16 * TB) + 16 * TB)
                    sp.dma_start(g.far_64[:, bass.ds(n * TB, TB), :], far[b][:, :, F + 5:FAR]).then_inc(stored[b], 16)

                def factors(n, b, turn):
                    cols = bass.ds(n * V, V)
                    sp.wait_ge(top_out[b], turn * 64 + 128)
                    sp.dma_start(line[b][:], g.top[:, cols]).then_inc(line_in[b], 16)
                    sp.dma_start(keep[b][:], o.keep[cols].rearrange("(a v) -> a v", a=1).to_broadcast([4, V])).then_inc(line_in[b], 16)
                    sp.wait_ge(made, n + 1)
                    sp.dma_start(g.factor[:, cols], line[b][:]).then_inc(factors_out[b], 16)
                    sp.dma_start(g.decay[:, cols], fade[b][:]).then_inc(factors_out[b], 16)
                    sp.wait_ge(factors_out[b], turn * 32 + 32)
                    for src, to in ((g.factor, factor), (g.decay, decay)):
                        sp.dma_start(to[b][:], src[:, cols].unsqueeze(0).to_broadcast([F + 1, 4, V])).then_inc(factors_in[b], 16)

                with sp.Fori(0, o.pairs - 1) as i:
                    for b in two:
                        store(i * 2 + b, b, i)
                        factors(i * 2 + b, b, i)
                        sp.wait_ge(summed, i * 2 + (b + 2))
                        sp.wait_ge(stored[b], i * 16 + 16)
                        load(i * 2 + (b + 2), b)
                for b in two:
                    store(o.blocks - 2 + b, b, o.pairs - 1)
                    factors(o.blocks - 2 + b, b, o.pairs - 1)
                for b in two:
                    sp.wait_ge(stored[b], 16 * o.pairs)

            @block.gpsimd
            def _(pool):
                with pool.Fori(0, o.pairs) as i:
                    for b in two:
                        pool.wait_ge(rec_in[b], i * 16 + 16)
                        pool.sem_inc(taken, 1)
                        for t in range(TB):
                            pool.indirect_dma_start(out=far[b][:, t, :], out_offset=None, in_=g.att_table[:, :],
                                                    in_offset=bass.IndirectOffsetOnAxis(ap=rec[b][:, t, 0:1], axis=0)).then_inc(far_in[b], 16)

            @block.tensor
            def _(pe):
                pe.sem_inc(summed, 1)
                pe.sem_inc(turned, 1)
                pe.sem_inc(turned_back, 1)
                pe.sem_inc(rows_turned, 1)

                def turn_rows(n, b):
                    pe.wait_ge(scanned, n + 1)
                    pe.wait_ge(rows_copied, n + 1)
                    pe.sem_inc(seen, 1)
                    for q in range(parts):
                        for h in range(4):
                            last = nc.tensor.transpose(ps_rows[:, q, h * (F + 1):(h + 1) * (F + 1)],
                                                       run[b][:, h, q * P:(q + 1) * P], g.ident[0:F + 1, 0:F + 1])
                    last.then_inc(rows_turned, 1)

                def pair(i, first):
                    for b in two:
                        n = i * 2 + b
                        pe.wait_ge(terms, n + 1)
                        pe.wait_ge(shifts, n + 1)
                        nc.tensor.transpose(ps_far[:].rearrange("p c s -> p (c s)"),
                                            term[:].rearrange("p h t -> p (h t)"), g.ident[:]).then_inc(turned, 1)
                        pe.wait_ge(probs, n + 2)
                        nc.tensor.transpose(ps_prob[:].rearrange("p h t -> p (h t)"), prob[:], g.ident[:]).then_inc(turned_back, 1)
                        pe.wait_ge(spreads, n + 1)
                        pe.wait_ge(copied, n + 1)
                        for t in range(TB):
                            last = nc.tensor.matmul(ps_sum[t // (TB // 2)][:, t % (TB // 2), :, :], far[b][:, t, 0:F + 1],
                                                    spread[:, t, :, :], start=True, stop=True)
                        last.then_inc(summed, 1)
                        if not (first and b == 0):
                            turn_rows(n - 1, 1 - b)

                pair(0, True)
                with pe.Fori(1, o.pairs) as i:
                    pair(i, False)
                turn_rows(o.blocks - 1, 1)

            @block.vector
            def _(dve):
                dve.sem_inc(shifts, 1)
                ch = Chain(dve, steps)

                def join(n, b, turn, first):
                    dve.wait_ge(factors_in[b], turn * 32 + 32)
                    dve.wait_ge(copied, n + 2)
                    ch.step(nc.vector.tensor_mul(sums[b][:].rearrange("f h t c -> f h (t c)"),
                                                 sums[b][:].rearrange("f h t c -> f h (t c)"), factor[b][:]))
                    if not first:
                        dve.wait_ge(rows_turned, n)
                    for h in range(4):
                        ch.put(nc.vector.tensor_tensor_scan(run[b][:, h, :], decay[b][:, h, :],
                                                            sums[b][:, h, :, :].rearrange("f t c -> f (t c)"),
                                                            run[1 - b][:, h, V - 1:V], ALU.mult, ALU.add))
                    ch.wait()
                    dve.sem_inc(scanned, 1)

                def factors(n, b, turn):
                    dve.wait_ge(line_in[b], turn * 32 + 32)
                    ch.step(nc.vector.tensor_scalar(fade[b][:], keep[b][:], 1.0e38, -1.0e38, ALU.mult, ALU.add))
                    ch.step(nc.vector.tensor_tensor_scan(upto[b][:], fade[b][:], line[b][:], upto[1 - b][:, V - 1:V], ALU.add, ALU.max))
                    nc.vector.tensor_sub(line[b][:], line[b][:], upto[b][:]).then_inc(differences, 1)
                    ch.put(nc.vector.tensor_sub(fade[b][:, 0:1], upto[1 - b][:, V - 1:V], upto[b][:, 0:1]))
                    ch.step(nc.vector.tensor_sub(fade[b][:, 1:V], upto[b][:, 0:V - 1], upto[b][:, 1:V]))
                    nc.vector.tensor_scalar(fade[b][:], fade[b][:], 0.0, None, ALU.min).then_inc(differences, 1)
                    dve.wait_ge(exps, n * 2 + 2)
                    nc.vector.tensor_mul(fade[b][:], fade[b][:], keep[b][:]).then_inc(made, 1)

                ch.put(nc.vector.memset(run[1][:], 0.0))
                ch.step(nc.vector.memset(upto[1][:], 0.0))

                def pair(i, first):
                    for b in two:
                        n = i * 2 + b
                        dve.wait_ge(turned, n + 2)
                        dve.wait_ge(near_in[b], i * 64 + 64)
                        ch.step(nc.vector.tensor_add(score[:], ps_far[:], near[b][:].unsqueeze(2).to_broadcast([P, C8, S])))
                        ch.step(nc.vector.scalar_tensor_tensor(leaky[:], score[:], 0.2, score[:], ALU.mult, ALU.max))
                        dve.wait_ge(top_out[b], i * 64 + 64)
                        ch.step(nc.vector.tensor_reduce(top[b][:], leaky[:], AX.X, ALU.max))
                        dve.wait_ge(probs, n + 1)
                        nc.vector.tensor_sub(shifted[:], leaky[:], top[b][:].unsqueeze(2).to_broadcast([P, C8, S])).then_inc(shifts, 1)
                        dve.wait_ge(turned_back, n + 2)
                        dve.wait_ge(summed, n + 1)
                        nc.vector.tensor_mul(spread[:], ps_prob[:].rearrange("p h t -> p t h").unsqueeze(3).to_broadcast([P, TB, 4, C8]),
                                             o.mask[:].unsqueeze(1).unsqueeze(1).to_broadcast([P, TB, 4, C8])).then_inc(spreads, 1)
                        if not (first and b == 0):
                            join(n - 1, 1 - b, i + (b - 1), first)
                        factors(n, b, i)

                pair(0, True)
                with dve.Fori(1, o.pairs) as i:
                    ch.restart()
                    pair(i, False)
                ch.restart()
                join(o.blocks - 1, 1, o.pairs - 1, False)

            @block.scalar
            def _(act):
                act.sem_inc(copied, 1)
                act.sem_inc(probs, 1)
                act.sem_inc(rows_copied, 1)
                for b in two:
                    act.sem_inc(top_out[b], 64)
                    act.sem_inc(rows_out[b], 16)

                def store_rows(n, b, turn):
                    act.wait_ge(rows_turned, n + 2)
                    act.wait_ge(rows_out[b], turn * 16 + 16)
                    nc.scalar.copy(rows[b][:], ps_rows[:, :, 0:W]).then_inc(rows_copied, 1)
                    act.wait_ge(rows_copied, n + 2)
                    act.dma_start(g.att_sums[bass.ds(n * V, V), :].rearrange("(q p) w -> p q w", p=P), rows[b][:]).then_inc(rows_out[b], 16)

                def pair(i, first):
                    for b in two:
                        n = i * 2 + b
                        act.wait_ge(far_in[b], i * (16 * TB) + 16 * TB)
                        act.wait_ge(turned, n + 1)
                        nc.scalar.copy(term[:], far[b][:, :, F + 1:F + 5].rearrange("p t h -> p h t")).then_inc(terms, 1)
                        act.wait_ge(shifts, n + 2)
                        act.wait_ge(turned_back, n + 1)
                        nc.scalar.activation(prob[:], shifted[:].rearrange("p c s -> p (c s)"), ACT.Exp).then_inc(probs, 1)
                        for h in range(4):
                            act.dma_start(g.top[h, bass.ds(n * o.vb, o.vb)].rearrange("(t c) -> t c", c=C8),
                                          top[b][h * TB:(h + 1) * TB, :]).then_inc(top_out[b], 16)
                        for k, exponent in enumerate((line[b], fade[b])):
                            act.wait_ge(differences, n * 2 + (k + 1))
                            nc.scalar.activation(exponent[:], exponent[:], ACT.Exp).then_inc(exps, 1)
                        act.wait_ge(summed, n + 2)
                        if not first:
                            act.wait_ge(scanned, n - 1)
                        for k in two:
                            half = slice(k * (TB // 2), (k + 1) * (TB // 2))
                            last = nc.scalar.copy(sums[b][:, :, half, :].rearrange("f h t c -> f t h c"), ps_sum[k][:])
                        last.then_inc(copied, 1)
                        if not (first and b == 0):
                            store_rows(n - 1, 1 - b, i + (b - 1))

                pair(0, True)
                with act.Fori(1, o.pairs) as i:
                    pair(i, False)
                store_rows(o.blocks - 1, 1, o.pairs - 1)
                for b in two:
                    act.wait_ge(rows_out[b], 16 * o.pairs + 16)
                    act.wait_ge(top_out[b], 64 * o.pairs + 64)


def stage_attention_mean(nc, g, got, normed):
    with ExitStack() as c:
        weight = c.enter_context(nc.sbuf_tensor("am_weight", [P, NB, 4], F32))
        steps = new_sem(nc, c, "am_steps")
        with nc.Block() as block:
            @block.vector
            def _(dve):
                ch = Chain(dve, steps)
                v = got[:].rearrange("p b (h f) -> p b h f", f=F + 1)
                ch.step(nc.vector.tensor_scalar(weight[:], v[:, :, :, F], 1e-30, None, ALU.max))
                ch.step(nc.vector.reciprocal(weight[:], weight[:]))
                ch.step(nc.vector.tensor_mul(normed[:].rearrange("p b (h f) -> p b h f", f=F), v[:, :, :, 0:F],
                                             weight[:].unsqueeze(3).to_broadcast([P, NB, 4, F])))



class Spline:
    def __init__(self, nc, c, g, name, fin, fout, sums, stored=None, near=None):
        o = g.R
        self.nc, self.g, self.o, self.fin, self.fout, self.sums = nc, g, o, fin, fout, sums
        self.stored, self.near = stored, near
        self.C8, self.V = o.per_tile, o.vb
        self.K, self.J = (125, fin) if fin > 1 else (25, 5)
        self.parts = self.V // P
        self.XT = 4 if fin > 1 else TB
        self.XS = TB // self.XT
        self.HT = TB // 2
        self.bufs = 2 if near is not None else 1
        width = fin + 3 if near is not None else fin
        sb = lambda nm, shape, dt=F32: c.enter_context(nc.sbuf_tensor(f"{name}_{nm}", shape, dt))
        sem = lambda nm: new_sem(nc, c, f"{name}_{nm}")
        K, J, C8, V = self.K, self.J, self.C8, self.V
        self.w = sb("w", [K, J, fout])
        self.rec = [sb(f"rec{b}", [P, TB, o.words], I32) for b in range(self.bufs)]
        self.far = [sb(f"far{b}", [P, TB, width]) for b in range(self.bufs)]
        self.shift = [sb(f"shift{b}", [C8, TB, 3]) for b in range(self.bufs)] if near is not None else []
        self.keep = sb("keep", [fout, V])
        self.pos = sb("pos", [P, TB, 3])
        self.up, self.down = sb("up", [P, TB * 3, 5]), sb("down", [P, TB * 3, 5])
        self.pair = sb("pair", [P, TB, 25]) if fin > 1 else None
        self.basis = [sb(f"basis{k}", [P, self.HT, K]) for k in range(2)]
        self.third = sb("third", [P, TB, 5]) if fin == 1 else None
        self.lows, self.highs, self.floor, self.roof = (sb(n, [P, 5]) for n in ("lows", "highs", "floor", "roof"))
        self.spread_to = [sb(f"spread{k}", [P, self.XT, J, C8]) for k in range(2 if fin > 1 else 1)]
        self.outer = sb("outer", [K, J, V])
        self.run, self.carry = sb("run", [fout, V]), sb("carry", [fout, 1])
        self.rows = sb("rows", [P, self.parts, fout])
        if near is not None:
            self.gathered = [rows_sem(nc, f"{name}_gathered{b}") for b in range(2)]
        self.loaded = [sem(f"loaded{b}") for b in range(self.bufs)]
        self.loads = 16 * (1 + (stored is not None) + (near is not None))
        self.const, self.keep_in, self.out = sem("const"), sem("keep_in"), sem("out")
        self.shifts, self.positions, self.bases, self.spreads = sem("shifts"), sem("positions"), sem("bases"), sem("spreads")
        self.products, self.outers, self.made, self.scanned = sem("products"), sem("outers"), sem("made"), sem("scanned")
        self.turned, self.copied, self.seen = sem("turned"), sem("copied"), sem("seen")
        self.rec_v = o.rec.rearrange("(p t) w -> p t w", p=P)
        self.keep_v = o.keep.rearrange("(a v) -> a v", a=1)

    def banks(self, c, name):
        ps = lambda nm, shape: c.enter_context(self.nc.psum_tensor(f"{name}_{nm}", shape, F32))
        if self.fin > 1:
            self.ps_outer = [ps(f"ps_outer{k}", [self.K, self.fin, self.C8]) for k in range(3)]
        else:
            self.bank = 512 // (self.J * self.C8)
            self.ps_outer = [ps(f"ps_outer{k}", [self.K, min(self.bank, TB - t), self.J, self.C8])
                             for k, t in enumerate(range(0, TB, self.bank))]
        self.ps_out = ps("ps_out", [self.fout, self.V])
        self.ps_by_chunk = ps("ps_by_chunk", [P, self.parts, self.fout])
        if self.near is not None:
            self.ps_shift = ps("ps_shift", [P, TB, 3])


    def begin_sync(self, sp, weights):
        sp.dma_start(self.w[:], weights).then_inc(self.const, 16)

    def load(self, sp, m, b):
        sp.dma_start(self.rec[b][:], self.rec_v[:, bass.ds(m * TB, TB), :]).then_inc(self.loaded[b], 16)
        if self.stored is not None:
            sp.dma_start(self.far[b][:], self.stored[:, bass.ds(m * TB, TB), :]).then_inc(self.loaded[b], 16)
        if self.near is not None:
            sp.dma_start(self.shift[b][:], self.near[bass.ds(m * self.V, self.V), :].rearrange("(t c) d -> c t d", c=self.C8)).then_inc(self.loaded[b], 16)


    def begin_vector(self, dve, ch):
        nc = self.nc
        ends = 3.0e38
        for k, (lo, hi) in enumerate(((ends, 0.0), (-ends, 0.0), (0.0, 0.0), (0.0, -ends), (0.0, ends))):
            nc.vector.memset(self.lows[:, k:k + 1], float(k - 1))
            nc.vector.memset(self.highs[:, k:k + 1], float(k + 1))
            nc.vector.memset(self.floor[:, k:k + 1], lo)
            nc.vector.memset(self.roof[:, k:k + 1], hi)
        ch.step(nc.vector.memset(self.carry[:], 0.0))
        dve.sem_inc(self.scanned, 1)
        dve.sem_inc(self.positions, 1)
        dve.sem_inc(self.spreads, 1)

    def points(self, dve, ch, m, b, turn, first=False):
        nc, far = self.nc, self.far[b]
        dve.wait_ge(self.loaded[b], turn * self.loads + self.loads)
        pseudo = self.rec[b][:, :, 1:4].bitcast(F32)
        if self.near is not None:
            dve.wait_ge(self.shifts, m + 1)
            dve.wait_ge(self.gathered[b], turn * (16 * TB) + 16 * TB)
            ch.step(nc.vector.tensor_add(self.pos[:], pseudo, far[:, :, self.fin:self.fin + 3]))
            nc.vector.tensor_sub(self.pos[:], self.pos[:], self.ps_shift[:]).then_inc(self.positions, 1)
            dve.wait_ge(self.positions, m + 2)
            ch.step(nc.vector.tensor_scalar(self.pos[:], self.pos[:], 0.0, 1.0, ALU.max, ALU.min))
            ch.step(nc.vector.tensor_scalar(self.pos[:], self.pos[:], 4.0, None, ALU.mult))
        else:
            ch.step(nc.vector.tensor_scalar(self.pos[:], pseudo, 4.0, None, ALU.mult))
        b5, b55, b255 = [P, TB * 3, 5], [P, TB, 5, 5], [P, self.HT, 25, 5]
        wide = lambda ap: ap.unsqueeze(1).to_broadcast(b5)
        x = self.pos[:].rearrange("p t d -> p (t d)").unsqueeze(2).to_broadcast(b5)
        up, down = self.up, self.down
        ch.put(nc.vector.tensor_sub(up[:], x, wide(self.lows[:])))
        ch.step(nc.vector.tensor_sub(down[:], wide(self.highs[:]), x))
        ch.put(nc.vector.tensor_tensor(up[:], up[:], wide(self.floor[:]), ALU.max))
        ch.step(nc.vector.tensor_tensor(down[:], down[:], wide(self.roof[:]), ALU.max))
        ch.step(nc.vector.tensor_tensor(up[:], up[:], down[:], ALU.min))
        v = up[:].rearrange("p (t d) k -> p t d k", d=3)
        if self.fin > 1:
            ch.step(nc.vector.tensor_mul(self.pair[:].rearrange("p t (a b) -> p t a b", a=5),
                                         v[:, :, 0, :].unsqueeze(3).to_broadcast(b55), v[:, :, 1, :].unsqueeze(2).to_broadcast(b55)))
        for k in range(2):
            if k == 1 or not first:
                dve.wait_ge(self.products, m * TB + (1 - (1 - k) * self.HT))
            ts = slice(k * self.HT, (k + 1) * self.HT)
            if self.fin > 1:
                nc.vector.tensor_mul(self.basis[k][:].rearrange("p t (a b) -> p t a b", b=5),
                                     self.pair[:, ts, :].unsqueeze(3).to_broadcast(b255),
                                     v[:, ts, 2, :].unsqueeze(2).to_broadcast(b255)).then_inc(self.bases, 1)
            else:
                nc.vector.tensor_mul(self.basis[k][:].rearrange("p t (a b) -> p t a b", a=5),
                                     v[:, ts, 0, :].unsqueeze(3).to_broadcast([P, self.HT, 5, 5]),
                                     v[:, ts, 1, :].unsqueeze(2).to_broadcast([P, self.HT, 5, 5])).then_inc(self.bases, 1)
        if self.fin == 1:
            ch.step(nc.vector.tensor_scalar(far[:, :, 0], self.rec[b][:, :, 0], float(N), None, ALU.is_lt))
            ch.step(nc.vector.tensor_mul(self.third[:], v[:, :, 2, :], far[:].to_broadcast([P, TB, 5])))

    def spread(self, dve, m, b, steps):
        nc = self.nc
        bx = [P, self.XT, self.J, self.C8]
        for s in steps:
            if s >= 2:
                dve.wait_ge(self.products, m * TB + ((s - 1) * self.XT + 1))
            rows = self.third[:] if self.fin == 1 else self.far[b][:, s * self.XT:(s + 1) * self.XT, 0:self.fin]
            nc.vector.tensor_mul(self.spread_to[s % 2][:], rows.unsqueeze(3).to_broadcast(bx),
                                 self.o.mask[:].unsqueeze(1).unsqueeze(1).to_broadcast(bx)).then_inc(self.spreads, 1)

    def scan(self, dve, ch, m):
        nc = self.nc
        dve.wait_ge(self.made, m + 2)
        dve.wait_ge(self.keep_in, m * 16 + 16)
        dve.wait_ge(self.turned, m + 1)
        nc.vector.tensor_tensor_scan(self.run[:], self.keep[:], self.ps_out[:], self.carry[:], ALU.mult, ALU.add).then_inc(self.scanned, 1)
        dve.wait_ge(self.scanned, m + 2)
        ch.step(nc.vector.tensor_copy(self.carry[:], self.run[:, self.V - 1:self.V]))


    def begin_tensor(self, pe):
        pe.wait_ge(self.const, 16)
        pe.sem_inc(self.products, 1)
        pe.sem_inc(self.made, 1)
        pe.sem_inc(self.turned, 1)

    def near_shifts(self, pe, m, b, turn):
        pe.wait_ge(self.loaded[b], turn * self.loads + self.loads)
        pe.wait_ge(self.positions, m + 1)
        self.nc.tensor.matmul(self.ps_shift[:].rearrange("p t d -> p (t d)"), self.o.mask_t[:],
                              self.shift[b][:].rearrange("c t d -> c (t d)"), start=True, stop=True).then_inc(self.shifts, 1)

    def outer_products(self, pe, m):
        ring = len(self.ps_outer)
        for t in range(TB):
            if t % self.HT == 0:
                pe.wait_ge(self.bases, m * 2 + (t // self.HT + 1))
            if t % self.XT == 0:
                pe.wait_ge(self.spreads, m * self.XS + (t // self.XT + 2))
            if self.fin == 1:
                if t == 0:
                    pe.wait_ge(self.outers, m + 1)
                to = self.ps_outer[t // self.bank][:, t % self.bank, :, :].rearrange("k f c -> k (f c)")
            else:
                if t >= ring:
                    pe.wait_ge(self.outers, m * TB + (t - ring + 2))
                to = self.ps_outer[t % ring][:].rearrange("k f c -> k (f c)")
            self.nc.tensor.matmul(to, self.basis[t // self.HT][:, t % self.HT, :],
                                  self.spread_to[(t // self.XT) % 2][:, t % self.XT, :, :].rearrange("p f c -> p (f c)"),
                                  start=True, stop=True).then_inc(self.products, 1)

    def through_weights(self, pe, m):
        pe.wait_ge(self.outers, m + 2 if self.fin == 1 else m * TB + (TB + 1))
        pe.wait_ge(self.scanned, m + 1)
        for f in range(self.J):
            last = self.nc.tensor.matmul(self.ps_out[:], self.w[:, f, :], self.outer[:, f, :], start=(f == 0), stop=(f == self.J - 1))
        last.then_inc(self.made, 1)

    def turn(self, pe, m):
        pe.wait_ge(self.scanned, m + 2)
        pe.wait_ge(self.copied, m + 1)
        pe.sem_inc(self.seen, 1)
        for q in range(self.parts):
            last = self.nc.tensor.transpose(self.ps_by_chunk[:, q, :], self.run[:, q * P:(q + 1) * P], self.g.ident[0:self.fout, 0:self.fout])
        last.then_inc(self.turned, 1)


    def load_marks(self, act, m):
        act.dma_start(self.keep[:], self.keep_v[:, bass.ds(m * self.V, self.V)].to_broadcast([self.fout, self.V])).then_inc(self.keep_in, 16)

    def begin_scalar(self, act):
        self.load_marks(act, 0)
        act.sem_inc(self.outers, 1)
        act.sem_inc(self.copied, 1)
        act.sem_inc(self.out, 16)

    def copy_products(self, act, m):
        act.wait_ge(self.made, m + 1)
        if self.fin == 1:
            act.wait_ge(self.products, m * TB + (TB + 1))
            for k, bank in enumerate(self.ps_outer):
                cols = slice(k * self.bank * self.C8, (k * self.bank + bank.shape[1]) * self.C8)
                last = self.nc.scalar.copy(self.outer[:, :, cols].rearrange("k f (t c) -> k t f c", c=self.C8), bank[:])
            last.then_inc(self.outers, 1)
            return
        for t in range(TB):
            act.wait_ge(self.products, m * TB + (t + 2))
            self.nc.scalar.copy(self.outer[:, :, t * self.C8:(t + 1) * self.C8], self.ps_outer[t % len(self.ps_outer)][:]).then_inc(self.outers, 1)

    def store_rows(self, act, m):
        act.wait_ge(self.turned, m + 2)
        act.wait_ge(self.out, m * 16 + 16)
        self.nc.scalar.copy(self.rows[:], self.ps_by_chunk[:]).then_inc(self.copied, 1)
        act.wait_ge(self.copied, m + 2)
        act.dma_start(self.sums[bass.ds(m * self.V, self.V), :].rearrange("(q p) w -> p q w", p=P), self.rows[:]).then_inc(self.out, 16)
        self.load_marks(act, m + 1)

    def end_scalar(self, act):
        act.wait_ge(self.out, 16 * self.o.blocks + 16)
        act.wait_ge(self.keep_in, 16 * self.o.blocks + 16)


def stage_spline_gathered(nc, g, name, weights, fin, fout, sums, table, near):
    with ExitStack() as c:
        sl = Spline(nc, c, g, name, fin, fout, sums, near=near)
        sl.banks(c, name)
        steps, taken = new_sem(nc, c, f"{name}_steps"), new_sem(nc, c, f"{name}_taken")
        o, two = g.R, range(2)
        with nc.Block() as block:
            @block.sync
            def _(sp):
                sl.begin_sync(sp, weights)
                for b in two:
                    sl.load(sp, b, b)
                with sp.Fori(1, o.pairs) as i:
                    for b in two:
                        sp.wait_ge(sl.spreads, i * (2 * sl.XS) + ((b - 1) * sl.XS + 1))
                        sl.load(sp, i * 2 + b, b)

            @block.gpsimd
            def _(pool):
                with pool.Fori(0, o.pairs) as i:
                    for b in two:
                        pool.wait_ge(sl.loaded[b], i * sl.loads + sl.loads)
                        pool.sem_inc(taken, 1)
                        for t in range(TB):
                            pool.indirect_dma_start(out=sl.far[b][:, t, :], out_offset=None, in_=table[:, :],
                                                    in_offset=bass.IndirectOffsetOnAxis(ap=sl.rec[b][:, t, 0:1], axis=0)).then_inc(sl.gathered[b], 16)

            @block.vector
            def _(dve):
                ch = Chain(dve, steps)
                first, rest = range(2), range(2, sl.XS)
                sl.begin_vector(dve, ch)
                sl.points(dve, ch, 0, 0, 0, first=True)
                sl.spread(dve, 0, 0, range(sl.XS))
                sl.points(dve, ch, 1, 1, 0)
                sl.spread(dve, 1, 1, first)
                sl.scan(dve, ch, 0)
                sl.spread(dve, 1, 1, rest)
                with dve.Fori(1, o.pairs) as i:
                    ch.restart()
                    for b in two:
                        n = i * 2 + b
                        sl.points(dve, ch, n, b, i)
                        sl.spread(dve, n, b, first)
                        sl.scan(dve, ch, i * 2 + (b - 1))
                        sl.spread(dve, n, b, rest)
                ch.restart()
                sl.scan(dve, ch, o.blocks - 1)

            @block.tensor
            def _(pe):
                sl.begin_tensor(pe)
                sl.near_shifts(pe, 0, 0, 0)
                sl.outer_products(pe, 0)
                sl.near_shifts(pe, 1, 1, 0)
                sl.through_weights(pe, 0)
                sl.turn(pe, 0)
                with pe.Fori(0, o.pairs - 1) as i:
                    for b in two:
                        sl.outer_products(pe, i * 2 + (b + 1))
                        sl.near_shifts(pe, i * 2 + (b + 2), b, i + 1)
                        sl.through_weights(pe, i * 2 + (b + 1))
                        sl.turn(pe, i * 2 + (b + 1))
                sl.outer_products(pe, o.blocks - 1)
                sl.through_weights(pe, o.blocks - 1)
                sl.turn(pe, o.blocks - 1)

            @block.scalar
            def _(act):
                sl.begin_scalar(act)
                with act.Fori(0, o.blocks) as n:
                    sl.copy_products(act, n)
                    sl.store_rows(act, n)
                sl.end_scalar(act)



def stage_aggregate(nc, g, name, table, sums, gauss=None, sl=None, sl_from=0, sl_count=0, sl_weights=None):
    o = g.D
    Q = QUARTERS
    GT = o.block_tiles // Q
    V = GT * o.per_tile
    parts = V // P
    width = 3 * F if gauss is not None else F
    per = o.tiles // Q
    with ExitStack() as c:
        sb = lambda nm, shape, dt=F32: c.enter_context(nc.sbuf_tensor(f"{name}_{nm}", shape, dt))
        ps = lambda nm, shape: c.enter_context(nc.psum_tensor(f"{name}_{nm}", shape, F32))
        sem = lambda nm: new_sem(nc, c, f"{name}_{nm}")
        two = range(2)
        rec = [sb(f"rec{b}", [P, Q, GT, o.words], I32) for b in two]
        keep = [sb(f"keep{b}", [Q * F, V]) for b in two]
        got = [sb(f"got{b}", [P, GT, Q, width]) for b in two]
        mixed = [sb(f"mixed{b}", [P, GT, Q, F]) for b in two] if gauss is not None else got
        run = [sb(f"run{b}", [Q * F, V]) for b in two]
        rows = [sb(f"rows{b}", [P, parts, Q * F]) for b in two]
        ps_sum = [ps(f"ps_sum{b}", [Q * F, V]) for b in two]
        ps_rows = ps("ps_rows", [P, parts, Q * F])
        loaded, out = ([sem(f"{n}{b}") for b in two] for n in ("loaded", "out"))
        gathered = [rows_sem(nc, f"{name}_gathered{b}") for b in two]
        steps, taken, seen = sem("steps"), sem("taken"), sem("seen")
        mixes, summed, scanned, turned, copied = (sem(n) for n in ("mixes", "summed", "scanned", "turned", "copied"))
        rec_v = o.rec.rearrange("(p q t) w -> p q t w", p=P, q=Q)
        loads = 16 * (1 + Q)
        sl.banks(c, f"{name}_sl")
        with nc.Block() as block:
            @block.sync
            def _(sp):
                def load(n, b):
                    sp.dma_start(rec[b][:].rearrange("p q t w -> p q (t w)"),
                                 rec_v[:, :, bass.ds(n * GT, GT), :].rearrange("p q t w -> p q (t w)")).then_inc(loaded[b], 16)
                    for q in range(Q):
                        marks = o.keep[bass.ds(n * V + q * (o.chunks // Q), V)]
                        sp.dma_start(keep[b][q * F:(q + 1) * F, :], marks.rearrange("(a v) -> a v", a=1).to_broadcast([F, V])).then_inc(loaded[b], 16)

                def next_pair(i):
                    for b in two:
                        sp.wait_ge(scanned, i * 2 + b)
                        load(i * 2 + b, b)

                for b in two:
                    load(b, b)
                if sl_count:
                    if sl_from == 0:
                        sl.begin_sync(sp, sl_weights)
                        sl.load(sp, 0, 0)
                    else:
                        sl.load(sp, sl_from, 0)
                    with sp.Fori(1, sl_count) as i:
                        sp.wait_ge(sl.spreads, i * sl.XS + (sl_from * sl.XS + 1))
                        sl.load(sp, i + sl_from, 0)
                        next_pair(i)
                if max(sl_count, 1) < o.pairs:
                    with sp.Fori(max(sl_count, 1), o.pairs) as i:
                        next_pair(i)

            @block.gpsimd
            def _(pool):
                with pool.Fori(0, o.pairs) as i:
                    for b in two:
                        pool.wait_ge(loaded[b], i * loads + loads)
                        pool.sem_inc(taken, 1)
                        for t in range(GT):
                            for q in range(Q):
                                pool.indirect_dma_start(out=got[b][:, t, q, :], out_offset=None, in_=table[:, :],
                                                        in_offset=bass.IndirectOffsetOnAxis(ap=rec[b][:, q, t, 0:1], axis=0)).then_inc(gathered[b], 16)

            @block.tensor
            def _(pe):
                def products(i, b):
                    if gauss is not None:
                        pe.wait_ge(mixes, i * 2 + (b + 1))
                    else:
                        pe.wait_ge(gathered[b], i * (16 * o.block_tiles) + 16 * o.block_tiles)
                    pe.wait_ge(scanned, i * 2 + 1)
                    for t in range(GT):
                        last = nc.tensor.matmul(ps_sum[b][:, t * o.per_tile:(t + 1) * o.per_tile],
                                                mixed[b][:, t, :, :].rearrange("p q f -> p (q f)"), o.mask[:], start=True, stop=True)
                    last.then_inc(summed, 1)

                def transposes(i, b):
                    pe.wait_ge(scanned, i * 2 + (b + 2))
                    pe.wait_ge(copied, i * 2 + (b + 1))
                    pe.sem_inc(seen, 1)
                    for k in range(parts):
                        last = nc.tensor.transpose(ps_rows[:, k, :], run[b][:, k * P:(k + 1) * P], g.ident[:])
                    last.then_inc(turned, 1)

                pe.sem_inc(turned, 1)
                if sl_count:
                    if sl_from == 0:
                        sl.begin_tensor(pe)
                    with pe.Fori(0, sl_count) as i:
                        sl.outer_products(pe, i + sl_from)
                        products(i, 0)
                        sl.through_weights(pe, i + sl_from)
                        transposes(i, 0)
                        sl.turn(pe, i + sl_from)
                        products(i, 1)
                        transposes(i, 1)
                if sl_count < o.pairs:
                    with pe.Fori(sl_count, o.pairs) as i:
                        for b in two:
                            products(i, b)
                            transposes(i, b)

            @block.vector
            def _(dve):
                ch = Chain(dve, steps)

                def mix(i, b):
                    if gauss is not None:
                        dve.wait_ge(gathered[b], i * (16 * o.block_tiles) + 16 * o.block_tiles)
                        rows3 = got[b][:].rearrange("p t q (k f) -> p (t q) k f", k=3)
                        by = gauss[:, bass.ds(i * (2 * GT) + b * GT, GT), :, :].rearrange("p t q k -> p (t q) k")
                        ch.step(nc.vector.tensor_mul(rows3, rows3, by.unsqueeze(3).to_broadcast([P, o.block_tiles, 3, F])))
                        to = mixed[b][:].rearrange("p t q f -> p (t q) f")
                        ch.step(nc.vector.tensor_add(to, rows3[:, :, 0, :], rows3[:, :, 1, :]))
                        nc.vector.tensor_add(to, to, rows3[:, :, 2, :]).then_inc(mixes, 1)

                def sums_of(i, b):
                    dve.wait_ge(summed, i * 2 + (b + 1))
                    dve.wait_ge(loaded[b], i * loads + loads)
                    dve.wait_ge(turned, i * 2 + 1)
                    nc.vector.tensor_tensor_scan(run[b][:], keep[b][:], ps_sum[b][:], run[1 - b][:, V - 1:V],
                                                 ALU.mult, ALU.add).then_inc(scanned, 1)
                    dve.wait_ge(scanned, i * 2 + (b + 2))

                ch.step(nc.vector.memset(run[1][:], 0.0))
                dve.sem_inc(scanned, 1)
                if sl_count:
                    first, rest = range(2), range(2, sl.XS)
                    if sl_from == 0:
                        sl.begin_vector(dve, ch)
                    sl.points(dve, ch, sl_from, 0, sl_from, first=sl_from == 0)
                    sl.spread(dve, sl_from, 0, range(sl.XS))
                    mix(0, 0)
                    sums_of(0, 0)
                    with dve.Fori(1, sl_count) as i:
                        ch.restart()
                        m = i + sl_from
                        sl.points(dve, ch, m, 0, m)
                        sl.spread(dve, m, 0, first)
                        mix(i - 1, 1)
                        sl.scan(dve, ch, i + (sl_from - 1))
                        sums_of(i - 1, 1)
                        sl.spread(dve, m, 0, rest)
                        mix(i, 0)
                        sums_of(i, 0)
                    ch.restart()
                    mix(sl_count - 1, 1)
                    sl.scan(dve, ch, sl_from + sl_count - 1)
                    sums_of(sl_count - 1, 1)
                if sl_count < o.pairs:
                    with dve.Fori(sl_count, o.pairs) as i:
                        ch.restart()
                        for b in two:
                            mix(i, b)
                            sums_of(i, b)

            @block.scalar
            def _(act):
                def store(i, b):
                    act.wait_ge(turned, i * 2 + (b + 2))
                    act.wait_ge(out[b], i * 16 + 16)
                    nc.scalar.copy(rows[b][:], ps_rows[:]).then_inc(copied, 1)
                    act.wait_ge(copied, i * 2 + (b + 2))
                    act.dma_start(sums.rearrange("(v q) f -> v (q f)", q=Q)[bass.ds(i * (2 * V) + b * V, V), :]
                                  .rearrange("(k p) w -> p k w", p=P), rows[b][:]).then_inc(out[b], 16)

                act.sem_inc(copied, 1)
                for b in two:
                    act.sem_inc(out[b], 16)
                if sl_count:
                    if sl_from == 0:
                        sl.begin_scalar(act)
                    with act.Fori(0, sl_count) as i:
                        sl.copy_products(act, i + sl_from)
                        store(i, 0)
                        sl.store_rows(act, i + sl_from)
                        store(i, 1)
                if sl_count < o.pairs:
                    with act.Fori(sl_count, o.pairs) as i:
                        for b in two:
                            store(i, b)
                for b in two:
                    act.wait_ge(out[b], 16 * o.pairs + 16)
                if sl_count and sl_from + sl_count == g.R.blocks:
                    sl.end_scalar(act)



def stage_nodes(nc, g, name, rows, work, stores=(), collect=None):
    with ExitStack() as c:
        sem = lambda nm: new_sem(nc, c, f"{name}_{nm}")
        t = NormBuffers(nc, c, name)
        steps, finished, stored, act_in, act_out = (
            sem(n) for n in ("steps", "finished", "stored", "act_in", "act_out"))
        calls = []

        with nc.Block() as block:
            if collect is not None:
                collected = rows_sem(nc, f"{name}_collected")

                @block.gpsimd
                def _(pool):
                    collect_rows(pool, collect[0], collect[1], collect[2], collected, *collect[3:])

            @block.sync
            def _(sp):
                sp.wait_ge(finished, 1)
                for table, tile in stores:
                    sp.dma_start(table, tile).then_inc(stored, 16)
                if stores:
                    sp.wait_ge(stored, 16 * len(stores))

            @block.vector
            def _(dve):
                ch = Chain(dve, steps)

                def act_in_place(ap, func):
                    calls.append((ap, func))
                    dve.sem_inc(act_in, 1)
                    dve.wait_ge(act_out, len(calls))

                work(ch, rows, act_in_place, t)
                dve.sem_inc(finished, 1)

            @block.scalar
            def _(act):
                for k, (ap, func) in enumerate(calls):
                    act.wait_ge(act_in, k + 1)
                    nc.scalar.activation(ap, ap, func).then_inc(act_out, 1)


def layers(nc, g, ins, out):
    bc = lambda ap, width: ap.unsqueeze(1).to_broadcast([P, NB, width])
    per_node = lambda ap, width: ap.unsqueeze(2).to_broadcast([P, NB, width])

    def elu(ch, act, to, tmp):
        ch.step(nc.vector.tensor_scalar(tmp, to, 0.0, None, ALU.min))
        act(tmp, ACT.Exp)
        ch.step(nc.vector.tensor_scalar(tmp, tmp, -1.0, None, ALU.add))
        ch.step(nc.vector.scalar_tensor_tensor(to, to, 0.0, tmp, ALU.max, ALU.add))

    def scope():
        c = ExitStack()
        return c, (lambda name, shape: c.enter_context(nc.sbuf_tensor(name, shape, F32)))

    def spline_mean(ch, to, bias, width):
        ch.step(nc.vector.tensor_mul(to, to, per_node(g.R.inv_degree[:], width)))
        ch.step(nc.vector.tensor_add(to, to, bc(bias, width)))

    c, sb = scope()
    with c:
        g.near = sb("l0_near", [P, NB, 4])
        g.spline_h, tmp = sb("l3_h1", [P, NB, 64]), sb("l3_tmp1", [P, NB, 64])
        stage_chunks(nc, g)
        stage_attention_inputs(nc, g, ins)
        stage_nodes(nc, g, "n_in", [], lambda ch, rows, act, t: layernorm(ch, nc, g, t, g.h[:], act),
                    collect=(g.R, g.sums_r64, g.spline_h))

        def work(ch, rows, act, t):
            spline_mean(ch, g.spline_h[:], rows[0][:], 64)
            elu(ch, act, g.spline_h[:], tmp[:])
            ch.step(nc.vector.tensor_mul(g.spline_h[:], g.spline_h[:], per_node(g.valid[:], 64)))

        stage_nodes(nc, g, "n_p1", [g.bias["L3_gnn_stn1_b"]], work)

        stage_dense(nc, g, "d_att", g.h, F, 8, g.att, [(0, 0, g.att_w[:])])
        stage_attention_tables(nc, g, ins)
        stage_spread(nc, g, "s_near", g.near, g.near_table, 4, g.near_marks, g.near_chunk)
    stage_attention(nc, g)
    c, sb = scope()
    with c:
        got, normed, mean = sb("l0_got", [P, NB, 4 * (F + 1)]), sb("l0_normed", [P, NB, 4 * F]), sb("l0_mean", [P, NB, F])
        stage_collect(nc, g, "c_att", g.R, g.att_sums, got)
        stage_attention_mean(nc, g, got, normed)
        stage_dense(nc, g, "d_l0", normed, 4 * F, F, mean, [(0, 0, ins["L0_gnn_w"].rearrange("h f o -> (h f) o"))])

        def work(ch, rows, act, t):
            ch.step(nc.vector.scalar_tensor_tensor(g.x[:], mean[:], 0.25, g.x[:], ALU.mult, ALU.add))
            ch.step(nc.vector.tensor_add(g.x[:], g.x[:], bc(rows[0][:], F)))
            layernorm(ch, nc, g, t, g.h[:], act)

        stage_nodes(nc, g, "n_l0", [g.bias["L0_gnn_bias"]], work, [(node_rows(g.table_32), g.h[:])])

    cs = ExitStack()
    with cs:
        sl = Spline(nc, cs, g, "p_2", 64, 64, g.sums_r64, stored=g.far_64)
        beside = [min(g.D.pairs, g.R.blocks - k * g.D.pairs) for k in range(3)]
        assert sum(beside) == g.R.blocks and min(beside) > 0
        stage_aggregate(nc, g, "g_l1", g.table_32, g.sums_d, sl=sl, sl_from=0, sl_count=beside[0], sl_weights=ins["L3_gnn_stn2_w"])
        cg, sbg = scope()
        gauss = sbg("l2_gauss", [P, g.D.tiles // QUARTERS, QUARTERS, 3])
        c, sb = scope()
        with c:
            got, hid, both = sb("l1_got", [P, NB, F]), sb("l1_hid", [P, NB, 64]), sb("l1_both", [P, NB, 64])
            c2, sb2 = scope()
            with c2:
                cat, y = sb2("l1_cat", [P, NB, 2 * F]), sb2("l1_y", [P, NB, F])
                stage_collect_quarters(nc, g, "c_l1", g.sums_d, got)

                def work(ch, rows, act, t):
                    ch.step(nc.vector.tensor_mul(cat[:, :, 0:F], got[:], per_node(g.D.inv_degree[:], F)))
                    ch.step(nc.vector.tensor_copy(cat[:, :, F:2 * F], g.h[:]))

                stage_nodes(nc, g, "n_l1a", [], work)
                stage_dense(nc, g, "d_l1a", cat, 64, 64, hid, [(0, 0, ins["L1_gnn_W1_l"]), (F, 0, ins["L1_gnn_W1_r"])])

                def work(ch, rows, act, t):
                    ch.step(nc.vector.tensor_add(hid[:], hid[:], bc(rows[0][:], 64)))
                    ch.step(nc.vector.tensor_scalar(hid[:], hid[:], 0.0, None, ALU.max))

                stage_nodes(nc, g, "n_l1b", [g.bias["L1_gnn_b1"]], work)
                stage_dense(nc, g, "d_l1b", hid, 64, 64, both, [(0, 0, ins["L1_gnn_W2_l"]), (0, F, ins["L1_gnn_W2_r"])])

                def work(ch, rows, act, t):
                    ch.step(nc.vector.tensor_mul(y[:], both[:, :, 0:F], per_node(g.valid[:], F)))

                stage_nodes(nc, g, "n_l1c", [], work, [(node_rows(g.table_32), y[:])])
            stage_aggregate(nc, g, "g_l1d", g.table_32, g.sums_d, sl=sl, sl_from=beside[0], sl_count=beside[1])
            stage_collect_quarters(nc, g, "c_l1d", g.sums_d, got, gaussians=(ins["L2_gnn_mu"], ins["L2_gnn_sigma"], gauss))

            def work(ch, rows, act, t):
                ch.step(nc.vector.tensor_mul(got[:], got[:], per_node(g.D.inv_degree[:], F)))
                ch.step(nc.vector.tensor_add(got[:], got[:], bc(rows[0][:], F)))
                ch.step(nc.vector.tensor_add(got[:], got[:], both[:, :, F:2 * F]))
                ch.step(nc.vector.tensor_add(g.x[:], g.x[:], got[:]))
                layernorm(ch, nc, g, t, g.h[:], act)

            stage_nodes(nc, g, "n_l1d", [g.bias["L1_gnn_b2"]], work)

        with cg:
            c2, sb2 = scope()
            with c2:
                three = sb2("l2_three", [P, NB, 3 * F])
                stage_dense(nc, g, "d_l2", g.h, F, 3 * F, three, [(0, 0, ins["L2_gnn_g"])])
                stage_nodes(nc, g, "n_l2", [], lambda ch, rows, act, t: None, [(node_rows(g.table_96), three[:])])
            stage_aggregate(nc, g, "g_l2", g.table_96, g.sums_d, gauss=gauss, sl=sl, sl_from=beside[0] + beside[1], sl_count=beside[2])
    c, sb = scope()
    with c:
        t3 = sb("l3_t3", [P, NB, 3])
        c1, sb1 = scope()
        with c1:
            hid = sb1("l3_hid", [P, NB, 64])
            got, res = sb1("l2_got", [P, NB, F]), sb1("l2_res", [P, NB, F])
            tmp, hid2 = sb1("l3_tmp2", [P, NB, 64]), sb1("l3_hid2", [P, NB, 64])
            row = sb1("l3_row", [P, NB, F + 3])
            stage_dense(nc, g, "d_l2b", g.h, F, F, res, [(0, 0, ins["L2_gnn_root"])], collect=(g.R, g.sums_r64, hid))

            def work(ch, rows, act, t):
                spline_mean(ch, hid[:], rows[0][:], 64)
                elu(ch, act, hid[:], tmp[:])

            thirds = [range(k * NB // 3, (k + 1) * NB // 3) for k in range(3)]
            stage_nodes(nc, g, "n_p2", [g.bias["L3_gnn_stn2_b"]], work, collect=(g.D, g.sums_d, got, thirds[0]))
            stage_dense(nc, g, "d_p3", hid, 64, 64, hid2, [(0, 0, ins["L3_gnn_stn3_w"])], collect=(g.D, g.sums_d, got, thirds[1]))

            def work(ch, rows, act, t):
                ch.step(nc.vector.tensor_add(hid2[:], hid2[:], bc(rows[0][:], 64)))
                elu(ch, act, hid2[:], tmp[:])

            stage_nodes(nc, g, "n_p3", [g.bias["L3_gnn_stn3_b"]], work, collect=(g.D, g.sums_d, got, thirds[2]))
            stage_dense(nc, g, "d_p4", hid2, 64, 3, t3, [(0, 0, ins["L3_gnn_stn4_w"])])
            stage_collect_quarters(nc, g, "c_l2", g.sums_d, got, collected=True)

            def work(ch, rows, act, t):
                ch.step(nc.vector.tensor_mul(got[:], got[:], per_node(g.D.inv_degree[:], F)))
                ch.step(nc.vector.tensor_add(got[:], got[:], res[:]))
                ch.step(nc.vector.tensor_add(got[:], got[:], bc(rows[0][:], F)))
                ch.step(nc.vector.tensor_add(g.x[:], g.x[:], got[:]))
                layernorm(ch, nc, g, t, g.h[:], act)
                ch.step(nc.vector.tensor_add(t3[:], t3[:], bc(rows[1][:], 3)))
                ch.step(nc.vector.tensor_copy(row[:, :, 0:F], g.h[:]))
                ch.step(nc.vector.tensor_copy(row[:, :, F:F + 3], t3[:]))

            stage_nodes(nc, g, "n_l2b", [g.bias["L2_gnn_bias"], g.bias["L3_gnn_stn4_b"]], work,
                        [(node_rows(g.table_35), row[:]), (node_rows(g.shift_table), t3[:])])
        stage_spread(nc, g, "s_shift", t3, g.shift_table, 3, g.shift_marks, g.shift_chunk)
        stage_spline_gathered(nc, g, "p_3", ins["L3_gnn_conv_w"], F, F, g.sums_r32, g.table_35, g.shift_chunk)
        c2, sb2 = scope()
        with c2:
            got = sb2("l3_got", [P, NB, F])
            stage_collect(nc, g, "c_p3", g.R, g.sums_r32, got)

            def work(ch, rows, act, t):
                spline_mean(ch, got[:], rows[0][:], F)
                ch.step(nc.vector.tensor_add(got[:], got[:], g.x[:]))

            full = (NB - 1) * P
            stage_nodes(nc, g, "n_p5", [g.bias["L3_gnn_conv_b"]], work,
                        [(out[0:full, :].rearrange("(b p) f -> p b f", p=P), got[:, 0:NB - 1, :]),
                         (out[full:N, :], got[0:N - full, NB - 1, :])])


def build(nc, ins, out):
    g = Shared()
    g.R = Order("r", 16, 4, 19, TB, True)
    g.D = Order("d", 2, 3, 13, TB_D, False)
    g.orders = (g.R, g.D)
    with ExitStack() as c:
        dram = lambda name, shape, dt=F32: nc.dram_tensor(name, shape, dt, kind="Internal").ap()
        sb = lambda name, shape, dt=F32: c.enter_context(nc.sbuf_tensor(name, shape, dt))
        g.pad_lo = {k: dram(f"pad_lo_{k}", [EP], BF16) for k in ("src", "dst")}
        g.pad = {"src": dram("pad_src", [EP], I32), "dst": dram("pad_dst", [EP], I32)}
        for o, key, other, attr in ((g.R, "src", "dst", "edge_attr_3"), (g.D, "dst", "src", "edge_attr_2")):
            o.key, o.other, o.attr = key, other, attr
            o.rec = dram(f"rec_{o.name}", [o.slots, o.words], I32)
            o.marks = dram(f"marks_{o.name}", [o.chunks + o.vb, 1])
            o.keep = o.marks.rearrange("v w -> (v w)")
            o.mask = sb(f"mask_{o.name}", [P, o.per_tile])
            o.slot0 = sb(f"slot0_{o.name}", [P, NH])
            o.last = sb(f"last_{o.name}", [P, NB], I32)
            o.start = sb(f"start_{o.name}", [P, NB], I32)
            o.inv_degree = sb(f"inv_degree_{o.name}", [P, NB])
        V = g.R.chunks
        g.chunk_row = sb("chunk_row", [P, 1], I32)
        g.att_table, g.near_table, g.near_chunk = dram("att_table", [NP, FAR]), dram("near_table", [NP, 4]), dram("near_chunk", [V, 4])
        g.top, g.factor, g.decay = dram("top", [4, V]), dram("factor", [4, V]), dram("decay", [4, V])
        g.att_sums = dram("att_sums", [V, 4 * (F + 1)])
        g.table_32, g.table_35 = dram("table_32", [NP, F]), dram("table_35", [NP, F + 3])
        g.sums_d, g.table_96 = dram("sums_d", [g.D.chunks, F]), dram("table_96", [NP, 3 * F])
        g.far_64 = dram("far_64", [P, g.R.tiles, 64])
        g.sums_r64, g.sums_r32 = dram("sums_r64", [V, 64]), dram("sums_r32", [V, F])
        g.near_marks, g.shift_marks = dram("near_marks", [V, 4]), dram("shift_marks", [V, 3])
        g.shift_table, g.shift_chunk = dram("shift_table", [NP, 3]), dram("shift_chunk", [V, 3])
        g.R.mask_t = sb("mask_t", [g.R.per_tile, P])
        g.iota_row, g.pidx, g.minus_pidx = sb("iota_row", [P, P]), sb("pidx", [P, 1]), sb("minus_pidx", [P, 1])
        g.later = sb("later", [P, NH, HB + 1])
        g.digits = sb("digits", [P, P, HB], BF16)
        g.ident, g.below, g.before = sb("ident", [P, P]), sb("below", [P, P]), sb("before", [P, P])
        g.zero = sb("zero", [P, 1])
        g.ones, g.zero_bf = sb("ones", [P, P]), sb("zero_bf", [P, P], BF16)
        g.valid = sb("valid", [P, NB])
        g.crossing = sb("crossing", [P, QUARTERS - 1, NB])
        g.degree = {k: sb(f"degree_{k}", [P, NH]) for k in ("src", "dst")}
        g.bias = {name: sb(f"bias_{name}", [P, ins[name].shape[0]])
                  for name in ("L0_gnn_bias", "L1_gnn_b1", "L1_gnn_b2", "L2_gnn_bias", "L3_gnn_stn1_b", "L3_gnn_stn2_b",
                               "L3_gnn_stn3_b", "L3_gnn_stn4_b", "L3_gnn_conv_b")}
        with ExitStack() as cs:
            sbs = lambda name, shape, dt=F32: cs.enter_context(nc.sbuf_tensor(name, shape, dt))
            cols = STEPS * HB
            g.key_i = {k: sbs(f"key_i_{k}", [P, cols], I32) for k in ("src", "dst")}
            g.key_f = {k: sbs(f"key_f_{k}", [P, cols]) for k in ("src", "dst")}
            g.lo = {k: sbs(f"lo_{k}", [P, cols], BF16) for k in ("src", "dst")}
            g.hi = {k: sbs(f"hi_{k}", [P, cols], BF16) for k in ("src", "dst")}
            g.attr = {"edge_attr_3": sbs("attr_3", [P, cols * 3]), "edge_attr_2": sbs("attr_2", [P, cols * 2])}
            stage_setup(nc, g, ins)
            stage_histogram(nc, g)
            stage_starts(nc, g, g.R)
            stage_sort(nc, g, g.R, tally=g.D)
            stage_starts(nc, g, g.D)
            stage_sort(nc, g, g.D, ones_weights=ins["L3_gnn_stn1_w"])
        g.x, g.h = sb("x_nodes", [P, NB, F]), sb("h_nodes", [P, NB, F])
        g.att_w, g.att = sb("att_w", [F, 8]), sb("att", [P, NB, 8])
        layers(nc, g, ins, out)


_INS = ["x", "src", "dst", "edge_attr_2", "edge_attr_3", "L0_gnn_w", "L0_gnn_fc_w", "L0_gnn_fc_b", "L0_gnn_bias",
        "L1_gnn_W1_l", "L1_gnn_b1", "L1_gnn_W1_r", "L1_gnn_W2_l", "L1_gnn_b2", "L1_gnn_W2_r",
        "L2_gnn_g", "L2_gnn_mu", "L2_gnn_sigma", "L2_gnn_root", "L2_gnn_bias",
        "L3_gnn_stn1_w", "L3_gnn_stn1_b", "L3_gnn_stn2_w", "L3_gnn_stn2_b", "L3_gnn_stn3_w", "L3_gnn_stn3_b",
        "L3_gnn_stn4_w", "L3_gnn_stn4_b", "L3_gnn_conv_w", "L3_gnn_conv_b"]


def kernel(**inputs):
    import numpy as _np
    import concourse.bacc as _bacc
    from concourse import mybir as _mybir
    from concourse.bass_utils import run_bass_kernel_spmd as _run

    nc = _bacc.Bacc("TRN2", target_bir_lowering=False, num_devices=1)
    arrays, args = {}, {}
    for name in _INS:
        a = _np.ascontiguousarray(inputs[name])
        arrays[f"in_{name}_dram"] = a
        args[name] = nc.dram_tensor(f"in_{name}_dram", a.shape, _mybir.dt.from_np(a.dtype), kind="ExternalInput").ap()
    out = nc.dram_tensor("out_dram", (N, F), F32, kind="ExternalOutput").ap()
    build(nc, args, out)
    r = _run(nc, [arrays], core_ids=[0])
    return r.results[0]["out_dram"]
```
